# Optimizing a Trainium2 kernel written in Bass

```python
import numpy as np
import jax
import jax.numpy as jnp

def _softmax(x, axis=-1):
    return jax.nn.softmax(x, axis=axis)

def _gelu(x):
    return jax.nn.gelu(x, approximate=True)

def _silu(x):
    return jax.nn.silu(x)

def _sigmoid(x):
    return jax.nn.sigmoid(x)

def _layernorm(x, axis=-1, eps=1e-05):
    m = jnp.mean(x, axis=axis, keepdims=True)
    v = jnp.var(x, axis=axis, keepdims=True)
    return (x - m) / jnp.sqrt(v + eps)

def _scatter_add(tgt, idx, src, axis=0):
    return tgt.at[idx].add(src)

def _segment_sum(src, seg, n):
    return jax.ops.segment_sum(src, seg, n)
kernel_name = 'mk_pixart_resid_d4_seqx_r8_e43115'

def setup_inputs(seed: int=0):
    np.random.seed(seed)
    _w = jnp.asarray

    def _rec_inputs():
        import jax
        import jax.numpy as jnp
        _rk = jax.random.key(seed)
        x = -0.003379 + 0.9984 * jax.random.normal(jax.random.fold_in(_rk, 1), (8, 256, 128), jnp.float32)
        _lenS = 256 - jax.random.randint(jax.random.fold_in(_rk, 7), (8,), 0, max(1, 256 // 4) + 1, jnp.int32)
        _lenS2 = 64 - jax.random.randint(jax.random.fold_in(_rk, 8), (8,), 0, max(1, 64 // 4) + 1, jnp.int32)
        cond_1024 = -0.0142567 + 1.00875 * jax.random.normal(jax.random.fold_in(_rk, 11), (8, 128), jnp.float32)
        _ctx_1024P = jax.random.normal(jax.random.fold_in(_rk, 12), (8, 16, 128), jnp.float32)
        _ctx_1024c = jax.random.dirichlet(jax.random.fold_in(_rk, 512), 0.3 * jnp.ones((16,), jnp.float32), (8, 64))
        _ctx_1024t = jnp.einsum('bsk,bkd->bsd', _ctx_1024c, _ctx_1024P)
        _ctx_1024t = _ctx_1024t * jax.lax.rsqrt(jnp.mean(jnp.square(_ctx_1024t)) + 1e-12) * 0.953939
        ctx_1024 = -5.72187e-05 + 0.999849 * (_ctx_1024t + 0.3 * jax.random.normal(jax.random.fold_in(_rk, 612), (8, 64, 128), jnp.float32))
        _validS = jnp.arange(256)[None, :] < _lenS[:, None]
        _validS2 = jnp.arange(64)[None, :] < _lenS2[:, None]
        _causal = jnp.tril(jnp.ones((256, 256), dtype=bool))
        mask_BxS_bf0 = jnp.logical_not(jnp.ones((8, 256), dtype=bool))
        mask_BxS2_bf0 = jnp.logical_not(jnp.ones((8, 64), dtype=bool))
        return (x, cond_1024, ctx_1024, mask_BxS_bf0, mask_BxS2_bf0)
    x, cond_1024, ctx_1024, mask_BxS_bf0, mask_BxS2_bf0 = _rec_inputs()

    def _L0_xcond_setup():
        import jax, jax.numpy as jnp
        import numpy as np
        B, N, K, D, T = (16, 512, 16, 128, 3)
        EPS_ATTN = 1e-08
        LN_EPS = 1e-05

        def _ln(x, g, b):
            mu = jnp.mean(x, axis=-1, keepdims=True)
            var = jnp.mean(jnp.square(x - mu), axis=-1, keepdims=True)
            return (x - mu) * jax.lax.rsqrt(var + LN_EPS) * g + b
        key = jax.random.key(seed)
        ks = jax.random.split(key, 16)
        w = lambda k, i, o: jax.random.normal(k, (i, o), jnp.float32) * 0.02
        inp = {'x_cls': jax.random.normal(ks[0], (B, D), jnp.float32), 'x': jax.random.normal(ks[1], (B, N, D), jnp.float32), 'noise': jax.random.normal(ks[2], (B, K, D), jnp.float32), 'q_mu': jax.random.normal(ks[3], (1, 1, D), jnp.float32), 'q_logsig': jax.random.normal(ks[4], (1, 1, D), jnp.float32) * 0.02, 'lnkv_g': jnp.ones((D,), jnp.float32), 'lnkv_b': jnp.zeros((D,), jnp.float32), 'lnq_g': jnp.ones((D,), jnp.float32), 'lnq_b': jnp.zeros((D,), jnp.float32), 'lnm_g': jnp.ones((D,), jnp.float32), 'lnm_b': jnp.zeros((D,), jnp.float32), 'lnp_g': jnp.ones((D,), jnp.float32), 'lnp_b': jnp.zeros((D,), jnp.float32), 'wk': w(ks[5], D, D), 'bk': jnp.zeros((D,), jnp.float32), 'wv': w(ks[6], D, D), 'bv': jnp.zeros((D,), jnp.float32), 'wq': w(ks[7], D, D), 'bq': jnp.zeros((D,), jnp.float32), 'wu': w(ks[8], D, D), 'bu': jnp.zeros((D,), jnp.float32), 'w1': w(ks[9], D, D), 'b1': jnp.zeros((D,), jnp.float32), 'w2': w(ks[10], D, D), 'b2': jnp.zeros((D,), jnp.float32)}
        return inp
    _L0_xcond_all = _L0_xcond_setup()
    _L0_xcond_in = {k: v for k, v in _L0_xcond_all.items() if k in ('q_mu', 'q_logsig', 'lnkv_g', 'lnkv_b', 'lnq_g', 'lnq_b', 'lnm_g', 'lnm_b', 'lnp_g', 'lnp_b', 'wk', 'bk', 'wv', 'bv', 'wq', 'bq', 'wu', 'bu', 'w1', 'b1', 'w2', 'b2')}
    del _L0_xcond_all

    def _L0_ffn_setup():
        import jax, jax.numpy as jnp
        import numpy as np
        N_HEAD, N_ACTIVE, D_MODEL, D_ATTN = (16, 4, 128, 64)
        key = jax.random.key(seed)
        ks = jax.random.split(key, 12)
        s = 0.02
        B, S = (2, 512)
        return {'x': jax.random.normal(ks[0], (B, S, D_MODEL), dtype=jnp.float32), 'Wq': jax.random.normal(ks[1], (D_MODEL, N_HEAD * D_ATTN), dtype=jnp.float32) * s, 'bq': jnp.zeros((N_HEAD * D_ATTN,), dtype=jnp.float32), 'Wk': jax.random.normal(ks[2], (D_MODEL, N_HEAD * D_ATTN), dtype=jnp.float32) * s, 'bk': jnp.zeros((N_HEAD * D_ATTN,), dtype=jnp.float32), 'Wv': jax.random.normal(ks[3], (D_MODEL, N_HEAD * D_ATTN), dtype=jnp.float32) * s, 'bv': jnp.zeros((N_HEAD * D_ATTN,), dtype=jnp.float32), 'Wr': jax.random.normal(ks[4], (D_MODEL, N_HEAD), dtype=jnp.float32) * s, 'br': jnp.zeros((N_HEAD,), dtype=jnp.float32), 'Wo': jax.random.normal(ks[5], (N_ACTIVE * D_ATTN, D_MODEL), dtype=jnp.float32) * s, 'bo': jnp.zeros((D_MODEL,), dtype=jnp.float32)}
    _L0_ffn_all = _L0_ffn_setup()
    _L0_ffn_in = {k: v for k, v in _L0_ffn_all.items() if k in ('Wq', 'bq', 'Wk', 'bk', 'Wv', 'bv', 'Wr', 'br', 'Wo', 'bo')}
    del _L0_ffn_all

    def _L1_xcond_setup():
        import jax, jax.numpy as jnp
        import numpy as np
        B, T, S, H, E = (128, 32, 32, 128, 128)
        key = jax.random.key(seed)
        ks = jax.random.split(key, 8)
        sc = lambda n: 1.0 / np.sqrt(n)
        return dict(dec_seq=jax.random.normal(ks[0], (B, T, E), jnp.float32), enc_hiddens=jax.random.normal(ks[1], (B, S, H), jnp.float32), last_hidden=jax.random.normal(ks[2], (B, H), jnp.float32), W_att=jax.random.normal(ks[3], (2 * H, H), jnp.float32) * sc(2 * H), V_att=jax.random.normal(ks[4], (H, 1), jnp.float32) * sc(H), Wi=jax.random.normal(ks[5], (E + H, 3 * H), jnp.float32) * sc(E + H), Uh=jax.random.normal(ks[6], (H, 3 * H), jnp.float32) * sc(H), b=jnp.zeros((3 * H,), jnp.float32))
    _L1_xcond_all = _L1_xcond_setup()
    _L1_xcond_in = {k: v for k, v in _L1_xcond_all.items() if k in ('W_att', 'V_att', 'Wi', 'Uh', 'b')}
    del _L1_xcond_all

    def _L1_ffn_setup():
        import jax, jax.numpy as jnp
        import numpy as np
        NUM_EXPERTS = 8
        CAPACITY_FACTOR = 1.0
        key = jax.random.key(seed)
        k1, k2, k3, k4 = jax.random.split(key, 4)
        B, S, D, E, F = (8, 256, 128, NUM_EXPERTS, 512)
        x = jax.random.normal(k1, (B, S, D), dtype=jnp.float32)
        router_w = jax.random.normal(k2, (D, E), dtype=jnp.float32) * D ** (-0.5)
        w1 = jax.random.normal(k3, (E, D, F), dtype=jnp.float32) * D ** (-0.5)
        w2 = jax.random.normal(k4, (E, F, D), dtype=jnp.float32) * F ** (-0.5)
        return {'x': x, 'router_w': router_w, 'w1': w1, 'w2': w2}
    _L1_ffn_all = _L1_ffn_setup()
    _L1_ffn_in = {k: v for k, v in _L1_ffn_all.items() if k in ('router_w', 'w1', 'w2')}
    del _L1_ffn_all

    def _L2_xcond_setup():
        import jax, jax.numpy as jnp
        import numpy as np
        NL, D, H, DFF = (6, 128, 16, 512)
        HD = D // H

        def _rope(x):
            L = x.shape[1]
            half = HD // 2
            inv = 1.0 / 10000.0 ** (jnp.arange(half, dtype=jnp.float32) / half)
            ang = jnp.arange(L, dtype=jnp.float32)[:, None] * inv
            cos = jnp.cos(ang)[None, :, None, :]
            sin = jnp.sin(ang)[None, :, None, :]
            x1, x2 = (x[..., :half], x[..., half:])
            return jnp.concatenate([x1 * cos - x2 * sin, x1 * sin + x2 * cos], axis=-1)

        def _ln(x, eps=1e-05):
            m = jnp.mean(x, axis=-1, keepdims=True)
            v = jnp.var(x, axis=-1, keepdims=True)
            return (x - m) * jax.lax.rsqrt(v + eps)

        def _adaln(x, emb, w, b):
            gb = emb[:, 0, :] @ w.T + b
            g, be = jnp.split(gb, 2, axis=-1)
            return _ln(x) * (1.0 + g[:, None, :]) + be[:, None, :]

        def _attn(q, k, v, mask):
            scores = jnp.einsum('bqhd,bkhd->bhqk', q, k) / np.float32(np.sqrt(HD))
            scores = jnp.where(mask[:, None, None, :], jnp.float32(-jnp.inf), scores)
            w = jax.nn.softmax(scores, axis=-1)
            return jnp.einsum('bhqk,bkhd->bqhd', w, v)
        key = jax.random.key(seed)
        ks = jax.random.split(key, 20)
        B, L, LC = (4, 128, 64)
        s = 0.02
        inp = {'x': jax.random.normal(ks[0], (B, L, D), jnp.float32), 'noise_emb': jax.random.normal(ks[1], (B, 1, D), jnp.float32), 'context': jax.random.normal(ks[2], (B, LC, D), jnp.float32), 'src_mask': jnp.zeros((B, L), bool), 'ctx_mask': jnp.zeros((B, LC), bool), 'n1_w': jax.random.normal(ks[3], (NL, 2 * D, D), jnp.float32) * s, 'n1_b': jnp.zeros((NL, 2 * D), jnp.float32), 'n2_w': jax.random.normal(ks[4], (NL, 2 * D, D), jnp.float32) * s, 'n2_b': jnp.zeros((NL, 2 * D), jnp.float32), 'n3_w': jax.random.normal(ks[5], (NL, 2 * D, D), jnp.float32) * s, 'n3_b': jnp.zeros((NL, 2 * D), jnp.float32), 'qkv_w': jax.random.normal(ks[6], (NL, 3 * D, D), jnp.float32) * s, 'so_w': jax.random.normal(ks[7], (NL, D, D), jnp.float32) * s, 'cq_w': jax.random.normal(ks[8], (NL, D, D), jnp.float32) * s, 'ck_w': jax.random.normal(ks[9], (NL, D, D), jnp.float32) * s, 'cv_w': jax.random.normal(ks[10], (NL, D, D), jnp.float32) * s, 'co_w': jax.random.normal(ks[11], (NL, D, D), jnp.float32) * s, 'f1_w': jax.random.normal(ks[12], (NL, DFF, D), jnp.float32) * s, 'f1_b': jnp.zeros((NL, DFF), jnp.float32), 'f2_w': jax.random.normal(ks[13], (NL, D, DFF), jnp.float32) * s, 'f2_b': jnp.zeros((NL, D), jnp.float32)}
        return inp
    _L2_xcond_all = _L2_xcond_setup()
    _L2_xcond_in = {k: v for k, v in _L2_xcond_all.items() if k in ('n1_w', 'n1_b', 'n2_w', 'n2_b', 'n3_w', 'n3_b', 'qkv_w', 'so_w', 'cq_w', 'ck_w', 'cv_w', 'co_w', 'f1_w', 'f1_b', 'f2_w', 'f2_b')}
    del _L2_xcond_all

    def _L2_ffn_setup():
        import jax, jax.numpy as jnp
        import numpy as np
        B, S, D, H, E, K, F = (1, 128, 128, 16, 8, 2, 512)

        def layernorm(x, g, b, eps=1e-05):
            m = x.mean(-1, keepdims=True)
            v = ((x - m) ** 2).mean(-1, keepdims=True)
            return (x - m) * jax.lax.rsqrt(v + eps) * g + b
        key = jax.random.key(seed)
        ks = jax.random.split(key, 8)
        n = lambda k, shape, sc: jax.random.normal(k, shape, dtype=jnp.float32) * sc
        return {'x': n(ks[0], (B, S, D), 1.0), 'w_qkv': n(ks[1], (D, 3 * D), D ** (-0.5)), 'w_o': n(ks[2], (D, D), D ** (-0.5)), 'g1': jnp.ones((D,), jnp.float32), 'b1': jnp.zeros((D,), jnp.float32), 'wg': n(ks[3], (D, E), D ** (-0.5)), 'w1': n(ks[4], (E, D, F), D ** (-0.5)), 'bb1': jnp.zeros((E, F), jnp.float32), 'w2': n(ks[5], (E, F, D), F ** (-0.5)), 'bb2': jnp.zeros((E, D), jnp.float32), 'g2': jnp.ones((D,), jnp.float32), 'b2': jnp.zeros((D,), jnp.float32)}
    _L2_ffn_all = _L2_ffn_setup()
    _L2_ffn_in = {k: v for k, v in _L2_ffn_all.items() if k in ('w_qkv', 'w_o', 'g1', 'b1', 'wg', 'w1', 'bb1', 'w2', 'bb2', 'g2', 'b2')}
    del _L2_ffn_all

    def _L3_xcond_setup():
        import jax, jax.numpy as jnp
        import numpy as np
        import math
        B, S, CTX, D, H, DH = (2, 256, 32, 128, 16, 64)
        INNER = H * DH
        DFF = 4 * D

        def layernorm(x, eps=1e-05):
            m = jnp.mean(x, axis=-1, keepdims=True)
            v = jnp.var(x, axis=-1, keepdims=True)
            return (x - m) * jax.lax.rsqrt(v + eps)

        def adaln(x, t, w, b):
            emb = t @ w + b
            scale, shift = jnp.split(emb, 2, axis=-1)
            return layernorm(x) * (1.0 + scale) + shift

        def mha(xq, ctx, wq, wk, wv, wo, bo):
            b, sq, _ = xq.shape
            sk = ctx.shape[1]
            q = (xq @ wq).reshape(b, sq, H, DH).transpose(0, 2, 1, 3)
            k = (ctx @ wk).reshape(b, sk, H, DH).transpose(0, 2, 1, 3)
            v = (ctx @ wv).reshape(b, sk, H, DH).transpose(0, 2, 1, 3)
            scores = jnp.einsum('bhqd,bhkd->bhqk', q, k) / math.sqrt(DH)
            attn = jax.nn.softmax(scores, axis=-1)
            out = jnp.einsum('bhqk,bhkd->bhqd', attn, v)
            out = out.transpose(0, 2, 1, 3).reshape(b, sq, INNER)
            return out @ wo + bo

        def glu_ff(x, w1, b1, w2, b2):
            u = x @ w1 + b1
            a, gate = jnp.split(u, 2, axis=-1)
            return a * jax.nn.gelu(gate, approximate=False) @ w2 + b2
        key = jax.random.key(seed)
        ks = jax.random.split(key, 24)
        s = 1.0 / math.sqrt(D)

        def n(k, shape, scale=1.0):
            return jax.random.normal(k, shape, dtype=jnp.float32) * scale
        return {'x': n(ks[0], (B, S, D)), 't': n(ks[1], (B, 1, D)), 'context': n(ks[2], (B, CTX, D)), 'attn1_wq': n(ks[3], (D, INNER), s), 'attn1_wk': n(ks[4], (D, INNER), s), 'attn1_wv': n(ks[5], (D, INNER), s), 'attn1_wo': n(ks[6], (INNER, D), s), 'attn1_bo': n(ks[7], (D,), 0.01), 'attn2_wq': n(ks[8], (D, INNER), s), 'attn2_wk': n(ks[9], (D, INNER), s), 'attn2_wv': n(ks[10], (D, INNER), s), 'attn2_wo': n(ks[11], (INNER, D), s), 'attn2_bo': n(ks[12], (D,), 0.01), 'ff_w1': n(ks[13], (D, 2 * DFF), s), 'ff_b1': n(ks[14], (2 * DFF,), 0.01), 'ff_w2': n(ks[15], (DFF, D), 1.0 / math.sqrt(DFF)), 'ff_b2': n(ks[16], (D,), 0.01), 'norm1_w': n(ks[17], (D, 2 * D), s), 'norm1_b': n(ks[18], (2 * D,), 0.01), 'norm2_w': n(ks[19], (D, 2 * D), s), 'norm2_b': n(ks[20], (2 * D,), 0.01), 'norm3_w': n(ks[21], (D, 2 * D), s), 'norm3_b': n(ks[22], (2 * D,), 0.01)}
    _L3_xcond_all = _L3_xcond_setup()
    _L3_xcond_in = {k: v for k, v in _L3_xcond_all.items() if k in ('attn1_wq', 'attn1_wk', 'attn1_wv', 'attn1_wo', 'attn1_bo', 'attn2_wq', 'attn2_wk', 'attn2_wv', 'attn2_wo', 'attn2_bo', 'ff_w1', 'ff_b1', 'ff_w2', 'ff_b2', 'norm1_w', 'norm1_b', 'norm2_w', 'norm2_b', 'norm3_w', 'norm3_b')}
    del _L3_xcond_all

    def _L3_ffn_setup():
        import jax, jax.numpy as jnp
        import numpy as np
        IN_FEATURES = 128
        ACT_BITS = 4

        def _hadamard(size: int) -> np.ndarray:
            h = np.array([[1.0]], dtype=np.float64)
            while h.shape[0] < size:
                h = np.block([[h, h], [h, -h]])
            return (h / np.sqrt(size)).astype(np.float32)

        def _quantize_activations(x, bits=ACT_BITS):
            pos = 2 ** (bits - 1) - 1
            neg = 2 ** (bits - 1)
            scale = jnp.clip(jnp.max(jnp.abs(jax.lax.stop_gradient(x)), axis=-1, keepdims=True), 1e-05) / pos
            q = jnp.clip(jnp.round(x / scale), -neg, pos) * scale
            return x + jax.lax.stop_gradient(q - x)

        def _ternary_quantize_ste(w):
            scale = jnp.clip(jnp.mean(jnp.abs(jax.lax.stop_gradient(w)), axis=1, keepdims=True), 1e-05)
            n = w / scale
            tern = jnp.where(n > 0.5, 1.0, jnp.where(n < -0.5, -1.0, 0.0))
            q = tern * scale
            return w + jax.lax.stop_gradient(q - w)
        key = jax.random.key(seed)
        k1, k2 = jax.random.split(key)
        x = jax.random.normal(k1, (8, 1024, IN_FEATURES), dtype=jnp.float32)
        bound = 1.0 / np.sqrt(IN_FEATURES)
        weight = jax.random.uniform(k2, (128, IN_FEATURES), dtype=jnp.float32, minval=-bound, maxval=bound)
        return {'x': x, 'weight': weight}
    _L3_ffn_all = _L3_ffn_setup()
    _L3_ffn_in = {k: v for k, v in _L3_ffn_all.items() if k in ('weight',)}
    del _L3_ffn_all
    return {'x': x, 'cond_1024': cond_1024, 'ctx_1024': ctx_1024, 'mask_BxS_bf0': mask_BxS_bf0, 'mask_BxS2_bf0': mask_BxS2_bf0, 'L0_xcond_q_mu': _L0_xcond_in['q_mu'], 'L0_xcond_q_logsig': _L0_xcond_in['q_logsig'], 'L0_xcond_lnkv_g': _L0_xcond_in['lnkv_g'], 'L0_xcond_lnkv_b': _L0_xcond_in['lnkv_b'], 'L0_xcond_lnq_g': _L0_xcond_in['lnq_g'], 'L0_xcond_lnq_b': _L0_xcond_in['lnq_b'], 'L0_xcond_lnm_g': _L0_xcond_in['lnm_g'], 'L0_xcond_lnm_b': _L0_xcond_in['lnm_b'], 'L0_xcond_lnp_g': _L0_xcond_in['lnp_g'], 'L0_xcond_lnp_b': _L0_xcond_in['lnp_b'], 'L0_xcond_wk': _L0_xcond_in['wk'], 'L0_xcond_bk': _L0_xcond_in['bk'], 'L0_xcond_wv': _L0_xcond_in['wv'], 'L0_xcond_bv': _L0_xcond_in['bv'], 'L0_xcond_wq': _L0_xcond_in['wq'], 'L0_xcond_bq': _L0_xcond_in['bq'], 'L0_xcond_wu': _L0_xcond_in['wu'], 'L0_xcond_bu': _L0_xcond_in['bu'], 'L0_xcond_w1': _L0_xcond_in['w1'], 'L0_xcond_b1': _L0_xcond_in['b1'], 'L0_xcond_w2': _L0_xcond_in['w2'], 'L0_xcond_b2': _L0_xcond_in['b2'], 'L0_ffn_Wq': _L0_ffn_in['Wq'], 'L0_ffn_bq': _L0_ffn_in['bq'], 'L0_ffn_Wk': _L0_ffn_in['Wk'], 'L0_ffn_bk': _L0_ffn_in['bk'], 'L0_ffn_Wv': _L0_ffn_in['Wv'], 'L0_ffn_bv': _L0_ffn_in['bv'], 'L0_ffn_Wr': _L0_ffn_in['Wr'], 'L0_ffn_br': _L0_ffn_in['br'], 'L0_ffn_Wo': _L0_ffn_in['Wo'], 'L0_ffn_bo': _L0_ffn_in['bo'], 'L1_xcond_W_att': _L1_xcond_in['W_att'], 'L1_xcond_V_att': _L1_xcond_in['V_att'], 'L1_xcond_Wi': _L1_xcond_in['Wi'], 'L1_xcond_Uh': _L1_xcond_in['Uh'], 'L1_xcond_b': _L1_xcond_in['b'], 'L1_ffn_router_w': _L1_ffn_in['router_w'], 'L1_ffn_w1': _L1_ffn_in['w1'], 'L1_ffn_w2': _L1_ffn_in['w2'], 'L2_xcond_n1_w': _L2_xcond_in['n1_w'], 'L2_xcond_n1_b': _L2_xcond_in['n1_b'], 'L2_xcond_n2_w': _L2_xcond_in['n2_w'], 'L2_xcond_n2_b': _L2_xcond_in['n2_b'], 'L2_xcond_n3_w': _L2_xcond_in['n3_w'], 'L2_xcond_n3_b': _L2_xcond_in['n3_b'], 'L2_xcond_qkv_w': _L2_xcond_in['qkv_w'], 'L2_xcond_so_w': _L2_xcond_in['so_w'], 'L2_xcond_cq_w': _L2_xcond_in['cq_w'], 'L2_xcond_ck_w': _L2_xcond_in['ck_w'], 'L2_xcond_cv_w': _L2_xcond_in['cv_w'], 'L2_xcond_co_w': _L2_xcond_in['co_w'], 'L2_xcond_f1_w': _L2_xcond_in['f1_w'], 'L2_xcond_f1_b': _L2_xcond_in['f1_b'], 'L2_xcond_f2_w': _L2_xcond_in['f2_w'], 'L2_xcond_f2_b': _L2_xcond_in['f2_b'], 'L2_ffn_w_qkv': _L2_ffn_in['w_qkv'], 'L2_ffn_w_o': _L2_ffn_in['w_o'], 'L2_ffn_g1': _L2_ffn_in['g1'], 'L2_ffn_b1': _L2_ffn_in['b1'], 'L2_ffn_wg': _L2_ffn_in['wg'], 'L2_ffn_w1': _L2_ffn_in['w1'], 'L2_ffn_bb1': _L2_ffn_in['bb1'], 'L2_ffn_w2': _L2_ffn_in['w2'], 'L2_ffn_bb2': _L2_ffn_in['bb2'], 'L2_ffn_g2': _L2_ffn_in['g2'], 'L2_ffn_b2': _L2_ffn_in['b2'], 'L3_xcond_attn1_wq': _L3_xcond_in['attn1_wq'], 'L3_xcond_attn1_wk': _L3_xcond_in['attn1_wk'], 'L3_xcond_attn1_wv': _L3_xcond_in['attn1_wv'], 'L3_xcond_attn1_wo': _L3_xcond_in['attn1_wo'], 'L3_xcond_attn1_bo': _L3_xcond_in['attn1_bo'], 'L3_xcond_attn2_wq': _L3_xcond_in['attn2_wq'], 'L3_xcond_attn2_wk': _L3_xcond_in['attn2_wk'], 'L3_xcond_attn2_wv': _L3_xcond_in['attn2_wv'], 'L3_xcond_attn2_wo': _L3_xcond_in['attn2_wo'], 'L3_xcond_attn2_bo': _L3_xcond_in['attn2_bo'], 'L3_xcond_ff_w1': _L3_xcond_in['ff_w1'], 'L3_xcond_ff_b1': _L3_xcond_in['ff_b1'], 'L3_xcond_ff_w2': _L3_xcond_in['ff_w2'], 'L3_xcond_ff_b2': _L3_xcond_in['ff_b2'], 'L3_xcond_norm1_w': _L3_xcond_in['norm1_w'], 'L3_xcond_norm1_b': _L3_xcond_in['norm1_b'], 'L3_xcond_norm2_w': _L3_xcond_in['norm2_w'], 'L3_xcond_norm2_b': _L3_xcond_in['norm2_b'], 'L3_xcond_norm3_w': _L3_xcond_in['norm3_w'], 'L3_xcond_norm3_b': _L3_xcond_in['norm3_b'], 'L3_ffn_weight': _L3_ffn_in['weight']}

def reference(x, cond_1024, ctx_1024, mask_BxS_bf0, mask_BxS2_bf0, L0_xcond_q_mu, L0_xcond_q_logsig, L0_xcond_lnkv_g, L0_xcond_lnkv_b, L0_xcond_lnq_g, L0_xcond_lnq_b, L0_xcond_lnm_g, L0_xcond_lnm_b, L0_xcond_lnp_g, L0_xcond_lnp_b, L0_xcond_wk, L0_xcond_bk, L0_xcond_wv, L0_xcond_bv, L0_xcond_wq, L0_xcond_bq, L0_xcond_wu, L0_xcond_bu, L0_xcond_w1, L0_xcond_b1, L0_xcond_w2, L0_xcond_b2, L0_ffn_Wq, L0_ffn_bq, L0_ffn_Wk, L0_ffn_bk, L0_ffn_Wv, L0_ffn_bv, L0_ffn_Wr, L0_ffn_br, L0_ffn_Wo, L0_ffn_bo, L1_xcond_W_att, L1_xcond_V_att, L1_xcond_Wi, L1_xcond_Uh, L1_xcond_b, L1_ffn_router_w, L1_ffn_w1, L1_ffn_w2, L2_xcond_n1_w, L2_xcond_n1_b, L2_xcond_n2_w, L2_xcond_n2_b, L2_xcond_n3_w, L2_xcond_n3_b, L2_xcond_qkv_w, L2_xcond_so_w, L2_xcond_cq_w, L2_xcond_ck_w, L2_xcond_cv_w, L2_xcond_co_w, L2_xcond_f1_w, L2_xcond_f1_b, L2_xcond_f2_w, L2_xcond_f2_b, L2_ffn_w_qkv, L2_ffn_w_o, L2_ffn_g1, L2_ffn_b1, L2_ffn_wg, L2_ffn_w1, L2_ffn_bb1, L2_ffn_w2, L2_ffn_bb2, L2_ffn_g2, L2_ffn_b2, L3_xcond_attn1_wq, L3_xcond_attn1_wk, L3_xcond_attn1_wv, L3_xcond_attn1_wo, L3_xcond_attn1_bo, L3_xcond_attn2_wq, L3_xcond_attn2_wk, L3_xcond_attn2_wv, L3_xcond_attn2_wo, L3_xcond_attn2_bo, L3_xcond_ff_w1, L3_xcond_ff_b1, L3_xcond_ff_w2, L3_xcond_ff_b2, L3_xcond_norm1_w, L3_xcond_norm1_b, L3_xcond_norm2_w, L3_xcond_norm2_b, L3_xcond_norm3_w, L3_xcond_norm3_b, L3_ffn_weight):
    import jax
    import jax.numpy as jnp

    def _L0_xcond_ref(x_cls, x, noise, q_mu, q_logsig, lnkv_g, lnkv_b, lnq_g, lnq_b, lnm_g, lnm_b, lnp_g, lnp_b, wk, bk, wv, bv, wq, bq, wu, bu, w1, b1, w2, b2):
        import jax, jax.numpy as jnp
        import numpy as np
        B, N, K, D, T = (16, 512, 16, 128, 3)
        EPS_ATTN = 1e-08
        LN_EPS = 1e-05

        def _ln(x, g, b):
            mu = jnp.mean(x, axis=-1, keepdims=True)
            var = jnp.mean(jnp.square(x - mu), axis=-1, keepdims=True)
            return (x - mu) * jax.lax.rsqrt(var + LN_EPS) * g + b
        scale = D ** (-0.5)
        x_in = _ln(x, lnkv_g, lnkv_b)
        k = x_in @ wk + bk
        v = x_in @ wv + bv
        slots = q_mu + jnp.exp(q_logsig) * noise
        for _ in range(T):
            prev = slots
            q = _ln(slots, lnq_g, lnq_b) @ wq + bq
            logits = jnp.einsum('bnd,bkd->bnk', k, q) / scale
            attn = jax.nn.softmax(logits, axis=-1) + EPS_ATTN
            attn = attn / jnp.sum(attn, axis=1, keepdims=True)
            upd = jnp.einsum('bnk,bnd->bkd', attn, v)
            slots = upd @ wu + bu + prev
            h = _ln(slots, lnm_g, lnm_b) @ w1 + b1
            slots = jax.nn.gelu(h, approximate=False) @ w2 + b2 + slots
            slots = _ln(slots + x_cls[:, None, :], lnp_g, lnp_b)
        return slots

    def _L0_ffn_ref(x, Wq, bq, Wk, bk, Wv, bv, Wr, br, Wo, bo):
        import jax, jax.numpy as jnp
        import numpy as np
        N_HEAD, N_ACTIVE, D_MODEL, D_ATTN = (16, 4, 128, 64)
        B, S, D = x.shape
        H, K, dh = (N_HEAD, N_ACTIVE, D_ATTN)
        dist = jax.nn.softmax(jnp.mean(x @ Wr + br, axis=1), axis=-1)
        top_vals, top_idx = jax.lax.top_k(dist, K)
        sparse = jnp.zeros_like(dist).at[jnp.arange(B)[:, None], top_idx].set(top_vals)
        gates_all = jax.nn.softmax(sparse, axis=1)
        g = jnp.take_along_axis(gates_all, top_idx, axis=1)[:, :, None, None]

        def proj(W, b):
            return (x @ W + b).reshape(B, S, H, dh).transpose(0, 2, 1, 3)
        Q, Kt, V = (proj(Wq, bq), proj(Wk, bk), proj(Wv, bv))
        idx = top_idx[:, :, None, None]
        Qk = jnp.take_along_axis(Q, idx, axis=1) * g
        Kk = jnp.take_along_axis(Kt, idx, axis=1) * g
        Vk = jnp.take_along_axis(V, idx, axis=1) * g
        scores = jnp.einsum('bksd,bktd->bkst', Qk, Kk) / jnp.sqrt(jnp.float32(dh))
        attn = jax.nn.softmax(scores, axis=-1)
        out = jnp.einsum('bkst,bktd->bksd', attn, Vk)
        out = out.transpose(0, 2, 1, 3).reshape(B, S, K * dh)
        return out @ Wo + bo

    def _L1_xcond_ref(dec_seq, enc_hiddens, last_hidden, W_att, V_att, Wi, Uh, b):
        import jax, jax.numpy as jnp
        import numpy as np
        B, T, S, H, E = (128, 32, 32, 128, 128)
        Bn, Sn, Hn = enc_hiddens.shape

        def step(h, x_t):
            hid = jnp.broadcast_to(h[:, None, :], (Bn, Sn, Hn))
            combined = jnp.concatenate([hid, enc_hiddens], axis=2)
            score = jnp.tanh(jnp.einsum('bsk,kh->bsh', combined, W_att))
            score = jnp.einsum('bsh,h->bs', score, V_att[:, 0])
            attn = jax.nn.softmax(score, axis=-1)
            context = jnp.einsum('bs,bsh->bh', attn, enc_hiddens)
            inp = jnp.concatenate([x_t, context], axis=1)
            gz, gr, gh = jnp.split(inp @ Wi + b, 3, axis=1)
            rz, rr, rh = jnp.split(h @ Uh, 3, axis=1)
            z = jax.nn.sigmoid(gz + rz)
            r = jax.nn.sigmoid(gr + rr)
            hh = jnp.tanh(gh + r * rh)
            h_new = z * h + (1.0 - z) * hh
            return (h_new, h_new)
        _, outs = jax.lax.scan(step, last_hidden, jnp.swapaxes(dec_seq, 0, 1))
        return jnp.swapaxes(outs, 0, 1)

    def _L1_ffn_ref(x, router_w, w1, w2):
        import jax, jax.numpy as jnp
        import numpy as np
        NUM_EXPERTS = 8
        CAPACITY_FACTOR = 1.0
        B, S, D = x.shape
        E = router_w.shape[1]
        T = B * S
        C = int(CAPACITY_FACTOR * T / E)
        x_flat = x.reshape(T, D)
        logits = x_flat @ router_w
        probs = jax.nn.softmax(logits, axis=-1)
        expert_idx = jnp.argmax(probs, axis=-1)
        gate = jnp.take_along_axis(probs, expert_idx[:, None], axis=1)[:, 0]
        onehot = jax.nn.one_hot(expert_idx, E, dtype=jnp.float32)
        pos_all = jnp.cumsum(onehot, axis=0) - 1.0
        pos = jnp.take_along_axis(pos_all, expert_idx[:, None], axis=1)[:, 0]
        pos = pos.astype(jnp.int32)
        keep = (pos < C).astype(x_flat.dtype)
        pos_c = jnp.clip(pos, 0, C - 1)
        expert_in = jnp.zeros((E, C, D), dtype=x_flat.dtype)
        expert_in = expert_in.at[expert_idx, pos_c].add(x_flat * keep[:, None])
        hidden = jax.nn.gelu(jnp.einsum('ecd,edf->ecf', expert_in, w1))
        expert_out = jnp.einsum('ecf,efd->ecd', hidden, w2)
        y = expert_out[expert_idx, pos_c] * (gate * keep)[:, None]
        return y.reshape(B, S, D)

    def _L2_xcond_ref(x, noise_emb, context, src_mask, ctx_mask, n1_w, n1_b, n2_w, n2_b, n3_w, n3_b, qkv_w, so_w, cq_w, ck_w, cv_w, co_w, f1_w, f1_b, f2_w, f2_b):
        import jax, jax.numpy as jnp
        import numpy as np
        NL, D, H, DFF = (6, 128, 16, 512)
        HD = D // H

        def _rope(x):
            L = x.shape[1]
            half = HD // 2
            inv = 1.0 / 10000.0 ** (jnp.arange(half, dtype=jnp.float32) / half)
            ang = jnp.arange(L, dtype=jnp.float32)[:, None] * inv
            cos = jnp.cos(ang)[None, :, None, :]
            sin = jnp.sin(ang)[None, :, None, :]
            x1, x2 = (x[..., :half], x[..., half:])
            return jnp.concatenate([x1 * cos - x2 * sin, x1 * sin + x2 * cos], axis=-1)

        def _ln(x, eps=1e-05):
            m = jnp.mean(x, axis=-1, keepdims=True)
            v = jnp.var(x, axis=-1, keepdims=True)
            return (x - m) * jax.lax.rsqrt(v + eps)

        def _adaln(x, emb, w, b):
            gb = emb[:, 0, :] @ w.T + b
            g, be = jnp.split(gb, 2, axis=-1)
            return _ln(x) * (1.0 + g[:, None, :]) + be[:, None, :]

        def _attn(q, k, v, mask):
            scores = jnp.einsum('bqhd,bkhd->bhqk', q, k) / np.float32(np.sqrt(HD))
            scores = jnp.where(mask[:, None, None, :], jnp.float32(-jnp.inf), scores)
            w = jax.nn.softmax(scores, axis=-1)
            return jnp.einsum('bhqk,bkhd->bqhd', w, v)
        B, L, _ = x.shape
        LC = context.shape[1]
        for i in range(NL):
            xn = _adaln(x, noise_emb, n1_w[i], n1_b[i])
            qkv = xn @ qkv_w[i].T
            q, k, v = jnp.split(qkv, 3, axis=-1)
            q = _rope(q.reshape(B, L, H, HD))
            k = _rope(k.reshape(B, L, H, HD))
            v = v.reshape(B, L, H, HD)
            a = _attn(q, k, v, src_mask).reshape(B, L, D) @ so_w[i].T
            x = x + a
            xn = _adaln(x, noise_emb, n2_w[i], n2_b[i])
            q = _rope((xn @ cq_w[i].T).reshape(B, L, H, HD))
            k = _rope((context @ ck_w[i].T).reshape(B, LC, H, HD))
            v = (context @ cv_w[i].T).reshape(B, LC, H, HD)
            a = _attn(q, k, v, ctx_mask).reshape(B, L, D) @ co_w[i].T
            x = x + a
            xn = _adaln(x, noise_emb, n3_w[i], n3_b[i])
            h = jax.nn.gelu(xn @ f1_w[i].T + f1_b[i], approximate=False)
            x = x + (h @ f2_w[i].T + f2_b[i])
        return x

    def _L2_ffn_ref(x, w_qkv, w_o, g1, b1, wg, w1, bb1, w2, bb2, g2, b2):
        import jax, jax.numpy as jnp
        import numpy as np
        B, S, D, H, E, K, F = (1, 128, 128, 16, 8, 2, 512)

        def layernorm(x, g, b, eps=1e-05):
            m = x.mean(-1, keepdims=True)
            v = ((x - m) ** 2).mean(-1, keepdims=True)
            return (x - m) * jax.lax.rsqrt(v + eps) * g + b
        b, s, d = x.shape
        hd = d // H
        qkv = x @ w_qkv
        q, k, v = jnp.split(qkv, 3, axis=-1)
        to_heads = lambda t: t.reshape(b, s, H, hd).transpose(0, 2, 1, 3)
        q, k, v = (to_heads(q), to_heads(k), to_heads(v))
        scores = jnp.einsum('bhqd,bhkd->bhqk', q, k) / jnp.sqrt(jnp.float32(hd))
        causal = jnp.tril(jnp.ones((s, s), bool))
        scores = jnp.where(causal, scores, jnp.finfo(scores.dtype).min)
        attn = jax.nn.softmax(scores, axis=-1)
        o = jnp.einsum('bhqk,bhkd->bhqd', attn, v)
        o = o.transpose(0, 2, 1, 3).reshape(b, s, d) @ w_o
        h = layernorm(x + o, g1, b1)
        probs = jax.nn.softmax(h @ wg, axis=-1)
        topv, topi = jax.lax.top_k(probs, K)
        topv = topv / topv.sum(-1, keepdims=True)
        w = (topv[..., None] * jax.nn.one_hot(topi, E, dtype=h.dtype)).sum(-2)
        h1 = jax.nn.gelu(jnp.einsum('bsd,edf->ebsf', h, w1) + bb1[:, None, None, :])
        y = jnp.einsum('ebsf,efd->ebsd', h1, w2) + bb2[:, None, None, :]
        moe = jnp.einsum('ebsd,bse->bsd', y, w)
        return layernorm(h + moe, g2, b2)

    def _L3_xcond_ref(x, t, context, attn1_wq, attn1_wk, attn1_wv, attn1_wo, attn1_bo, attn2_wq, attn2_wk, attn2_wv, attn2_wo, attn2_bo, ff_w1, ff_b1, ff_w2, ff_b2, norm1_w, norm1_b, norm2_w, norm2_b, norm3_w, norm3_b):
        import jax, jax.numpy as jnp
        import numpy as np
        import math
        B, S, CTX, D, H, DH = (2, 256, 32, 128, 16, 64)
        INNER = H * DH
        DFF = 4 * D

        def layernorm(x, eps=1e-05):
            m = jnp.mean(x, axis=-1, keepdims=True)
            v = jnp.var(x, axis=-1, keepdims=True)
            return (x - m) * jax.lax.rsqrt(v + eps)

        def adaln(x, t, w, b):
            emb = t @ w + b
            scale, shift = jnp.split(emb, 2, axis=-1)
            return layernorm(x) * (1.0 + scale) + shift

        def mha(xq, ctx, wq, wk, wv, wo, bo):
            b, sq, _ = xq.shape
            sk = ctx.shape[1]
            q = (xq @ wq).reshape(b, sq, H, DH).transpose(0, 2, 1, 3)
            k = (ctx @ wk).reshape(b, sk, H, DH).transpose(0, 2, 1, 3)
            v = (ctx @ wv).reshape(b, sk, H, DH).transpose(0, 2, 1, 3)
            scores = jnp.einsum('bhqd,bhkd->bhqk', q, k) / math.sqrt(DH)
            attn = jax.nn.softmax(scores, axis=-1)
            out = jnp.einsum('bhqk,bhkd->bhqd', attn, v)
            out = out.transpose(0, 2, 1, 3).reshape(b, sq, INNER)
            return out @ wo + bo

        def glu_ff(x, w1, b1, w2, b2):
            u = x @ w1 + b1
            a, gate = jnp.split(u, 2, axis=-1)
            return a * jax.nn.gelu(gate, approximate=False) @ w2 + b2
        h1 = adaln(x, t, norm1_w, norm1_b)
        x = mha(h1, h1, attn1_wq, attn1_wk, attn1_wv, attn1_wo, attn1_bo) + x
        h2 = adaln(x, t, norm2_w, norm2_b)
        x = mha(h2, context, attn2_wq, attn2_wk, attn2_wv, attn2_wo, attn2_bo) + x
        h3 = adaln(x, t, norm3_w, norm3_b)
        x = glu_ff(h3, ff_w1, ff_b1, ff_w2, ff_b2) + x
        return x

    def _L3_ffn_ref(x, weight):
        import jax, jax.numpy as jnp
        import numpy as np
        IN_FEATURES = 128
        ACT_BITS = 4

        def _hadamard(size: int) -> np.ndarray:
            h = np.array([[1.0]], dtype=np.float64)
            while h.shape[0] < size:
                h = np.block([[h, h], [h, -h]])
            return (h / np.sqrt(size)).astype(np.float32)

        def _quantize_activations(x, bits=ACT_BITS):
            pos = 2 ** (bits - 1) - 1
            neg = 2 ** (bits - 1)
            scale = jnp.clip(jnp.max(jnp.abs(jax.lax.stop_gradient(x)), axis=-1, keepdims=True), 1e-05) / pos
            q = jnp.clip(jnp.round(x / scale), -neg, pos) * scale
            return x + jax.lax.stop_gradient(q - x)

        def _ternary_quantize_ste(w):
            scale = jnp.clip(jnp.mean(jnp.abs(jax.lax.stop_gradient(w)), axis=1, keepdims=True), 1e-05)
            n = w / scale
            tern = jnp.where(n > 0.5, 1.0, jnp.where(n < -0.5, -1.0, 0.0))
            q = tern * scale
            return w + jax.lax.stop_gradient(q - w)
        H = jnp.asarray(_hadamard(IN_FEATURES))
        xh = x @ H
        xq = _quantize_activations(xh)
        wq = _ternary_quantize_ste(weight)
        return jnp.einsum('bsi,oi->bso', xq, wq)
    x = x + _L0_xcond_ref(cond_1024, ctx_1024, _layernorm(x, axis=-1), L0_xcond_q_mu, L0_xcond_q_logsig, L0_xcond_lnkv_g, L0_xcond_lnkv_b, L0_xcond_lnq_g, L0_xcond_lnq_b, L0_xcond_lnm_g, L0_xcond_lnm_b, L0_xcond_lnp_g, L0_xcond_lnp_b, L0_xcond_wk, L0_xcond_bk, L0_xcond_wv, L0_xcond_bv, L0_xcond_wq, L0_xcond_bq, L0_xcond_wu, L0_xcond_bu, L0_xcond_w1, L0_xcond_b1, L0_xcond_w2, L0_xcond_b2)
    x = x + _L0_ffn_ref(_layernorm(x, axis=-1), L0_ffn_Wq, L0_ffn_bq, L0_ffn_Wk, L0_ffn_bk, L0_ffn_Wv, L0_ffn_bv, L0_ffn_Wr, L0_ffn_br, L0_ffn_Wo, L0_ffn_bo)
    x = x + _L1_xcond_ref(_layernorm(x, axis=-1), ctx_1024, cond_1024, L1_xcond_W_att, L1_xcond_V_att, L1_xcond_Wi, L1_xcond_Uh, L1_xcond_b)
    x = x + _L1_ffn_ref(_layernorm(x, axis=-1), L1_ffn_router_w, L1_ffn_w1, L1_ffn_w2)
    x = x + _L2_xcond_ref(_layernorm(x, axis=-1), cond_1024[:, None, :], ctx_1024, mask_BxS_bf0, mask_BxS2_bf0, L2_xcond_n1_w, L2_xcond_n1_b, L2_xcond_n2_w, L2_xcond_n2_b, L2_xcond_n3_w, L2_xcond_n3_b, L2_xcond_qkv_w, L2_xcond_so_w, L2_xcond_cq_w, L2_xcond_ck_w, L2_xcond_cv_w, L2_xcond_co_w, L2_xcond_f1_w, L2_xcond_f1_b, L2_xcond_f2_w, L2_xcond_f2_b)
    x = x + _L2_ffn_ref(_layernorm(x, axis=-1), L2_ffn_w_qkv, L2_ffn_w_o, L2_ffn_g1, L2_ffn_b1, L2_ffn_wg, L2_ffn_w1, L2_ffn_bb1, L2_ffn_w2, L2_ffn_bb2, L2_ffn_g2, L2_ffn_b2)
    x = x + _L3_xcond_ref(_layernorm(x, axis=-1), cond_1024[:, None, :], ctx_1024, L3_xcond_attn1_wq, L3_xcond_attn1_wk, L3_xcond_attn1_wv, L3_xcond_attn1_wo, L3_xcond_attn1_bo, L3_xcond_attn2_wq, L3_xcond_attn2_wk, L3_xcond_attn2_wv, L3_xcond_attn2_wo, L3_xcond_attn2_bo, L3_xcond_ff_w1, L3_xcond_ff_b1, L3_xcond_ff_w2, L3_xcond_ff_b2, L3_xcond_norm1_w, L3_xcond_norm1_b, L3_xcond_norm2_w, L3_xcond_norm2_b, L3_xcond_norm3_w, L3_xcond_norm3_b)
    x = x + _L3_ffn_ref(_layernorm(x, axis=-1), L3_ffn_weight)
    return x

_drawn_inputs = setup_inputs


def setup_inputs(seed=0):
    import zlib

    import numpy as np

    out = dict(_drawn_inputs(seed))
    spreads = {'L0_xcond_lnkv_g': (1.0, 0.6),
     'L0_xcond_lnkv_b': (0.0, 0.8),
     'L0_xcond_lnq_g': (1.0, 0.6),
     'L0_xcond_lnq_b': (0.0, 2.0),
     'L0_xcond_lnm_g': (1.0, 0.6),
     'L0_xcond_lnm_b': (0.0, 0.8),
     'L0_xcond_lnp_g': (1.0, 0.2),
     'L0_xcond_lnp_b': (0.0, 0.1),
     'L0_xcond_bk': (0.0, 2.0),
     'L0_xcond_bv': (0.0, 0.349),
     'L0_xcond_bq': (0.0, 2.0),
     'L0_xcond_bu': (0.0, 0.1),
     'L0_xcond_b1': (0.0, 0.595),
     'L0_xcond_b2': (0.0, 0.1),
     'L0_ffn_bq': (0.0, 2.0),
     'L0_ffn_bk': (0.0, 2.0),
     'L0_ffn_bv': (0.0, 0.8),
     'L0_ffn_br': (0.0, 0.761),
     'L0_ffn_bo': (0.0, 0.1),
     'L1_xcond_b': (0.0, 0.1),
     'L2_xcond_n1_b': (0.0, 0.8),
     'L2_xcond_n2_b': (0.0, 2.0),
     'L2_xcond_n3_b': (0.0, 0.8),
     'L2_xcond_f1_b': (0.0, 0.307),
     'L2_xcond_f2_b': (0.0, 0.1),
     'L2_ffn_g1': (1.0, 0.2),
     'L2_ffn_b1': (0.0, 0.1),
     'L2_ffn_bb1': (0.0, 0.682),
     'L2_ffn_bb2': (0.0, 0.456),
     'L2_ffn_g2': (1.0, 0.2),
     'L2_ffn_b2': (0.0, 0.273)}
    factors = {'L0_xcond_q_logsig': 8.0,
     'L0_xcond_wk': 147.79,
     'L0_xcond_wq': 138.857,
     'L0_ffn_Wq': 181.899,
     'L0_ffn_Wk': 200.0,
     'L0_ffn_Wv': 8.0,
     'L0_ffn_Wr': 8.0,
     'L0_ffn_Wo': 8.0,
     'L2_xcond_n1_w': 3.537,
     'L2_xcond_n2_w': 8.0,
     'L2_xcond_n3_w': 3.46,
     'L2_xcond_cq_w': 8.0,
     'L2_xcond_ck_w': 8.0,
     'L3_xcond_attn1_bo': 30.2,
     'L3_xcond_attn2_bo': 35.446,
     'L3_xcond_ff_b1': 22.784,
     'L3_xcond_ff_b2': 35.485,
     'L3_xcond_norm1_b': 8.0,
     'L3_xcond_norm2_b': 27.869,
     'L3_xcond_norm3_b': 8.0}
    for name, (base, spread) in spreads.items():
        noise = np.random.default_rng([zlib.crc32(name.encode()), seed]).standard_normal(out[name].shape)
        drawn = base * np.exp(spread * noise) if base else spread * noise
        out[name] = jnp.asarray(drawn.astype(out[name].dtype))
    for name, factor in factors.items():
        out[name] = (out[name] * factor).astype(out[name].dtype)
    return out
```

```python
from contextlib import ExitStack, contextmanager

import numpy as np

import concourse.bass as bass
from concourse import mybir

ALU = mybir.AluOpType
ACT = mybir.ActivationFunctionType
AX = mybir.AxisListType
F32 = mybir.dt.float32
BF16 = mybir.dt.bfloat16
U8 = mybir.dt.uint8
U32 = mybir.dt.uint32
ds = bass.ds

P = 128
D = 128
B, S = 8, 256
C = 64
TILES = B * S // P
PAIRS = B // 2
PT = 4
PTOK = PT * P
H = 16
GROUP = 4
E, EF = 8, 4
EPS = 1e-5
NEG = -1e30


class Signals:

    def __init__(self, nc, ctx):
        self.nc, self.ctx, self.found = nc, ctx, {}

    def __getitem__(self, name):
        if name not in self.found:
            self.found[name] = self.ctx.enter_context(self.nc.semaphore(name))
        return self.found[name]


@contextmanager
def engines_pass(nc):
    with ExitStack() as ctx:
        sig = Signals(nc, ctx)
        with nc.Block() as block:
            yield block, sig
        numbers = sorted(s.num for s in sig.found.values())
        runs = [n for n in numbers if n - 1 not in numbers]
        for first in runs:
            end = next(n for n in range(first, 257) if n not in numbers)
            nc.sync.sem_clear(range(first, end))
        if runs:
            nc.all_engine_barrier()


class Steps:

    def __init__(self, engine, sem):
        self.engine, self.sem, self.n = engine, sem, 0

    def after(self, instruction):
        self.n += 1
        instruction.then_inc(self.sem, 1)
        self.engine.wait_ge(self.sem, self.n)



def norm_vector(dve, sig, steps, tag, src, w, out, tiles=PT, rows=P):
    for t in range(tiles):
        last = dve.bn_stats(w["stats"][0:rows, t, :], src(t))
    steps.after(last)
    for t in range(tiles):
        last = dve.bn_aggr(w["mv"][0:rows, t, :], w["stats"][0:rows, t, :])
    last.then_inc(sig[tag + "_var_ready"], 1)
    dve.wait_ge(sig[tag + "_rstd_ready"], 1)
    for t in range(tiles):
        last = dve.tensor_scalar(out(t), src(t), w["mv"][0:rows, t, 0:1], w["rstd"][0:rows, t, :],
                                 ALU.subtract, ALU.mult)
    last.then_inc(sig[tag + "_normed"], 1)
    dve.wait_ge(sig[tag + "_normed"], 1)


def norm_pool(pool, sig, tag, w, tiles=PT, rows=P):
    pool.wait_ge(sig[tag + "_var_ready"], 1)
    pool.tensor_scalar(w["veps"][0:rows, 0:tiles, :], w["mv"][0:rows, 0:tiles, 1:2], EPS, 1.0,
                       ALU.add, ALU.mult).then_inc(sig[tag + "_veps_ready"], 1)
    pool.wait_ge(sig[tag + "_veps_ready"], 1)
    pool.tensor_tensor(w["rstd"][0:rows, 0:tiles, :], w["veps"][0:rows, 0:tiles, :],
                       w["mhalf"][0:rows, 0:tiles, :], ALU.pow).then_inc(sig[tag + "_rstd_ready"], 1)


def turn_tensor(pe, ident, bank, src, tiles=PT, rows=P, width=P):
    for t in range(tiles):
        last = pe.transpose(bank[0:width, t * rows:(t + 1) * rows], src(t), ident[0:rows, 0:rows])
    return last


def norm_buffers(sb, name):
    return {
        "stats": sb(name + "_stats", [P, PT, 6]), "mv": sb(name + "_mv", [P, PT, 2]),
        "veps": sb(name + "_veps", [P, PT, 1]), "rstd": sb(name + "_rstd", [P, PT, 1]),
    }



def prob_cols(h, first, n=P):
    at = 256 * (2 * (h % 2) + h // 2) + first
    return slice(at, at + n)


class Attention:

    def __init__(self, tag, units, chunks, rounds, dh, groups, width, scale):
        self.tag, self.units, self.chunks, self.rounds = tag, units, chunks, rounds
        self.dh, self.groups, self.width, self.scale = dh, groups, width, scale


def attention_tensor(pe, sig, a, psum, m, probs):
    tag = a.tag

    def max_scores(u):
        for h in range(GROUP):
            n = u * GROUP + h
            if n >= 2:
                pe.wait_ge(sig[tag + "_row_max_ready"], n - 1)
            for out, products in a.max_products(u, h):
                for i, (lhsT, rhs) in enumerate(products):
                    last = pe.matmul(psum[:, n % 2, out], lhsT, rhs, start=i == 0, stop=i == len(products) - 1)
            last.then_inc(sig[tag + "_max_scores_ready"], 1)

    def key_scores(u):
        pe.wait_ge(sig[tag + "_row_max_ready"], GROUP * (u + 1))
        for c in range(a.chunks):
            n = u * a.chunks + c
            if n >= 2:
                pe.wait_ge(sig[tag + "_probs_ready"], n - 1)
            for h in range(GROUP):
                bank, col = 2 + 2 * (n % 2) + h % 2, 256 * (h // 2)
                for out, products in a.score_products(u, c, h):
                    rows = slice(out, out + P // len(a.score_products(u, c, h)))
                    pe.matmul(psum[rows, bank, col:col + 256], *products[0], start=True, stop=False)
                    for lhsT, rhs in products[1:]:
                        pe.matmul(psum[rows, bank, col:col + 256], lhsT, rhs, start=False, stop=False)
                    for t in range(2):
                        mcol = a.max_column(u, h, out, t)
                        last = pe.matmul(psum[rows, bank, col + P * t:col + P * (t + 1)],
                                         m[:, mcol:mcol + 1].to_broadcast([P, rows.stop - rows.start]),
                                         a.neg_ident, start=False, stop=t == 1)
            last.then_inc(sig[tag + "_scores_ready"], 1)

    def values(u):
        pe.wait_ge(sig[tag + "_probs_ready"], a.chunks * (u + 1))
        for r in range(a.rounds):
            n = u * a.rounds + r
            if n >= 1:
                pe.wait_ge(sig[tag + "_values_taken"], n)
            for t in range(2):
                for h in range(GROUP):
                    products = a.value_products(u, h, r, t, probs[:, u % 2])
                    for i, (lhsT, rhs) in enumerate(products):
                        last = pe.matmul(psum[:, 6 + t, h * (a.dh + 1):(h + 1) * (a.dh + 1)], lhsT, rhs,
                                         start=i == 0, stop=i == len(products) - 1)
            last.then_inc(sig[tag + "_values_ready"], 1)

    max_scores(0)
    for u in range(a.units + 1):
        if u < a.units:
            key_scores(u)
        if u + 1 < a.units:
            max_scores(u + 1)
        if u >= 1:
            values(u - 1)


def attention_scalar(act, sig, a, psum, probs):
    tag = a.tag
    for u in range(a.units):
        if u >= 2:
            act.wait_ge(sig[tag + "_values_ready"], a.rounds * (u - 1))
        for c in range(a.chunks):
            n = u * a.chunks + c
            act.wait_ge(sig[tag + "_scores_ready"], n + 1)
            bank = 2 + 2 * (n % 2)
            act.activation(probs[:, u % 2, c, :], psum[:, bank:bank + 2, :].rearrange("p a n -> p (a n)"),
                           ACT.Exp, bias=a.key_bias(u, c), scale=a.scale).then_inc(sig[tag + "_probs_ready"], 1)


def attention_vector(dve, sig, steps, a, psum, m, rsum, out):
    tag = a.tag

    def row_max(u):
        for h in range(GROUP):
            n = u * GROUP + h
            dve.wait_ge(sig[tag + "_max_scores_ready"], n + 1)
            scores = psum[:, n % 2, 0:a.groups * a.width].rearrange("p (g k) -> p g k", g=a.groups)
            dve.tensor_reduce(m[:, n * a.groups:(n + 1) * a.groups], scores, AX.X, ALU.max)\
               .then_inc(sig[tag + "_row_max_ready"], 1)

    def normalise(u):
        for r in range(a.rounds):
            n = u * a.rounds + r
            dve.wait_ge(sig[tag + "_values_ready"], n + 1)
            sums = psum[:, 6:8, 0:GROUP * (a.dh + 1)].rearrange("p t (h e) -> p t h e", e=a.dh + 1)
            steps.after(dve.reciprocal(rsum[:, :, :], sums[:, :, :, a.dh]))
            for t in range(2):
                last = dve.tensor_tensor(out(u, r, t), sums[:, t, :, 0:a.dh],
                                         rsum[:, t, :].unsqueeze(2).to_broadcast([P, GROUP, a.dh]), ALU.mult)
            last.then_inc(sig[tag + "_values_taken"], 1)

    row_max(0)
    for u in range(a.units + 1):
        if u + 1 < a.units:
            row_max(u + 1)
        if u >= 1:
            normalise(u - 1)



def rope_tables():
    half = L2_DH // 2
    inv = (np.float32(1.0) / np.float32(10000.0) ** (np.arange(half, dtype=np.float32) / np.float32(half)))
    ang = np.arange(S, dtype=np.float32)[:, None] * inv.astype(np.float32)
    cos, sin = np.cos(ang).T, np.sin(ang).T
    cos8, sin8 = np.concatenate([cos, cos]), np.concatenate([-sin, sin])
    return np.tile(cos8, (H, 1)).astype(np.float32), np.tile(sin8, (H, 1)).astype(np.float32)


def hadamard(size):
    h = np.array([[1.0]], dtype=np.float64)
    while h.shape[0] < size:
        h = np.block([[h, h], [h, -h]])
    return (h / np.sqrt(size)).astype(np.float32)


def shape_constants():
    cos, sin = rope_tables()
    q = np.arange(P)
    causal = np.zeros((P, 2, S), np.float32)
    causalT = np.zeros((P, 2, S), np.float32)
    for t in range(2):
        causal[:, t, :] = np.where(np.arange(S)[None, :] > (q + P * t)[:, None], NEG, 0.0)
        causalT[:, t, :] = np.where((q + P * t)[:, None] > np.arange(S)[None, :], NEG, 0.0)
    head = np.stack([((q // L2_DH) % GROUP == j).astype(np.float32) for j in range(GROUP)], 1)
    keys = lambda table: np.concatenate([np.tile(table, (1, 2)), np.tile(table[:, :C], (1, 2))], 1)
    cos, sin = keys(cos), keys(sin)
    return {"c_ident": np.eye(P, dtype=np.float32), "c_cos": cos, "c_sin": sin, "c_head": head,
            "c_causal": causal.reshape(P, 2 * S), "c_causalT": causalT.reshape(P, 2 * S),
            "c_hadamard": hadamard(P), "c_before": np.triu(np.ones((P, P), np.float32), 1),
            "c_number": np.arange(H, dtype=np.float32)[None, :8]}


def swap_halves(w):
    s = w.shape
    return w.reshape(*s[:-2], H, 2, L2_DH // 2, s[-1])[..., ::-1, :, :].reshape(s)



SLOT_T = 3
SLOT_EPS = 1e-8


def slot_attention(nc, dram, X, psum, cst):
    with ExitStack() as ctx:
        def sb(name, shape, dt=F32):
            return ctx.enter_context(nc.sbuf_tensor("s0_" + name, shape, dt))

        W = sb("w", [P, 6, D])
        wk, wv, wq, wu, w1, w2 = (W[:, i, :] for i in range(6))
        col = sb("col", [P, 9])
        row = sb("row", [P, 7, D])
        cond = sb("cond", [P, B, D])
        context = sb("context", [P, PAIRS, D])
        ones = sb("ones", [P, 1])
        nx, nkv, nq, nm, np_ = (norm_buffers(sb, n) for n in ("nx", "nkv", "nq", "nm", "np"))
        for n in (nx, nkv, nq, nm, np_):
            n["mhalf"] = cst["mhalf"]
        xin, xinT = sb("xin", [P, D]), sb("xinT", [P, P])
        kT, v = sb("kT", [P, P]), sb("v", [P, D])
        slots, sn, snT = sb("slots", [P, PT, D]), sb("sn", [P, PT, D]), sb("snT", [P, PTOK])
        qT, ex, attn = sb("qT", [P, PTOK]), sb("ex", [P, S]), sb("attn", [P, S])
        smax, ssum = sb("smax", [P, 1]), sb("ssum", [P, 1])
        updT, rcount = sb("updT", [P, PTOK]), sb("rcount", [P, PT])
        mid, mn, mnT, hT = sb("mid", [P, PT, D]), sb("mn", [P, PT, D]), sb("mnT", [P, PTOK]), sb("hT", [P, PTOK])

        with engines_pass(nc) as (block, sig):
            @block.sync
            def _(sp):
                for dst, src in ((W, "S0_W"), (col, "S0_col"), (context, "ctx_rows")):
                    sp.dma_start(dst[:], dram[src]).then_inc(sig["loads"], 16)
                sp.dma_start(row[:].rearrange("p l d -> p (l d)"), dram["S0_row"].to_broadcast([P, 7 * D]))\
                    .then_inc(sig["loads"], 16)
                sp.dma_start(cond[:].rearrange("p l d -> p (l d)"), dram["cond_row"].to_broadcast([P, B * D]))\
                    .then_inc(sig["loads"], 16)
                sp.wait_ge(sig["loads"], 80)

            @block.gpsimd
            def _(pool):
                pool.memset(ones[:], 1.0)

            @block.scalar
            def _(act):
                act.wait_ge(sig["loads"], 80)
                act.activation(row[:, 1, :], row[:, 1, :], ACT.Exp)

        with nc.Fori(0, PAIRS) as pair:
            def x(t):
                return X[:, ds(pair * PT + t, 1), :].rearrange("p a d -> p (a d)")

            xall = X[:, ds(pair * PT, PT), :]

            def tiles(bank):
                return psum[:, bank, :].rearrange("p (t d) -> p t d", t=PT)

            def everywhere(i):
                return row[:, i, :].unsqueeze(1).to_broadcast([P, PT, D])

            with engines_pass(nc) as (block, sig):
                @block.tensor
                def _(pe):
                    pe.wait_ge(sig["nkv_normed"], 1)
                    pe.transpose(psum[:, 0, 0:P], xin[:], cst["ident"][:]).then_inc(sig["xin_turned"], 1)
                    pe.wait_ge(sig["xinT_ready"], 1)
                    pe.matmul(psum[:, 1, 0:P], wk, xinT[:], start=True, stop=True).then_inc(sig["k_ready"], 1)
                    pe.matmul(psum[:, 2, 0:P], xinT[:], wv, start=True, stop=True).then_inc(sig["v_ready"], 1)

                @block.gpsimd
                def _(pool):
                    norm_pool(pool, sig, "nkv", nkv, tiles=1)
                    norm_pool(pool, sig, "nx", nx)

                @block.vector
                def _(dve):
                    steps = Steps(dve, sig["vector_steps"])
                    norm_vector(dve, sig, steps, "nkv", lambda t: context[:, ds(pair, 1), :].rearrange("p a d -> p (a d)"),
                                nkv, lambda t: xin[:], tiles=1)
                    dve.wait_ge(sig["xin_turned"], 1)
                    dve.tensor_scalar(xinT[:], psum[:, 0, 0:P], col[:, 0:1], col[:, 1:2], ALU.mult, ALU.add)\
                        .then_inc(sig["xinT_ready"], 1)
                    norm_vector(dve, sig, steps, "nx", x, nx, lambda t: sn[:, t, :])
                    steps.after(dve.tensor_tensor(sn[:], sn[:], everywhere(1), ALU.mult))
                    dve.tensor_tensor(slots[:], sn[:], everywhere(0), ALU.add)
                    dve.wait_ge(sig["k_ready"], 1)
                    dve.tensor_scalar(kT[:], psum[:, 1, 0:P], col[:, 6:7], None, ALU.add)
                    dve.wait_ge(sig["v_ready"], 1)
                    dve.tensor_tensor(v[:], psum[:, 2, 0:P], row[:, 2, :], ALU.add)

            with nc.Fori(0, SLOT_T) as _step:
                with engines_pass(nc) as (block, sig):
                    @block.tensor
                    def _(pe):
                        pe.wait_ge(sig["nq_normed"], 1)
                        turn_tensor(pe, cst["ident"], psum[:, 0, :], lambda t: sn[:, t, :]).then_inc(sig["slots_turned"], 1)
                        pe.wait_ge(sig["snT_ready"], 1)
                        pe.matmul(psum[:, 1, :], wq, snT[:], start=True, stop=True).then_inc(sig["q_ready"], 1)
                        pe.wait_ge(sig["qT_ready"], 1)
                        for b in range(2):
                            last = pe.matmul(psum[C * b:C * b + C, 2, 0:S], kT[:, C * b:C * b + C], qT[:, S * b:S * b + S],
                                             start=True, stop=True)
                        last.then_inc(sig["logits_ready"], 1)
                        pe.wait_ge(sig["attn_ready"], 1)
                        for b in range(2):
                            r = slice(C * b, C * b + C)
                            last = pe.matmul(psum[:, 3 + b, 0:S], v[r, :], attn[r, :], start=True, stop=True)
                        last.then_inc(sig["upd_ready"], 1)
                        for b in range(2):
                            r = slice(C * b, C * b + C)
                            for t in range(2):
                                last = pe.matmul(psum[:, 5 + b, t:t + 1], attn[r, P * t:P * t + P], ones[r, :],
                                                 start=True, stop=True)
                        last.then_inc(sig["count_ready"], 1)
                        pe.wait_ge(sig["updT_ready"], 1)
                        for t in range(PT):
                            last = pe.matmul(psum[:, 7, P * t:P * t + P], updT[:, P * t:P * t + P], wu, start=True, stop=True)
                        last.then_inc(sig["wu_ready"], 1)
                        pe.wait_ge(sig["nm_normed"], 1)
                        turn_tensor(pe, cst["ident"], psum[:, 0, :], lambda t: mn[:, t, :]).then_inc(sig["mid_turned"], 1)
                        pe.wait_ge(sig["mnT_ready"], 1)
                        pe.matmul(psum[:, 1, :], w1, mnT[:], start=True, stop=True).then_inc(sig["units_ready"], 1)
                        pe.wait_ge(sig["gelu_ready"], 1)
                        for t in range(PT):
                            last = pe.matmul(psum[:, 2, P * t:P * t + P], hT[:, P * t:P * t + P], w2, start=True, stop=True)
                        last.then_inc(sig["mlp_ready"], 1)

                    @block.gpsimd
                    def _(pool):
                        norm_pool(pool, sig, "nq", nq)
                        norm_pool(pool, sig, "nm", nm)
                        norm_pool(pool, sig, "np", np_)

                    @block.scalar
                    def _(act):
                        act.wait_ge(sig["slots_turned"], 1)
                        act.activation(snT[:], psum[:, 0, :], ACT.Identity, bias=col[:, 3:4], scale=col[:, 2:3])\
                            .then_inc(sig["snT_ready"], 1)
                        act.wait_ge(sig["q_ready"], 1)
                        act.activation(qT[:], psum[:, 1, :], ACT.Identity, bias=col[:, 7:8]).then_inc(sig["qT_ready"], 1)
                        act.wait_ge(sig["max_ready"], 1)
                        act.activation(ex[:], psum[:, 2, 0:S], ACT.Exp, bias=smax[:], scale=float(D) ** 0.5,
                                       accum_out=ssum[:]).then_inc(sig["exp_ready"], 1)
                        act.wait_ge(sig["upd_ready"], 1)
                        act.copy(updT[:].rearrange("p (b s) -> p b s", b=2), psum[:, 3:5, 0:S]).then_inc(sig["updT_ready"], 1)
                        act.wait_ge(sig["mid_turned"], 1)
                        act.activation(mnT[:], psum[:, 0, :], ACT.Identity, bias=col[:, 5:6], scale=col[:, 4:5])\
                            .then_inc(sig["mnT_ready"], 1)
                        act.wait_ge(sig["units_ready"], 1)
                        act.activation(hT[:], psum[:, 1, :], ACT.Gelu, bias=col[:, 8:9]).then_inc(sig["gelu_ready"], 1)

                    @block.vector
                    def _(dve):
                        steps = Steps(dve, sig["vector_steps"])
                        norm_vector(dve, sig, steps, "nq", lambda t: slots[:, t, :], nq, lambda t: sn[:, t, :])
                        dve.tensor_tensor(mid[:], slots[:], everywhere(3), ALU.add)
                        dve.wait_ge(sig["logits_ready"], 1)
                        steps.after(dve.tensor_reduce(smax[:], psum[:, 2, 0:S], AX.X, ALU.max))
                        dve.tensor_scalar(smax[:], smax[:], -float(D) ** 0.5, None, ALU.mult).then_inc(sig["max_ready"], 1)
                        dve.wait_ge(sig["exp_ready"], 1)
                        steps.after(dve.reciprocal(ssum[:], ssum[:]))
                        dve.tensor_scalar(attn[:], ex[:], ssum[:], SLOT_EPS, ALU.mult, ALU.add)\
                            .then_inc(sig["attn_ready"], 1)
                        dve.wait_ge(sig["count_ready"], 1)
                        steps.after(dve.reciprocal(rcount[:].rearrange("p (b t) -> p b t", b=2), psum[:, 5:7, 0:2]))
                        dve.wait_ge(sig["wu_ready"], 1)
                        for t in range(PT):
                            last = dve.scalar_tensor_tensor(mid[:, t, :], psum[:, 7, P * t:P * t + P], rcount[:, t:t + 1],
                                                            mid[:, t, :], ALU.mult, ALU.add)
                        steps.after(last)
                        norm_vector(dve, sig, steps, "nm", lambda t: mid[:, t, :], nm, lambda t: mn[:, t, :])
                        steps.after(dve.tensor_tensor(mid[:], mid[:], everywhere(4), ALU.add))
                        for b in range(2):
                            c = cond[:, ds(pair * 2 + b, 1), :].to_broadcast([P, 2, D])
                            last = dve.tensor_tensor(mid[:, 2 * b:2 * b + 2, :], mid[:, 2 * b:2 * b + 2, :], c, ALU.add)
                        steps.after(last)
                        dve.wait_ge(sig["mlp_ready"], 1)
                        steps.after(dve.tensor_tensor(mid[:], mid[:], tiles(2), ALU.add))
                        norm_vector(dve, sig, steps, "np", lambda t: mid[:, t, :], np_, lambda t: mn[:, t, :])
                        steps.after(dve.tensor_tensor(mn[:], mn[:], everywhere(5), ALU.mult))
                        dve.tensor_tensor(slots[:], mn[:], everywhere(6), ALU.add)

            with engines_pass(nc) as (block, sig):
                @block.vector
                def _(dve):
                    dve.tensor_tensor(xall, xall, slots[:], ALU.add)



HEADS = 16
KEEP = GROUP
H_DH = 64


def top_heads(nc, dram, X, psum, cst):
    with ExitStack() as ctx:
        def sb(name, shape, dt=F32):
            return ctx.enter_context(nc.sbuf_tensor("h0_" + name, shape, dt))

        wr, br = sb("wr", [P, HEADS]), sb("br", [B, HEADS])
        wo, bo = sb("wo", [P, 2, D]), sb("bo", [P, D])
        onesb = sb("onesb", [B, P])
        n0, n1 = norm_buffers(sb, "n0"), norm_buffers(sb, "n1")
        for n in (n0, n1):
            n["mhalf"] = cst["mhalf"]
        z, zT = sb("z", [P, PT, D]), sb("zT", [P, PTOK])
        tokens_sum = sb("tokens_sum", [P, B])
        dist, dmax, dsum = sb("dist", [B, HEADS]), sb("dmax", [B, 1]), sb("dsum", [B, 1])
        top, topi = sb("top", [B, 8]), sb("topi", [B, 8], U32)
        gexp, gmax, gsum, gother = sb("gexp", [B, KEEP]), sb("gmax", [B, 1]), sb("gsum", [B, 1]), sb("gother", [B, 1])
        gdiag, gates = sb("gdiag", [B, B, KEEP]), sb("gates", [P, B * KEEP])
        picked = sb("picked", [1, B * 8], U32)
        W = sb("w", [P, 3, KEEP, H_DH])
        bcol = sb("bcol", [P, 2, 2])
        brow = sb("brow", [P, KEEP, H_DH])
        gcol, gbat = sb("gcol", [P, 2]), sb("gbat", [P, KEEP])
        t2, tT = sb("t2", [P, 2, D]), sb("tT", [P, S])
        qT, kT = sb("qT", [P, 2, S]), sb("kT", [P, 2, S])
        qb, kb = sb("qb", [P, 2, S], BF16), sb("kb", [P, 2, S], BF16)
        v = sb("v", [P, 2, KEEP, H_DH + 1])
        vt = sb("vt", [P, 2, KEEP, H_DH])
        m = sb("m", [P, 2 * KEEP], BF16)
        probs = sb("probs", [P, 2, 2, GROUP * S])
        rsum = sb("rsum", [P, 2, GROUP])
        o, oT = sb("o", [P, 2, KEEP * H_DH]), sb("oT", [P, 2, S])

        with engines_pass(nc) as (block, sig):
            @block.sync
            def _(sp):
                for dst, src in ((wr, "H0_wr"), (wo, "H0_wo")):
                    sp.dma_start(dst[:], dram[src]).then_inc(sig["loads"], 16)
                sp.dma_start(br[:], dram["H0_br"].to_broadcast([B, HEADS])).then_inc(sig["loads"], 16)
                sp.dma_start(bo[:], dram["H0_bo"].to_broadcast([P, D])).then_inc(sig["loads"], 16)
                sp.wait_ge(sig["loads"], 64)

            @block.gpsimd
            def _(pool):
                pool.memset(onesb[:], 1.0)
                pool.memset(v[:, :, :, H_DH:H_DH + 1], 1.0)

        with nc.Fori(0, PAIRS) as pair:
            def x(t):
                return X[:, ds(pair * PT + t, 1), :].rearrange("p a d -> p (a d)")

            with engines_pass(nc) as (block, sig):
                @block.tensor
                def _(pe):
                    pe.wait_ge(sig["n0_normed"], 1)
                    turn_tensor(pe, cst["ident"], psum[:, 0, :], lambda t: z[:, t, :]).then_inc(sig["z_turned"], 1)

                @block.gpsimd
                def _(pool):
                    norm_pool(pool, sig, "n0", n0)

                @block.vector
                def _(dve):
                    steps = Steps(dve, sig["vector_steps"])
                    norm_vector(dve, sig, steps, "n0", x, n0, lambda t: z[:, t, :])
                    dve.wait_ge(sig["z_turned"], 1)
                    dve.tensor_reduce(tokens_sum[:, ds(pair * 2, 2)], psum[:, 0, :].rearrange("p (b s) -> p b s", b=2),
                                      AX.X, ALU.add)

        with engines_pass(nc) as (block, sig):
            @block.tensor
            def _(pe):
                pe.matmul(psum[0:B, 0, 0:HEADS], tokens_sum[:], wr[:], start=True, stop=True).then_inc(sig["logits_ready"], 1)
                pe.wait_ge(sig["gdiag_ready"], 1)
                pe.matmul(psum[:, 1, 0:B * KEEP], onesb[:], gdiag[:].rearrange("p b k -> p (b k)"), start=True, stop=True)\
                    .then_inc(sig["gates_ready"], 1)

            @block.scalar
            def _(act):
                act.wait_ge(sig["dist_shifted"], 1)
                act.activation(dist[:], dist[:], ACT.Exp, accum_out=dsum[:]).then_inc(sig["dist_exp"], 1)
                act.wait_ge(sig["top_ready"], 1)
                act.activation(gexp[:], top[:, 0:KEEP], ACT.Exp, bias=gmax[:], accum_out=gsum[:])
                act.activation(gother[:], gmax[:], ACT.Exp).then_inc(sig["gate_exp"], 1)

            @block.vector
            def _(dve):
                steps = Steps(dve, sig["vector_steps"])
                dve.wait_ge(sig["logits_ready"], 1)
                steps.after(dve.scalar_tensor_tensor(dist[:], psum[0:B, 0, 0:HEADS], 1.0 / S, br[:], ALU.mult, ALU.add))
                steps.after(dve.tensor_reduce(dmax[:], dist[:], AX.X, ALU.max))
                dve.tensor_scalar(dist[:], dist[:], dmax[:], None, ALU.subtract).then_inc(sig["dist_shifted"], 1)
                dve.wait_ge(sig["dist_exp"], 1)
                steps.after(dve.reciprocal(dsum[:], dsum[:]))
                steps.after(dve.tensor_scalar(dist[:], dist[:], dsum[:], None, ALU.mult))
                steps.after(dve.max(top[:], dist[:]))
                dve.max_index(topi[:], top[:], dist[:]).then_inc(sig["picked_ready"], 1)
                dve.tensor_scalar(gmax[:], top[:, 0:1], -1.0, None, ALU.mult).then_inc(sig["top_ready"], 1)
                dve.wait_ge(sig["gate_exp"], 1)
                steps.after(dve.scalar_tensor_tensor(gsum[:], gother[:], float(HEADS - KEEP), gsum[:], ALU.mult, ALU.add))
                steps.after(dve.reciprocal(gsum[:], gsum[:]))
                steps.after(dve.tensor_scalar(gexp[:], gexp[:], gsum[:], None, ALU.mult))
                dve.tensor_tensor(gdiag[:], gexp[:].unsqueeze(1).to_broadcast([B, B, KEEP]),
                                  cst["ident"][0:B, 0:B].unsqueeze(2).to_broadcast([B, B, KEEP]), ALU.mult)\
                    .then_inc(sig["gdiag_ready"], 1)
                dve.wait_ge(sig["gates_ready"], 1)
                dve.tensor_copy(gates[:], psum[:, 1, 0:B * KEEP])

            @block.sync
            def _(sp):
                sp.wait_ge(sig["picked_ready"], 1)
                sp.dma_start(picked[:], topi[:]).then_inc(sig["picked_moved"], 16)
                sp.wait_ge(sig["picked_moved"], 16)

        with nc.Fori(0, B) as b:
            def xb(t):
                return X[:, ds(b * 2 + t, 1), :].rearrange("p a d -> p (a d)")

            xboth = X[:, ds(b * 2, 2), :]
            own = Attention("self", 1, 2, 1, H_DH, 2, S, H_DH ** -0.5)

            def place(h):
                return slice(H_DH * (h % 2), H_DH * (h % 2) + H_DH), h // 2

            def own_max(u, h):
                r, ch = place(h)
                return [(slice(256 * t, 256 * t + 256), [(qb[r, ch, P * t:P * t + P], kb[r, ch, :])]) for t in range(2)]

            def own_scores(u, c, h):
                r, ch = place(h)
                return [(0, [(kT[r, ch, P * c:P * c + P], qT[r, ch, :])])]

            def own_values(u, h, r, t, p):
                return [(p[:, c, prob_cols(h, P * t)], v[:, c, h, :]) for c in range(2)]

            own.max_products, own.score_products, own.value_products = own_max, own_scores, own_values
            own.max_column = lambda u, h, out, t: h * 2 + t
            own.key_bias = lambda u, c: 0.0
            own.neg_ident = cst["neg_ident"][:]

            with engines_pass(nc) as (block, sig):
                @block.sync
                def _(sp):
                    for k in range(KEEP):
                        head = sp.value_load(picked[0:1, ds(b * 8 + k, 1)], min_val=0, max_val=HEADS - 1)
                        r, ch = place(k)
                        sp.dma_start(W[:, :, k, :], dram["H0_W"][:, :, ds(head, 1), :].rearrange("p i a e -> p i (a e)"))\
                            .then_inc(sig["weights"], 16)
                        sp.dma_start(bcol[r, ch, :], dram["H0_bcol"][ds(head, 1), :, :].rearrange("a e i -> (a e) i"))\
                            .then_inc(sig["biases"], 16)
                        sp.dma_start(brow[:, k, :], dram["H0_bv"][ds(head, 1), :].to_broadcast([P, H_DH]))\
                            .then_inc(sig["biases"], 16)

                @block.tensor
                def _(pe):
                    pe.wait_ge(sig["n1_normed"], 1)
                    turn_tensor(pe, cst["ident"], psum[:, 7, :], lambda t: t2[:, t, :], tiles=2).then_inc(sig["turned"], 1)
                    pe.wait_ge(sig["tT_ready"], 1)
                    pe.wait_ge(sig["weights"], 16 * KEEP)
                    for i in range(2):
                        for ch in range(2):
                            pe.matmul(psum[:, 2 * i + ch, 0:S], W[:, i, 2 * ch:2 * ch + 2, :].rearrange("p k e -> p (k e)"),
                                      tT[:], start=True, stop=True).then_inc(sig["proj_ready"], 1)
                    for t in range(2):
                        pe.matmul(psum[:, 4 + t, 0:S], tT[:, P * t:P * t + P], W[:, 2, :, :].rearrange("p k e -> p (k e)"),
                                  start=True, stop=True).then_inc(sig["proj_ready"], 1)
                    pe.wait_ge(sig["operands_ready"], 1)
                    attention_tensor(pe, sig, own, psum, m, probs)
                    pe.wait_ge(sig["self_values_taken"], 1)
                    for ch in range(2):
                        last = turn_tensor(pe, cst["ident"], psum[:, ch, :], lambda t: o[:, t, P * ch:P * ch + P], tiles=2)
                    last.then_inc(sig["out_turned"], 1)
                    pe.wait_ge(sig["oT_ready"], 1)
                    for t in range(2):
                        for ch in range(2):
                            last = pe.matmul(psum[:, 2, P * t:P * t + P], oT[:, ch, P * t:P * t + P], wo[:, ch, :],
                                             start=ch == 0, stop=ch == 1)
                    last.then_inc(sig["projected"], 1)

                @block.gpsimd
                def _(pool):
                    norm_pool(pool, sig, "n1", n1, tiles=2)

                @block.scalar
                def _(act):
                    act.wait_ge(sig["turned"], 1)
                    act.copy(tT[:], psum[:, 7, 0:S]).then_inc(sig["tT_ready"], 1)
                    attention_scalar(act, sig, own, psum, probs)
                    act.wait_ge(sig["out_turned"], 1)
                    act.copy(oT[:], psum[:, 0:2, 0:S]).then_inc(sig["oT_ready"], 1)

                @block.vector
                def _(dve):
                    steps = Steps(dve, sig["vector_steps"])
                    norm_vector(dve, sig, steps, "n1", xb, n1, lambda t: t2[:, t, :], tiles=2)
                    dve.tensor_copy(gbat[:], gates[:, ds(b * KEEP, KEEP)]).then_inc(sig["gates_taken"], 1)
                    dve.wait_ge(sig["gates_taken"], 1)
                    halves = gbat[:].rearrange("p (c h) -> p c h", h=2)
                    dve.tensor_copy(gcol[0:H_DH, :], halves[0:H_DH, :, 0])
                    steps.after(dve.tensor_copy(gcol[H_DH:P, :], halves[H_DH:P, :, 1]))
                    dve.wait_ge(sig["biases"], 32 * KEEP)
                    for i, dst in enumerate((qT, kT)):
                        for ch in range(2):
                            dve.wait_ge(sig["proj_ready"], 2 * i + ch + 1)
                            last = dve.tensor_scalar(dst[:, ch, :], psum[:, 2 * i + ch, 0:S], bcol[:, ch, i:i + 1],
                                                     gcol[:, ch:ch + 1], ALU.add, ALU.mult)
                    steps.after(last)
                    dve.tensor_copy(qb[:], qT[:])
                    dve.tensor_copy(kb[:], kT[:])
                    dve.wait_ge(sig["proj_ready"], 6)
                    steps.after(dve.tensor_tensor(vt[:].rearrange("p t k e -> p t (k e)"), psum[:, 4:6, 0:S],
                                                  brow[:].rearrange("p k e -> p (k e)").unsqueeze(1).to_broadcast([P, 2, S]),
                                                  ALU.add))
                    for k in range(KEEP):
                        last = dve.tensor_scalar(v[:, :, k, 0:H_DH], vt[:, :, k, :], gbat[:, k:k + 1], None, ALU.mult)
                    last.then_inc(sig["operands_ready"], 1)
                    attention_vector(dve, sig, steps, own, psum, m, rsum,
                                     lambda u, r, t: o[:, t, :].rearrange("p (h e) -> p h e", e=H_DH))
                    steps.after(dve.tensor_tensor(xboth, xboth, bo[:].unsqueeze(1).to_broadcast([P, 2, D]), ALU.add))
                    dve.wait_ge(sig["projected"], 1)
                    dve.tensor_tensor(xboth, xboth, psum[:, 2, 0:2 * D].rearrange("p (t d) -> p t d", t=2), ALU.add)



STEPS_A_PASS = 8
HB = B // 2


def attentive_gru(nc, dram, X, psum, cst):
    with ExitStack() as ctx:
        def sb(name, shape, dt=F32):
            return ctx.enter_context(nc.sbuf_tensor("g1_" + name, shape, dt))

        wa = sb("wa", [P, 2, D])
        wi = sb("wi", [P, 2, 3, D])
        uh = sb("uh", [P, 3, D])
        bias = sb("bias", [P, 3])
        vcol = sb("vcol", [P, 1])
        vneg = sb("vneg", [P, B, B])
        ctxT, enc = sb("ctxT", [P, B * C]), sb("enc", [C, B, D])
        n0 = norm_buffers(sb, "n0")
        n0["mhalf"] = cst["mhalf"]
        z, zT = sb("z", [P, PT, D]), sb("zT", [P, PTOK])
        GX = sb("gx", [P, 3, B, S])
        HT = sb("ht", [P, B, S])
        encp = sb("encp", [P, B, C])
        h = sb("h", [P, 2, B])
        pre, th = sb("pre", [P, B, C]), sb("th", [P, B, C])
        smin, ssum, attn, attnT = sb("smin", [B, 1]), sb("ssum", [B, 1]), sb("attn", [B, C]), sb("attnT", [C, B])
        cvec = sb("cvec", [P, B])
        zr, tzr = sb("zr", [P, 2, B]), sb("tzr", [P, 2, B])
        gh, u, cand, keepz, omz, zh, part = (sb(n, [P, B]) for n in ("gh", "u", "cand", "keepz", "omz", "zh", "part"))

        with engines_pass(nc) as (block, sig):
            @block.sync
            def _(sp):
                for dst, src in ((wa, "G1_wa"), (wi, "G1_wi"), (uh, "G1_uh"), (bias, "G1_bias"), (vcol, "G1_v"),
                                 (ctxT, "ctxT"), (enc, "G1_enc")):
                    sp.dma_start(dst[:], dram[src]).then_inc(sig["loads"], 16)
                sp.dma_start(h[:, 0, :], dram["embT"]).then_inc(sig["loads"], 16)

            @block.tensor
            def _(pe):
                pe.wait_ge(sig["loads"], 128)
                pe.matmul(psum[:, 0, :], wa[:, 1, :], ctxT[:], start=True, stop=True).then_inc(sig["encp_ready"], 1)

            @block.scalar
            def _(act):
                act.wait_ge(sig["encp_ready"], 1)
                act.copy(encp[:].rearrange("p b s -> p (b s)"), psum[:, 0, :])

            @block.vector
            def _(dve):
                steps = Steps(dve, sig["vector_steps"])
                dve.wait_ge(sig["loads"], 128)
                steps.after(dve.memset(vneg[:], 0.0))
                for b in range(B):
                    dve.tensor_scalar(vneg[:, b, b:b + 1], vcol[:], -1.0, None, ALU.mult)

        with nc.Fori(0, PAIRS) as pair:
            def x(t):
                return X[:, ds(pair * PT + t, 1), :].rearrange("p a d -> p (a d)")

            with engines_pass(nc) as (block, sig):
                @block.tensor
                def _(pe):
                    pe.wait_ge(sig["n0_normed"], 1)
                    turn_tensor(pe, cst["ident"], psum[:, 0, :], lambda t: z[:, t, :]).then_inc(sig["z_turned"], 1)
                    pe.wait_ge(sig["zT_ready"], 1)
                    for i in range(3):
                        pe.matmul(psum[:, 1 + i, :], wi[:, 0, i, :], zT[:], start=True, stop=True)\
                            .then_inc(sig["gates_ready"], 1)

                @block.gpsimd
                def _(pool):
                    norm_pool(pool, sig, "n0", n0)

                @block.scalar
                def _(act):
                    act.wait_ge(sig["z_turned"], 1)
                    act.copy(zT[:], psum[:, 0, :]).then_inc(sig["zT_ready"], 1)
                    for i in range(3):
                        act.wait_ge(sig["gates_ready"], i + 1)
                        act.activation(GX[:, i, ds(pair * 2, 2), :], psum[:, 1 + i, :].rearrange("p (b s) -> p b s", b=2),
                                       ACT.Identity, bias=bias[:, i:i + 1])

                @block.vector
                def _(dve):
                    steps = Steps(dve, sig["vector_steps"])
                    norm_vector(dve, sig, steps, "n0", x, n0, lambda t: z[:, t, :])

        with nc.Fori(0, S // STEPS_A_PASS) as group:
            with engines_pass(nc) as (block, sig):
                @block.tensor
                def _(pe):
                    for s in range(STEPS_A_PASS):
                        hs = h[:, s % 2, :]
                        if s >= 1:
                            pe.wait_ge(sig["state_ready"], s)
                        pe.matmul(psum[:, 0, 0:B], wa[:, 0, :], hs, start=True, stop=True).then_inc(sig["query_ready"], 1)
                        pe.matmul(psum[:, 4, 0:B], uh[:, 0, :], hs, start=True, stop=False)
                        pe.matmul(psum[:, 5, 0:B], uh[:, 1, :], hs, start=True, stop=False)
                        pe.matmul(psum[:, 6, 0:B], uh[:, 2, :], hs, start=True, stop=True)
                        for b in range(B):
                            if b % HB == 0:
                                pe.wait_ge(sig["tanh_ready"], 2 * s + b // HB + 1)
                            last = pe.matmul(psum[0:B, 1, 0:C], vneg[:, b, :], th[:, b, :], start=b == 0, stop=b == B - 1)
                        last.then_inc(sig["scores_ready"], 1)
                        pe.wait_ge(sig["attn_ready"], s + 1)
                        pe.transpose(psum[0:C, 2, 0:B], attn[:], cst["ident"][0:B, 0:B]).then_inc(sig["attn_turned"], 1)
                        pe.wait_ge(sig["attnT_ready"], s + 1)
                        for b in range(B):
                            last = pe.matmul(psum[:, 3, b:b + 1], enc[:, b, :], attnT[:, b:b + 1], start=True, stop=True)
                        last.then_inc(sig["context_ready"], 1)
                        pe.wait_ge(sig["context_taken"], s + 1)
                        pe.matmul(psum[:, 5, 0:B], wi[:, 1, 1, :], cvec[:], start=False, stop=True)
                        pe.matmul(psum[:, 4, 0:B], wi[:, 1, 0, :], cvec[:], start=False, stop=True)\
                            .then_inc(sig["gates_ready"], 1)
                        pe.matmul(psum[:, 7, 0:B], wi[:, 1, 2, :], cvec[:], start=True, stop=True)\
                            .then_inc(sig["candidate_part_ready"], 1)

                @block.scalar
                def _(act):
                    for s in range(STEPS_A_PASS):
                        for half in range(2):
                            act.wait_ge(sig["tanh_input_ready"], 2 * s + half + 1)
                            bs = slice(HB * half, HB * half + HB)
                            act.activation(th[:, bs, :], pre[:, bs, :], ACT.Tanh).then_inc(sig["tanh_ready"], 1)
                        act.wait_ge(sig["smin_ready"], s + 1)
                        act.activation(attn[:], psum[0:B, 1, 0:C], ACT.Exp, bias=smin[:], scale=-1.0,
                                       accum_out=ssum[:]).then_inc(sig["exp_ready"], 1)
                        act.wait_ge(sig["zr_ready"], s + 1)
                        act.activation(tzr[:], zr[:], ACT.Tanh, scale=0.5).then_inc(sig["tanh_zr_ready"], 1)
                        act.wait_ge(sig["candidate_input_ready"], s + 1)
                        act.activation(cand[:], u[:], ACT.Tanh).then_inc(sig["candidate_ready"], 1)

                @block.gpsimd
                def _(pool):
                    for s in range(STEPS_A_PASS):
                        pool.wait_ge(sig["state_ready"], s + 1)
                        pool.tensor_copy(HT[:, :, ds(group * STEPS_A_PASS + s, 1)], h[:, (s + 1) % 2, :].unsqueeze(2))\
                            .then_inc(sig["state_kept"], 1)

                @block.vector
                def _(dve):
                    steps = Steps(dve, sig["vector_steps"])

                    def gx(i, n):
                        return GX[:, i:i + n, :, ds(group * STEPS_A_PASS + s, 1)].rearrange("p i b a -> p i (b a)")

                    for s in range(STEPS_A_PASS):
                        dve.wait_ge(sig["query_ready"], s + 1)
                        for half in range(2):
                            bs = slice(HB * half, HB * half + HB)
                            dve.tensor_tensor(pre[:, bs, :], encp[:, bs, :],
                                              psum[:, 0, bs].unsqueeze(2).to_broadcast([P, HB, C]), ALU.add)\
                                .then_inc(sig["tanh_input_ready"], 1)
                        dve.wait_ge(sig["scores_ready"], s + 1)
                        dve.tensor_reduce(smin[:], psum[0:B, 1, 0:C], AX.X, ALU.min).then_inc(sig["smin_ready"], 1)
                        dve.wait_ge(sig["exp_ready"], s + 1)
                        steps.after(dve.reciprocal(ssum[:], ssum[:]))
                        dve.tensor_scalar(attn[:], attn[:], ssum[:], None, ALU.mult).then_inc(sig["attn_ready"], 1)
                        dve.wait_ge(sig["attn_turned"], s + 1)
                        dve.tensor_copy(attnT[:], psum[0:C, 2, 0:B]).then_inc(sig["attnT_ready"], 1)
                        dve.wait_ge(sig["context_ready"], s + 1)
                        dve.tensor_copy(cvec[:], psum[:, 3, 0:B]).then_inc(sig["context_taken"], 1)
                        dve.wait_ge(sig["gates_ready"], s + 1)
                        dve.tensor_tensor(zr[:], psum[:, 4:6, 0:B], gx(0, 2), ALU.add).then_inc(sig["zr_ready"], 1)
                        dve.wait_ge(sig["candidate_part_ready"], s + 1)
                        steps.after(dve.tensor_tensor(gh[:].unsqueeze(1), psum[:, 7:8, 0:B], gx(2, 1), ALU.add))
                        dve.wait_ge(sig["tanh_zr_ready"], s + 1)
                        steps.after(dve.scalar_tensor_tensor(u[:], tzr[:, 1, :], 1.0, psum[:, 6, 0:B], ALU.add, ALU.mult))
                        dve.scalar_tensor_tensor(u[:], u[:], 0.5, gh[:], ALU.mult, ALU.add)\
                            .then_inc(sig["candidate_input_ready"], 1)
                        dve.tensor_scalar(omz[:], tzr[:, 0, :], -0.5, 0.5, ALU.mult, ALU.add)
                        steps.after(dve.tensor_scalar(keepz[:], tzr[:, 0, :], 0.5, 0.5, ALU.mult, ALU.add))
                        steps.after(dve.tensor_tensor(zh[:], keepz[:], h[:, s % 2, :], ALU.mult))
                        dve.wait_ge(sig["candidate_ready"], s + 1)
                        steps.after(dve.tensor_tensor(part[:], omz[:], cand[:], ALU.mult))
                        if s >= 1:
                            dve.wait_ge(sig["state_kept"], s)
                        dve.tensor_tensor(h[:, (s + 1) % 2, :], part[:], zh[:], ALU.add).then_inc(sig["state_ready"], 1)
                        dve.wait_ge(sig["state_ready"], s + 1)

        with engines_pass(nc) as (block, sig):
            @block.tensor
            def _(pe):
                for i in range(PAIRS):
                    for t in range(PT):
                        b, half = 2 * i + t // 2, t % 2
                        last = pe.transpose(psum[:, i, P * t:P * t + P], HT[:, b, P * half:P * half + P], cst["ident"][:])
                    last.then_inc(sig["states_turned"], 1)

            @block.vector
            def _(dve):
                for i in range(PAIRS):
                    dve.wait_ge(sig["states_turned"], i + 1)
                    xs = X[:, PT * i:PT * i + PT, :]
                    dve.tensor_tensor(xs, xs, psum[:, i, :].rearrange("p (t d) -> p t d", t=PT), ALU.add)



CAP = B * S // 8


def switch_experts(nc, dram, X, psum, cst):
    with ExitStack() as ctx:
        def sb(name, shape, dt=F32):
            return ctx.enter_context(nc.sbuf_tensor("s1_" + name, shape, dt))

        sent = nc.dram_tensor("s1_sent", (E * CAP, D), F32, kind="Internal").ap()
        back = nc.dram_tensor("s1_back", (E * CAP, D), F32, kind="Internal").ap()
        wr, number, before, ones = sb("wr", [P, E]), sb("number", [P, E]), sb("before", [P, P]), sb("ones", [P, P])
        zeros = sb("zeros", [P, 2, D])
        n0 = norm_buffers(sb, "n0")
        n0["mhalf"] = cst["mhalf"]
        XN = sb("xn", [P, TILES, D])
        z, zT = sb("z", [P, PT, D]), sb("zT", [P, PTOK])
        logits, ex, lmax, lsum = sb("logits", [P, PT, E]), sb("ex", [P, PT, E]), sb("lmax", [P, PT]), sb("lsum", [P, PT])
        top, topi, topf = sb("top", [P, PT, 8]), sb("topi", [P, PT, 8], U32), sb("topf", [P, PT, 1])
        chosen = sb("chosen", [P, TILES, E])
        earlier = sb("earlier", [P, TILES, E])
        gate, expert = sb("gate", [P, TILES]), sb("expert", [P, TILES])
        place3, place = sb("place3", [P, TILES, E]), sb("place", [P, TILES])
        keep, slot, away = sb("keep", [P, TILES]), sb("slot", [P, TILES]), sb("away", [P, TILES])
        slot_i, away_i = sb("slot_i", [P, TILES], U32), sb("away_i", [P, TILES], U32)
        w1, w2 = sb("w1", [P, EF, P]), sb("w2", [P, EF, D])
        tok, tokT, hid, res = sb("tok", [P, 2, D]), sb("tokT", [P, CAP]), sb("hid", [P, EF, CAP]), sb("res", [P, 2, D])
        got = sb("got", [P, TILES, D])

        with engines_pass(nc) as (block, sig):
            @block.sync
            def _(sp):
                sp.dma_start(wr[:], dram["S1_wr"]).then_inc(sig["loads"], 16)
                sp.dma_start(before[:], dram["c_before"]).then_inc(sig["loads"], 16)
                sp.dma_start(number[:], dram["c_number"].to_broadcast([P, E])).then_inc(sig["loads"], 16)
                sp.wait_ge(sig["zeros_ready"], 1)
                for e in range(E):
                    sp.dma_start(sent[CAP * e:CAP * (e + 1), :].rearrange("(t p) d -> p t d", p=P), zeros[:])\
                        .then_inc(sig["cleared"], 16)
                sp.wait_ge(sig["cleared"], 16 * E)
                sp.wait_ge(sig["loads"], 48)

            @block.gpsimd
            def _(pool):
                pool.memset(zeros[:], 0.0).then_inc(sig["zeros_ready"], 1)
                pool.memset(ones[:], 1.0)

        with nc.Fori(0, PAIRS) as pair:
            def x(t):
                return X[:, ds(pair * PT + t, 1), :].rearrange("p a d -> p (a d)")

            with engines_pass(nc) as (block, sig):
                @block.tensor
                def _(pe):
                    pe.wait_ge(sig["n0_normed"], 1)
                    turn_tensor(pe, cst["ident"], psum[:, 0, :], lambda t: z[:, t, :]).then_inc(sig["z_turned"], 1)
                    pe.wait_ge(sig["zT_ready"], 1)
                    for t in range(PT):
                        last = pe.matmul(psum[:, 1, E * t:E * t + E], zT[:, P * t:P * t + P], wr[:], start=True, stop=True)
                    last.then_inc(sig["logits_ready"], 1)

                @block.gpsimd
                def _(pool):
                    norm_pool(pool, sig, "n0", n0)
                    pool.wait_ge(sig["n0_normed"], 1)
                    pool.tensor_copy(XN[:, ds(pair * PT, PT), :], z[:])

                @block.scalar
                def _(act):
                    act.wait_ge(sig["z_turned"], 1)
                    act.copy(zT[:], psum[:, 0, :]).then_inc(sig["zT_ready"], 1)
                    act.wait_ge(sig["shifted_logits_ready"], 1)
                    act.activation(ex[:], logits[:], ACT.Exp).then_inc(sig["exp_ready"], 1)

                @block.vector
                def _(dve):
                    steps = Steps(dve, sig["vector_steps"])

                    def wide(col):
                        return col.unsqueeze(2).to_broadcast([P, PT, E])

                    norm_vector(dve, sig, steps, "n0", x, n0, lambda t: z[:, t, :])
                    dve.wait_ge(sig["logits_ready"], 1)
                    steps.after(dve.tensor_copy(logits[:], psum[:, 1, 0:PT * E].rearrange("p (t e) -> p t e", e=E)))
                    steps.after(dve.tensor_reduce(lmax[:], logits[:], AX.X, ALU.max))
                    dve.tensor_tensor(logits[:], logits[:], wide(lmax[:]), ALU.subtract)\
                        .then_inc(sig["shifted_logits_ready"], 1)
                    dve.wait_ge(sig["exp_ready"], 1)
                    steps.after(dve.tensor_reduce(lsum[:], ex[:], AX.X, ALU.add))
                    for t in range(PT):
                        last = dve.max(top[:, t, :], ex[:, t, :])
                    steps.after(last)
                    for t in range(PT):
                        last = dve.max_index(topi[:, t, :], top[:, t, :], ex[:, t, :])
                    steps.after(last)
                    steps.after(dve.tensor_copy(topf[:], topi[:, :, 0:1]))
                    dve.reciprocal(gate[:, ds(pair * PT, PT)], lsum[:])
                    dve.tensor_copy(expert[:, ds(pair * PT, PT)].unsqueeze(2), topf[:])
                    dve.tensor_tensor(chosen[:, ds(pair * PT, PT), :], topf[:].to_broadcast([P, PT, E]),
                                      number[:].unsqueeze(1).to_broadcast([P, PT, E]), ALU.is_equal)

        with engines_pass(nc) as (block, sig):
            @block.tensor
            def _(pe):
                pe.wait_ge(sig["vector_steps"], TILES)
                for i in range(TILES):
                    out = psum[:, 0, E * i:E * i + E]
                    pe.matmul(out, before[:], chosen[:, i, :], start=True, stop=False)
                    last = pe.matmul(out, ones[:], earlier[:, i, :], start=False, stop=True)
                last.then_inc(sig["counts_ready"], 1)

            @block.vector
            def _(dve):
                steps = Steps(dve, sig["vector_steps"])
                steps.after(dve.memset(earlier[:, 0, :], 0.0))
                for i in range(1, TILES):
                    steps.after(dve.tensor_tensor(earlier[:, i, :], earlier[:, i - 1, :], chosen[:, i - 1, :], ALU.add))
                dve.wait_ge(sig["counts_ready"], 1)
                steps.after(dve.tensor_tensor(place3[:], psum[:, 0, 0:TILES * E].rearrange("p (t e) -> p t e", e=E),
                                              chosen[:], ALU.mult))
                steps.after(dve.tensor_reduce(place[:], place3[:], AX.X, ALU.add))
                steps.after(dve.tensor_scalar(keep[:], place[:], float(CAP), None, ALU.is_lt))
                steps.after(dve.tensor_scalar(slot[:], place[:], float(CAP - 1), None, ALU.min))
                steps.after(dve.scalar_tensor_tensor(slot[:], expert[:], float(CAP), slot[:], ALU.mult, ALU.add))
                steps.after(dve.tensor_scalar(away[:], keep[:], -float(2 * E * CAP), float(2 * E * CAP), ALU.mult, ALU.add))
                steps.after(dve.tensor_tensor(away[:], away[:], slot[:], ALU.add))
                steps.after(dve.tensor_tensor(gate[:], gate[:], keep[:], ALU.mult))
                dve.tensor_copy(slot_i[:], slot[:])
                dve.tensor_copy(away_i[:], away[:]).then_inc(sig["slots_ready"], 1)

            @block.gpsimd
            def _(pool):
                pool.wait_ge(sig["slots_ready"], 1)
                for i in range(TILES):
                    pool.indirect_dma_start(out=sent[:, :], out_offset=bass.IndirectOffsetOnAxis(ap=away_i[:, i:i + 1], axis=0),
                                            in_=XN[:, i, :], in_offset=None, bounds_check=E * CAP - 1, oob_is_err=False)\
                        .then_inc(cst["tokens_sent"], 16)
                pool.wait_ge(cst["tokens_sent"], 16 * TILES)

        with nc.Fori(0, E) as e:
            with engines_pass(nc) as (block, sig):
                @block.sync
                def _(sp):
                    sp.dma_start(tok[:], sent[ds(e * CAP, CAP), :].rearrange("(t p) d -> p t d", p=P))\
                        .then_inc(sig["tokens"], 16)
                    sp.dma_start(w1[:], dram["S1_w1"][ds(e, 1)].rearrange("a p f n -> (a p) f n")).then_inc(sig["w1"], 16)
                    sp.dma_start(w2[:], dram["S1_w2"][ds(e, 1)].rearrange("a p f n -> (a p) f n")).then_inc(sig["w2"], 16)
                    sp.wait_ge(sig["res_ready"], 1)
                    sp.dma_start(back[ds(e * CAP, CAP), :].rearrange("(t p) d -> p t d", p=P), res[:])\
                        .then_inc(sig["returned"], 16)
                    sp.wait_ge(sig["returned"], 16)

                @block.tensor
                def _(pe):
                    pe.wait_ge(sig["tokens"], 16)
                    turn_tensor(pe, cst["ident"], psum[:, 0, :], lambda t: tok[:, t, :], tiles=2)\
                        .then_inc(sig["tokens_turned"], 1)
                    pe.wait_ge(sig["tokT_ready"], 1)
                    pe.wait_ge(sig["w1"], 16)
                    for i in range(EF):
                        pe.matmul(psum[:, 1 + i, 0:CAP], w1[:, i, :], tokT[:], start=True, stop=True)\
                            .then_inc(sig["units_ready"], 1)
                    pe.wait_ge(sig["w2"], 16)
                    pe.wait_ge(sig["gelu_ready"], EF)
                    for t in range(2):
                        for i in range(EF):
                            last = pe.matmul(psum[:, 5, P * t:P * t + P], hid[:, i, P * t:P * t + P], w2[:, i, :],
                                             start=i == 0, stop=i == EF - 1)
                    last.then_inc(sig["result_ready"], 1)

                @block.vector
                def _(dve):
                    dve.wait_ge(sig["tokens_turned"], 1)
                    dve.tensor_copy(tokT[:], psum[:, 0, 0:CAP]).then_inc(sig["tokT_ready"], 1)
                    dve.wait_ge(sig["result_ready"], 1)
                    dve.tensor_copy(res[:].rearrange("p t d -> p (t d)"), psum[:, 5, 0:2 * D]).then_inc(sig["res_ready"], 1)

                @block.scalar
                def _(act):
                    for i in range(EF):
                        act.wait_ge(sig["units_ready"], i + 1)
                        act.activation(hid[:, i, :], psum[:, 1 + i, 0:CAP], ACT.Gelu_apprx_tanh)\
                            .then_inc(sig["gelu_ready"], 1)

        with engines_pass(nc) as (block, sig):
            @block.gpsimd
            def _(pool):
                for i in range(TILES):
                    pool.indirect_dma_start(out=got[:, i, :], out_offset=None, in_=back[:, :],
                                            in_offset=bass.IndirectOffsetOnAxis(ap=slot_i[:, i:i + 1], axis=0))\
                        .then_inc(cst["results_got"], 16)

            @block.vector
            def _(dve):
                dve.wait_ge(cst["results_got"], 16 * TILES)
                for i in range(TILES):
                    dve.scalar_tensor_tensor(X[:, i, :], got[:, i, :], gate[:, i:i + 1], X[:, i, :], ALU.mult, ALU.add)



L2_LAYERS = 6
L2_DH = 8
L2_FF = 4
L2_W = {"q": 0, "qs": 128, "k": 256, "ks": 384, "v": 512, "so": 640, "cq": 768, "cqs": 896, "ck": 1024,
        "cks": 1152, "cv": 1280, "co": 1408, "f1": 1536, "f2": 2048}
L2_WCOLS = 2560


def dit_layers(nc, dram, X, psum, cst):
    with ExitStack() as ctx:
        def sb(name, shape, dt=F32):
            return ctx.enter_context(nc.sbuf_tensor("l2_" + name, shape, dt))

        Y = sb("y", [P, TILES, D])
        nw = sb("nw", [P, L2_LAYERS * 3 * 2, D])
        nb = sb("nb", [P, L2_LAYERS * 3 * 2])
        embT = sb("embT", [P, B])
        ada = sb("ada", [P, L2_LAYERS * 3 * 2 * B])
        W = sb("w", [P, L2_WCOLS])
        f1b = sb("f1b", [P, L2_LAYERS * L2_FF])
        f2b = sb("f2b", [P, L2_LAYERS, D])
        f2bl = sb("f2bl", [P, D])
        ctxT = sb("ctxT", [P, B * C])
        cctx = sb("cctx", [P, 2 * C])
        mcol = sb("mcol", [P, TILES])
        mccol = sb("mccol", [P, PAIRS])
        mrow8 = sb("mrow8", [P, B * S], U8)
        mcrow8 = sb("mcrow8", [P, B * C], U8)
        mcol8 = sb("mcol8", [P, TILES], U8)
        mccol8 = sb("mccol8", [P, PAIRS], U8)
        mrow = sb("mrow", [P, B * S], BF16)
        mcrow = sb("mcrow", [P, B * C], BF16)
        ones = sb("ones", [P, P], BF16)
        pmask, pcmask = sb("pmask", [P, 2 * S], BF16), sb("pcmask", [P, 2 * C], BF16)
        n1, n2, n3 = (norm_buffers(sb, n) for n in ("n1", "n2", "n3"))
        for n in (n1, n2, n3):
            n["mhalf"] = cst["mhalf"]
        xn = sb("xn", [P, PT, D])
        xnT = sb("xnT", [P, PTOK])
        t1, t2 = sb("t1", [P, PTOK]), sb("t2", [P, PTOK])
        qT, kT = sb("qT", [P, PTOK]), sb("kT", [P, PTOK])
        qm = sb("qm", [P, GROUP, PTOK])
        qmb = sb("qmb", [P, GROUP, PTOK], BF16)
        kb = sb("kb", [P, PTOK], BF16)
        v = sb("v", [P, PT, H, L2_DH + 1])
        m = sb("m", [P, H * 4], BF16)
        m2 = sb("m2", [P, H * 4], BF16)
        probs = sb("probs", [P, 2, 2, GROUP * S])
        rsum = sb("rsum", [P, 2, GROUP])
        o = sb("o", [P, PT, D])
        oT = sb("oT", [P, PTOK])
        hT = sb("hT", [P, L2_FF, PTOK])

        with engines_pass(nc) as (block, sig):
            @block.sync
            def _(sp):
                for dst, src in ((nw, "L2_nw"), (nb, "L2_nb"), (embT, "embT"), (f1b, "L2_f1b"),
                                 (ctxT, "ctxT"), (mcol8, "mask_col"), (mccol8, "cmask_col")):
                    sp.dma_start(dst[:], dram[src]).then_inc(sig["loads"], 16)
                for dst, src, n in ((mrow8, "mask_row", B * S), (mcrow8, "cmask_row", B * C)):
                    sp.dma_start(dst[:], dram[src].to_broadcast([P, n])).then_inc(sig["loads"], 16)
                sp.dma_start(f2b[:].rearrange("p l d -> p (l d)"),
                             dram["L2_f2b"].to_broadcast([P, L2_LAYERS * D])).then_inc(sig["loads"], 16)

            @block.tensor
            def _(pe):
                pe.wait_ge(sig["loads"], 160)
                for i in range(L2_LAYERS * 3 * 2):
                    last = pe.matmul(psum[:, 0, i * B:(i + 1) * B], nw[:, i, :], embT[:], start=True, stop=True)
                last.then_inc(sig["ada_ready"], 1)

            @block.gpsimd
            def _(pool):
                pool.memset(ones[:], 1.0)
                pool.memset(v[:, :, :, L2_DH:L2_DH + 1], 1.0)
                for i in range(PAIRS):
                    w = {k: (t if k == "mhalf" else t) for k, t in n1.items()}
                    pool.wait_ge(sig["x_var_ready"], i + 1)
                    pool.tensor_scalar(w["veps"][:], w["mv"][:, :, 1:2], EPS, 1.0, ALU.add, ALU.mult)\
                        .then_inc(sig["x_veps_ready"], 1)
                    pool.wait_ge(sig["x_veps_ready"], i + 1)
                    pool.tensor_tensor(w["rstd"][:], w["veps"][:], w["mhalf"][:], ALU.pow)\
                        .then_inc(sig["x_rstd_ready"], 1)

            @block.vector
            def _(dve):
                steps = Steps(dve, sig["vector_steps"])
                for i in range(PAIRS):
                    for t in range(PT):
                        last = dve.bn_stats(n1["stats"][:, t, :], X[:, PT * i + t, :])
                    steps.after(last)
                    for t in range(PT):
                        last = dve.bn_aggr(n1["mv"][:, t, :], n1["stats"][:, t, :])
                    last.then_inc(sig["x_var_ready"], 1)
                    dve.wait_ge(sig["x_rstd_ready"], i + 1)
                    for t in range(PT):
                        last = dve.tensor_scalar(Y[:, PT * i + t, :], X[:, PT * i + t, :], n1["mv"][:, t, 0:1],
                                                 n1["rstd"][:, t, :], ALU.subtract, ALU.mult)
                    steps.after(last)
                dve.wait_ge(sig["loads"], 160)
                dve.tensor_scalar(mrow[:], mrow8[:], NEG, None, ALU.mult)
                dve.tensor_scalar(mcrow[:], mcrow8[:], NEG, None, ALU.mult)
                dve.tensor_scalar(mcol[:], mcol8[:], NEG, None, ALU.mult)
                dve.tensor_scalar(mccol[:], mccol8[:], NEG, None, ALU.mult)
                gains = nb[:].rearrange("p (i two) -> p i two", two=2)[:, :, 0]
                steps.after(dve.tensor_scalar(gains, gains, 1.0, None, ALU.add))
                dve.wait_ge(sig["ada_ready"], 1)
                dve.tensor_tensor(ada[:].rearrange("p (i b) -> p i b", b=B),
                                  psum[:, 0, 0:L2_LAYERS * 6 * B].rearrange("p (i b) -> p i b", b=B),
                                  nb[:].unsqueeze(2).to_broadcast([P, L2_LAYERS * 6, B]), ALU.add)

        with nc.Fori(0, L2_LAYERS) as layer:
            with engines_pass(nc) as (block, sig):
                @block.sync
                def _(sp):
                    sp.dma_start(W[:], dram["L2_W"][ds(layer, 1)].rearrange("a p n -> (a p) n"))\
                        .then_inc(sig["weights"], 16)
                    sp.wait_ge(sig["weights"], 16)

                @block.scalar
                def _(act):
                    act.copy(f2bl[:], f2b[:, ds(layer, 1), :].rearrange("p a d -> p (a d)"))

            with nc.Fori(0, PAIRS) as pair:
                tag = {}

                def w(name, cols=P):
                    return W[:, L2_W[name]:L2_W[name] + cols]

                def gain(norm, b):
                    return ada[:, ds(layer * (6 * B) + norm * (2 * B) + pair * 2 + b, 1)]

                def shift(norm, b):
                    return ada[:, ds(layer * (6 * B) + norm * (2 * B) + B + pair * 2 + b, 1)]

                def y(t):
                    return Y[:, ds(pair * PT + t, 1), :].rearrange("p a d -> p (a d)")

                yall = Y[:, ds(pair * PT, PT), :]

                def rows(g):
                    return slice(32 * g, 32 * g + 32)

                def one(g):
                    return slice(32 * g, 32 * g + 1)

                own = Attention("self", 2 * (H // GROUP), 2, 1, L2_DH, 2, S, L2_DH ** -0.5)

                def own_max(u, h):
                    b, g = u // 4, u % 4
                    return [(slice(256 * t, 256 * t + 256),
                             [(qmb[rows(g), h, S * b + P * t:S * b + P * t + P], kb[rows(g), S * b:S * b + S]),
                              (ones[one(g)], pmask[one(g), S * b:S * b + S])]) for t in range(2)]

                def own_scores(u, c, h):
                    b, g = u // 4, u % 4
                    return [(0, [(kT[rows(g), S * b + P * c:S * b + P * c + P], qm[rows(g), h, S * b:S * b + S])])]

                def own_values(u, h, r, t, p):
                    b, g = u // 4, u % 4
                    return [(p[:, c, prob_cols(h, P * t)], v[:, 2 * b + c, GROUP * g + h, :])
                            for c in range(2)]

                own.max_products, own.score_products, own.value_products = own_max, own_scores, own_values
                own.max_column = lambda u, h, out, t: (u * GROUP + h) * 2 + t
                own.key_bias = lambda u, c: mcol[:, ds(pair * PT + 2 * (u // 4) + c, 1)]
                own.neg_ident = cst["neg_ident"][:]

                cross = Attention("cross", H // GROUP, 1, 2, L2_DH, 4, C, L2_DH ** -0.5)

                def cross_max(u, h):
                    return [(slice(C * t, C * t + C),
                             [(qmb[rows(u), h, P * t:P * t + P], kb[rows(u), C * (t // 2):C * (t // 2) + C]),
                              (ones[one(u)], pcmask[one(u), C * (t // 2):C * (t // 2) + C])]) for t in range(PT)]

                def cross_scores(u, c, h):
                    return [(C * b, [(kT[rows(u), C * b:C * b + C], qm[rows(u), h, S * b:S * b + S])])
                            for b in range(2)]

                def cross_values(u, h, r, t, p):
                    return [(p[C * r:C * r + C, 0, prob_cols(h, P * t)],
                             v[C * r:C * r + C, 0, GROUP * u + h, :])]

                cross.max_products, cross.score_products, cross.value_products = cross_max, cross_scores, cross_values
                cross.max_column = lambda u, h, out, t: (u * GROUP + h) * 4 + 2 * (out // C) + t
                cross.key_bias = lambda u, c: mccol[:, ds(pair, 1)]
                cross.neg_ident = cst["neg_ident"][:]

                def heads(x):
                    return x.rearrange("p (h e) -> p h e", e=L2_DH)

                with engines_pass(nc) as (block, sig):
                    @block.tensor
                    def _(pe):
                        def turn_norm(n):
                            pe.wait_ge(sig[n + "_normed"], 1)
                            turn_tensor(pe, cst["ident"], psum[:, 7, :], lambda t: xn[:, t, :])\
                                .then_inc(sig[n + "_turned"], 1)
                            pe.wait_ge(sig[n + "_modulated"], 2)

                        def project_out(n, weight):
                            pe.wait_ge(sig[n + "_values_taken"], own.units if n == "self" else 2 * cross.units)
                            turn_tensor(pe, cst["ident"], psum[:, 0, :], lambda t: o[:, t, :])\
                                .then_inc(sig[n + "_out_turned"], 1)
                            pe.wait_ge(sig[n + "_outT_ready"], 1)
                            for t in range(PT):
                                last = pe.matmul(psum[:, 1, P * t:P * t + P], oT[:, P * t:P * t + P], w(weight),
                                                 start=True, stop=True)
                            last.then_inc(sig[n + "_projected"], 1)

                        turn_norm("n1")
                        for i, name in enumerate(("q", "qs", "k", "ks")):
                            pe.matmul(psum[:, 2 + i, :], w(name), xnT[:], start=True, stop=True)\
                                .then_inc(sig["self_proj_ready"], 1)
                        for t in range(PT):
                            last = pe.matmul(psum[:, 6, P * t:P * t + P], xnT[:, P * t:P * t + P], w("v"),
                                             start=True, stop=True)
                        last.then_inc(sig["self_v_ready"], 1)
                        pe.wait_ge(sig["self_operands_ready"], 1)
                        pe.wait_ge(sig["self_v_taken"], 1)
                        pe.wait_ge(sig["ctx_ready"], 1)
                        attention_tensor(pe, sig, own, psum, m, probs)
                        project_out("self", "so")
                        turn_norm("n2")
                        for i, name in enumerate(("cq", "cqs")):
                            pe.matmul(psum[:, 2 + i, :], w(name), xnT[:], start=True, stop=True)\
                                .then_inc(sig["cross_proj_ready"], 1)
                        for i, name in enumerate(("ck", "cks")):
                            pe.matmul(psum[:, 4 + i, 0:2 * C], w(name), cctx[:], start=True, stop=True)\
                                .then_inc(sig["cross_proj_ready"], 1)
                        pe.matmul(psum[:, 6, 0:P], cctx[:], w("cv"), start=True, stop=True)\
                            .then_inc(sig["cross_v_ready"], 1)
                        pe.wait_ge(sig["cross_operands_ready"], 1)
                        pe.wait_ge(sig["cross_v_taken"], 1)
                        attention_tensor(pe, sig, cross, psum, m2, probs)
                        project_out("cross", "co")
                        turn_norm("n3")
                        for i in range(L2_FF):
                            pe.matmul(psum[:, 2 + i, :], w("f1", 512)[:, P * i:P * i + P], xnT[:],
                                      start=True, stop=True).then_inc(sig["hidden_ready"], 1)
                        pe.wait_ge(sig["gelu_ready"], L2_FF)
                        for t in range(PT):
                            for i in range(L2_FF):
                                last = pe.matmul(psum[:, 6, P * t:P * t + P], hT[:, i, P * t:P * t + P],
                                                 w("f2", 512)[:, P * i:P * i + P], start=i == 0, stop=i == L2_FF - 1)
                        last.then_inc(sig["ff_ready"], 1)

                    @block.gpsimd
                    def _(pool):
                        pool.tensor_copy(pmask[:], mrow[:, ds(pair * (2 * S), 2 * S)])
                        pool.tensor_copy(pcmask[:], mcrow[:, ds(pair * (2 * C), 2 * C)])
                        pool.tensor_copy(cctx[:], ctxT[:, ds(pair * (2 * C), 2 * C)]).then_inc(sig["ctx_ready"], 1)
                        norm_pool(pool, sig, "n1", n1)
                        norm_pool(pool, sig, "n2", n2)
                        norm_pool(pool, sig, "n3", n3)

                    @block.scalar
                    def _(act):
                        def modulate(n, i):
                            act.wait_ge(sig[n + "_turned"], 1)
                            for b in range(2):
                                act.activation(xnT[:, S * b:S * b + S], psum[:, 7, S * b:S * b + S], ACT.Identity,
                                               bias=shift(i, b), scale=gain(i, b))\
                                    .then_inc(sig[n + "_modulated"], 1)

                        def out_turned(n):
                            act.wait_ge(sig[n + "_out_turned"], 1)
                            act.copy(oT[:], psum[:, 0, :]).then_inc(sig[n + "_outT_ready"], 1)

                        modulate("n1", 0)
                        act.wait_ge(sig["self_v_ready"], 1)
                        act.copy(v[:, :, :, 0:L2_DH], psum[:, 6, :].rearrange("p (t h e) -> p t h e", t=PT, h=H))\
                            .then_inc(sig["self_v_taken"], 1)
                        attention_scalar(act, sig, own, psum, probs)
                        out_turned("self")
                        modulate("n2", 1)
                        act.wait_ge(sig["cross_v_ready"], 1)
                        act.copy(v[:, 0, :, 0:L2_DH], heads(psum[:, 6, 0:P])).then_inc(sig["cross_v_taken"], 1)
                        attention_scalar(act, sig, cross, psum, probs)
                        out_turned("cross")
                        modulate("n3", 2)
                        for i in range(L2_FF):
                            act.wait_ge(sig["hidden_ready"], i + 1)
                            act.activation(hT[:, i, :], psum[:, 2 + i, :], ACT.Gelu,
                                           bias=f1b[:, ds(layer * L2_FF + i, 1)]).then_inc(sig["gelu_ready"], 1)

                    @block.vector
                    def _(dve):
                        steps = Steps(dve, sig["vector_steps"])

                        def rotate(n, first, bank, out, cols):
                            dve.wait_ge(sig[n + "_proj_ready"], first + 2)
                            dve.tensor_tensor(t1[:, 0:cols], psum[:, bank, 0:cols], cst["cos"](cols), ALU.mult)
                            steps.after(dve.tensor_tensor(t2[:, 0:cols], psum[:, bank + 1, 0:cols],
                                                          cst["sin"](cols), ALU.mult))
                            steps.after(dve.tensor_tensor(out, t1[:, 0:cols], t2[:, 0:cols], ALU.add))

                        def operands(n, kcols):
                            rotate(n, 0, 2, qT[:], PTOK)
                            for j in range(GROUP):
                                dve.tensor_scalar(qmb[:, j, :], qT[:], cst["head"][:, j:j + 1], None, ALU.mult)
                                dve.tensor_scalar(qm[:, j, :], qT[:], cst["head"][:, j:j + 1], None, ALU.mult)
                            rotate(n, 2, 4, kT[:, 0:kcols], kcols)
                            dve.tensor_copy(kb[:, 0:kcols], kT[:, 0:kcols]).then_inc(sig[n + "_operands_ready"], 1)

                        def residual(n, bank):
                            dve.wait_ge(sig[n], 1)
                            steps.after(dve.tensor_tensor(yall, yall, psum[:, bank, :].rearrange("p (t d) -> p t d", t=PT),
                                                          ALU.add))

                        norm_vector(dve, sig, steps, "n1", y, n1, lambda t: xn[:, t, :])
                        operands("self", PTOK)
                        attention_vector(dve, sig, steps, own, psum, m, rsum,
                                         lambda u, r, t: heads(o[:, 2 * (u // 4) + t, 32 * (u % 4):32 * (u % 4) + 32]))
                        residual("self_projected", 1)
                        norm_vector(dve, sig, steps, "n2", y, n2, lambda t: xn[:, t, :])
                        operands("cross", 2 * C)
                        attention_vector(dve, sig, steps, cross, psum, m2, rsum,
                                         lambda u, r, t: heads(o[:, 2 * r + t, 32 * u:32 * u + 32]))
                        residual("cross_projected", 1)
                        norm_vector(dve, sig, steps, "n3", y, n3, lambda t: xn[:, t, :])
                        steps.after(dve.tensor_tensor(yall, yall, f2bl[:].unsqueeze(1).to_broadcast([P, PT, D]), ALU.add))
                        residual("ff_ready", 6)

        with engines_pass(nc) as (block, sig):
            @block.vector
            def _(dve):
                dve.tensor_tensor(X[:], X[:], Y[:], ALU.add)



F_DH = 8


def top2_block(nc, dram, X, psum, cst):
    with ExitStack() as ctx:
        def sb(name, shape, dt=F32):
            return ctx.enter_context(nc.sbuf_tensor("f2_" + name, shape, dt))

        wqkv, wo, wg = sb("wqkv", [P, 3, D]), sb("wo", [P, D]), sb("wg", [P, E])
        w1, w2 = sb("w1", [P, E, EF, P]), sb("w2", [P, E, EF, D])
        b1 = sb("b1", [P, E * EF])
        b2 = sb("b2", [1, E * D])
        onerow = sb("onerow", [1, P])
        aff = sb("aff", [P, 4, D])
        number = sb("number", [P, E])
        causal32, causalT32 = sb("causal32", [P, 2 * S]), sb("causalT32", [P, 2 * S])
        causal, causalT = sb("causal", [P, 2, S], BF16), sb("causalT", [P, 2, S], BF16)
        n0, n1, n2 = (norm_buffers(sb, n) for n in ("n0", "n1", "n2"))
        for n in (n0, n1, n2):
            n["mhalf"] = cst["mhalf"]
        Z, zn = sb("z", [P, PT, D]), sb("zn", [P, PT, D])
        zT = sb("zT", [P, PTOK])
        qT, kT = sb("qT", [P, PTOK]), sb("kT", [P, PTOK])
        qm, qmb = sb("qm", [P, GROUP, PTOK]), sb("qmb", [P, GROUP, PTOK], BF16)
        kb = sb("kb", [P, PTOK], BF16)
        v = sb("v", [P, PT, H, F_DH + 1])
        m = sb("m", [P, H * 4], BF16)
        probs = sb("probs", [P, 2, 2, GROUP * S])
        rsum = sb("rsum", [P, 2, GROUP])
        o, oT = sb("o", [P, PT, D]), sb("oT", [P, PTOK])
        hm, hT = sb("hm", [P, PT, D]), sb("hT", [P, PTOK])
        logits, lmax, lsum = sb("logits", [P, PT, E]), sb("lmax", [P, PT]), sb("lsum", [P, PT])
        top, topi, topf = sb("top", [P, PT, 8]), sb("topi", [P, PT, 8], U32), sb("topf", [P, PT, 8])
        pair_sum = sb("pair_sum", [P, PT])
        w_a, w_b = sb("w_a", [P, PT, E]), sb("w_b", [P, PT, E])
        hid = sb("hid", [P, 2, EF, PTOK])

        with engines_pass(nc) as (block, sig):
            @block.sync
            def _(sp):
                for dst, src in ((wqkv, "F2_wqkv"), (wo, "F2_wo"), (wg, "F2_wg"), (w1, "F2_w1"), (w2, "F2_w2"),
                                 (b1, "F2_b1"), (b2, "F2_b2"), (causal32, "c_causal"), (causalT32, "c_causalT")):
                    sp.dma_start(dst[:], dram[src]).then_inc(sig["loads"], 16)
                sp.dma_start(aff[:].rearrange("p l d -> p (l d)"),
                             dram["F2_affine"].to_broadcast([P, 4 * D])).then_inc(sig["loads"], 16)
                sp.dma_start(number[:], dram["c_number"].to_broadcast([P, E])).then_inc(sig["loads"], 16)

            @block.gpsimd
            def _(pool):
                pool.memset(v[:, :, :, F_DH:F_DH + 1], 1.0)
                pool.memset(onerow[:], 1.0)

            @block.vector
            def _(dve):
                dve.wait_ge(sig["loads"], 176)
                dve.tensor_copy(causal[:].rearrange("p t k -> p (t k)"), causal32[:])
                dve.tensor_copy(causalT[:].rearrange("p t k -> p (t k)"), causalT32[:])

        with nc.Fori(0, PAIRS) as pair:
            def x(t):
                return X[:, ds(pair * PT + t, 1), :].rearrange("p a d -> p (a d)")

            def rows(g):
                return slice(32 * g, 32 * g + 32)

            own = Attention("self", 2 * (H // GROUP), 2, 1, F_DH, 2, S, F_DH ** -0.5)

            def own_max(u, h):
                b, g = u // 4, u % 4
                return [(slice(256 * t, 256 * t + 256),
                         [(qmb[rows(g), h, S * b + P * t:S * b + P * t + P], kb[rows(g), S * b:S * b + S]),
                          (cst["ident_bf"][:], causal[:, t, :])]) for t in range(2)]

            def own_scores(u, c, h):
                b, g = u // 4, u % 4
                return [(0, [(kT[rows(g), S * b + P * c:S * b + P * c + P], qm[rows(g), h, S * b:S * b + S]),
                             (cst["ident_bf"][:], causalT[:, c, :])])]

            def own_values(u, h, r, t, p):
                b, g = u // 4, u % 4
                return [(p[:, c, prob_cols(h, P * t)], v[:, 2 * b + c, GROUP * g + h, :]) for c in range(2)]

            own.max_products, own.score_products, own.value_products = own_max, own_scores, own_values
            own.max_column = lambda u, h, out, t: (u * GROUP + h) * 2 + t
            own.key_bias = lambda u, c: 0.0
            own.neg_ident = cst["neg_ident"][:]

            def heads(z):
                return z.rearrange("p (h e) -> p h e", e=F_DH)

            with engines_pass(nc) as (block, sig):
                @block.tensor
                def _(pe):
                    def turn(ready, bank, src, turned, taken, count=1):
                        pe.wait_ge(sig[ready], count)
                        turn_tensor(pe, cst["ident"], psum[:, bank, :], src).then_inc(sig[turned], 1)
                        pe.wait_ge(sig[taken], 1)

                    turn("n0_normed", 7, lambda t: Z[:, t, :], "z_turned", "zT_ready")
                    for i in range(2):
                        pe.matmul(psum[:, 2 + i, :], wqkv[:, i, :], zT[:], start=True, stop=True)\
                            .then_inc(sig["proj_ready"], 1)
                    for t in range(PT):
                        last = pe.matmul(psum[:, 6, P * t:P * t + P], zT[:, P * t:P * t + P], wqkv[:, 2, :],
                                         start=True, stop=True)
                    last.then_inc(sig["v_ready"], 1)
                    pe.wait_ge(sig["operands_ready"], 1)
                    pe.wait_ge(sig["v_taken"], 1)
                    attention_tensor(pe, sig, own, psum, m, probs)
                    turn("self_values_taken", 0, lambda t: o[:, t, :], "o_turned", "oT_ready", own.units)
                    for t in range(PT):
                        last = pe.matmul(psum[:, 1, P * t:P * t + P], oT[:, P * t:P * t + P], wo[:], start=True, stop=True)
                    last.then_inc(sig["projected"], 1)
                    turn("h_ready", 7, lambda t: hm[:, t, :], "h_turned", "hT_ready")
                    for t in range(PT):
                        last = pe.matmul(psum[:, 6, E * t:E * t + E], hT[:, P * t:P * t + P], wg[:], start=True, stop=True)
                    last.then_inc(sig["logits_ready"], 1)
                    for e in range(E + 1):
                        if e < E:
                            for i in range(EF):
                                if e >= 1:
                                    pe.wait_ge(sig["gelu_ready"], EF * (e - 1) + i + 1)
                                pe.matmul(psum[:, i, :], w1[:, e, i, :], hT[:], start=True, stop=True)\
                                    .then_inc(sig["units_ready"], 1)
                        if e >= 1:
                            pe.wait_ge(sig["gelu_ready"], EF * e)
                            if e >= 3:
                                pe.wait_ge(sig["expert_added"], e - 2)
                            for t in range(PT):
                                out = psum[:, 4 + (e - 1) % 2, P * t:P * t + P]
                                for i in range(EF):
                                    pe.matmul(out, hid[:, (e - 1) % 2, i, P * t:P * t + P], w2[:, e - 1, i, :],
                                              start=i == 0, stop=False)
                                last = pe.matmul(out, onerow[:], b2[:, D * (e - 1):D * e], start=False, stop=True)
                            last.then_inc(sig["expert_ready"], 1)

                @block.gpsimd
                def _(pool):
                    norm_pool(pool, sig, "n0", n0)
                    norm_pool(pool, sig, "n1", n1)
                    norm_pool(pool, sig, "n2", n2)

                @block.scalar
                def _(act):
                    def take(turned, bank, dst, ready):
                        act.wait_ge(sig[turned], 1)
                        act.copy(dst[:], psum[:, bank, :]).then_inc(sig[ready], 1)

                    take("z_turned", 7, zT, "zT_ready")
                    act.wait_ge(sig["v_ready"], 1)
                    act.copy(v[:, :, :, 0:F_DH], psum[:, 6, :].rearrange("p (t h e) -> p t h e", t=PT, h=H))\
                        .then_inc(sig["v_taken"], 1)
                    attention_scalar(act, sig, own, psum, probs)
                    take("o_turned", 0, oT, "oT_ready")
                    take("h_turned", 7, hT, "hT_ready")
                    act.wait_ge(sig["shifted_logits_ready"], 1)
                    act.activation(w_a[:], logits[:], ACT.Exp).then_inc(sig["router_exp_ready"], 1)
                    for e in range(E):
                        if e >= 2:
                            act.wait_ge(sig["expert_ready"], e - 1)
                        for i in range(EF):
                            act.wait_ge(sig["units_ready"], EF * e + i + 1)
                            act.activation(hid[:, e % 2, i, :], psum[:, i, :], ACT.Gelu_apprx_tanh,
                                           bias=b1[:, EF * e + i:EF * e + i + 1]).then_inc(sig["gelu_ready"], 1)

                @block.vector
                def _(dve):
                    steps = Steps(dve, sig["vector_steps"])

                    def wide(col):
                        return col.unsqueeze(2).to_broadcast([P, PT, E])

                    def affine(dst, src, g, b):
                        steps.after(dve.tensor_tensor(dst, src, aff[:, g, :].unsqueeze(1).to_broadcast([P, PT, D]), ALU.mult))
                        return dve.tensor_tensor(dst, dst, aff[:, b, :].unsqueeze(1).to_broadcast([P, PT, D]), ALU.add)

                    def tiles(bank):
                        return psum[:, bank, :].rearrange("p (t d) -> p t d", t=PT)

                    norm_vector(dve, sig, steps, "n0", x, n0, lambda t: Z[:, t, :])
                    dve.wait_ge(sig["proj_ready"], 1)
                    steps.after(dve.tensor_copy(qT[:], psum[:, 2, :]))
                    for j in range(GROUP):
                        dve.tensor_scalar(qmb[:, j, :], qT[:], cst["head"][:, j:j + 1], None, ALU.mult)
                        dve.tensor_scalar(qm[:, j, :], qT[:], cst["head"][:, j:j + 1], None, ALU.mult)
                    dve.wait_ge(sig["proj_ready"], 2)
                    steps.after(dve.tensor_copy(kT[:], psum[:, 3, :]))
                    dve.tensor_copy(kb[:], kT[:]).then_inc(sig["operands_ready"], 1)
                    attention_vector(dve, sig, steps, own, psum, m, rsum,
                                     lambda u, r, t: heads(o[:, 2 * (u // 4) + t, 32 * (u % 4):32 * (u % 4) + 32]))
                    dve.wait_ge(sig["projected"], 1)
                    steps.after(dve.tensor_tensor(Z[:], Z[:], tiles(1), ALU.add))
                    norm_vector(dve, sig, steps, "n1", lambda t: Z[:, t, :], n1, lambda t: zn[:, t, :])
                    affine(hm[:], zn[:], 0, 1).then_inc(sig["h_ready"], 1)
                    dve.wait_ge(sig["logits_ready"], 1)
                    steps.after(dve.tensor_copy(logits[:], psum[:, 6, 0:PT * E].rearrange("p (t e) -> p t e", e=E)))
                    steps.after(dve.tensor_reduce(lmax[:], logits[:], AX.X, ALU.max))
                    dve.tensor_tensor(logits[:], logits[:], wide(lmax[:]), ALU.subtract)\
                        .then_inc(sig["shifted_logits_ready"], 1)
                    dve.wait_ge(sig["router_exp_ready"], 1)
                    steps.after(dve.tensor_reduce(lsum[:], w_a[:], AX.X, ALU.add))
                    steps.after(dve.reciprocal(lsum[:], lsum[:]))
                    steps.after(dve.tensor_tensor(w_b[:], w_a[:], wide(lsum[:]), ALU.mult))
                    for t in range(PT):
                        last = dve.max(top[:, t, :], w_b[:, t, :])
                    steps.after(last)
                    for t in range(PT):
                        last = dve.max_index(topi[:, t, :], top[:, t, :], w_b[:, t, :])
                    steps.after(last)
                    steps.after(dve.tensor_copy(topf[:], topi[:]))
                    steps.after(dve.tensor_tensor(pair_sum[:], top[:, :, 0], top[:, :, 1], ALU.add))
                    steps.after(dve.reciprocal(pair_sum[:], pair_sum[:]))
                    numbers = number[:].unsqueeze(1).to_broadcast([P, PT, E])
                    dve.tensor_tensor(w_a[:], wide(topf[:, :, 0]), numbers, ALU.is_equal)
                    steps.after(dve.tensor_tensor(logits[:], wide(topf[:, :, 1]), numbers, ALU.is_equal))
                    steps.after(dve.tensor_tensor(w_a[:], w_a[:], logits[:], ALU.add))
                    steps.after(dve.tensor_tensor(w_a[:], w_a[:], w_b[:], ALU.mult))
                    steps.after(dve.tensor_tensor(w_a[:], w_a[:], wide(pair_sum[:]), ALU.mult))
                    for e in range(E):
                        dve.wait_ge(sig["expert_ready"], e + 1)
                        for t in range(PT):
                            last = dve.scalar_tensor_tensor(hm[:, t, :], psum[:, 4 + e % 2, P * t:P * t + P],
                                                            w_a[:, t, e:e + 1], hm[:, t, :], ALU.mult, ALU.add)
                        last.then_inc(sig["expert_added"], 1)
                        dve.wait_ge(sig["expert_added"], e + 1)
                    norm_vector(dve, sig, steps, "n2", lambda t: hm[:, t, :], n2, lambda t: zn[:, t, :])
                    steps.after(affine(zn[:], zn[:], 2, 3))
                    xall = X[:, ds(pair * PT, PT), :]
                    dve.tensor_tensor(xall, xall, zn[:], ALU.add)



L3_DH = 64
L3_CH = H * L3_DH // P
L3_FF = 4


def glu_block(nc, dram, X, psum, cst):
    with ExitStack() as ctx:
        def sb(name, shape, dt=F32):
            return ctx.enter_context(nc.sbuf_tensor("l3_" + name, shape, dt))

        W = sb("w", [P, 6, H * L3_DH])
        wo = sb("wo", [P, 2, L3_CH, D])
        w1 = sb("w1", [P, 2 * L3_FF, P])
        w2 = sb("w2", [P, L3_FF, D])
        b1 = sb("b1", [P, 2 * L3_FF])
        rows_b = sb("rows_b", [P, 3, D])
        nw = sb("nw", [P, 6, D])
        nb = sb("nb", [P, 6])
        embT = sb("embT", [P, B])
        ada = sb("ada", [P, 6 * B])
        ctxT = sb("ctxT", [P, B * C])
        cctx = sb("cctx", [P, 2 * C])
        n0, n1, n2, n3 = (norm_buffers(sb, n) for n in ("n0", "n1", "n2", "n3"))
        for n in (n0, n1, n2, n3):
            n["mhalf"] = cst["mhalf"]
        Y = sb("y", [P, PT, D])
        xn = sb("xn", [P, PT, D])
        xnT = sb("xnT", [P, PTOK])
        qT, kT = sb("qT", [P, L3_CH, PTOK]), sb("kT", [P, L3_CH, PTOK])
        qb, kb = sb("qb", [P, L3_CH, PTOK], BF16), sb("kb", [P, L3_CH, PTOK], BF16)
        v = sb("v", [P, PT, H, L3_DH + 1])
        m = sb("m", [P, H * 4], BF16)
        m2 = sb("m2", [P, H * 4], BF16)
        probs = sb("probs", [P, 2, 2, GROUP * S])
        rsum = sb("rsum", [P, 2, GROUP])
        o = sb("o", [P, PT, H * L3_DH])
        hT = kT[:, 0:L3_FF, :]
        gT = qT[:, 0:L3_FF, :]

        with engines_pass(nc) as (block, sig):
            @block.sync
            def _(sp):
                for dst, src in ((W, "L3_W"), (wo, "L3_wo"), (w1, "L3_w1"), (w2, "L3_w2"), (b1, "L3_b1"),
                                 (nw, "L3_nw"), (nb, "L3_nb"), (embT, "embT"), (ctxT, "ctxT")):
                    sp.dma_start(dst[:], dram[src]).then_inc(sig["loads"], 16)
                sp.dma_start(rows_b[:].rearrange("p l d -> p (l d)"),
                             dram["L3_rows"].to_broadcast([P, 3 * D])).then_inc(sig["loads"], 16)

            @block.tensor
            def _(pe):
                pe.wait_ge(sig["loads"], 160)
                for i in range(6):
                    last = pe.matmul(psum[:, 0, i * B:(i + 1) * B], nw[:, i, :], embT[:], start=True, stop=True)
                last.then_inc(sig["ada_ready"], 1)

            @block.gpsimd
            def _(pool):
                pool.memset(v[:, :, :, L3_DH:L3_DH + 1], 1.0)

            @block.vector
            def _(dve):
                steps = Steps(dve, sig["vector_steps"])
                dve.wait_ge(sig["loads"], 160)
                gains = nb[:].rearrange("p (i two) -> p i two", two=2)[:, :, 0]
                steps.after(dve.tensor_scalar(gains, gains, 1.0, None, ALU.add))
                dve.wait_ge(sig["ada_ready"], 1)
                dve.tensor_tensor(ada[:].rearrange("p (i b) -> p i b", b=B),
                                  psum[:, 0, 0:6 * B].rearrange("p (i b) -> p i b", b=B),
                                  nb[:].unsqueeze(2).to_broadcast([P, 6, B]), ALU.add)

        with nc.Fori(0, PAIRS) as pair:
            def gain(norm, b):
                return ada[:, ds(norm * (2 * B) + pair * 2 + b, 1)]

            def shift(norm, b):
                return ada[:, ds(norm * (2 * B) + B + pair * 2 + b, 1)]

            def x(t):
                return X[:, ds(pair * PT + t, 1), :].rearrange("p a d -> p (a d)")

            def y(t):
                return Y[:, t, :]

            own = Attention("self", 2 * (H // GROUP), 2, 1, L3_DH, 2, S, L3_DH ** -0.5)
            cross = Attention("cross", H // GROUP, 1, 2, L3_DH, 4, C, L3_DH ** -0.5)

            def place(head):
                return slice(L3_DH * (head % 2), L3_DH * (head % 2) + L3_DH), head // 2

            def own_max(u, h):
                b, (r, ch) = u // 4, place(GROUP * (u % 4) + h)
                return [(slice(256 * t, 256 * t + 256),
                         [(qb[r, ch, S * b + P * t:S * b + P * t + P], kb[r, ch, S * b:S * b + S])]) for t in range(2)]

            def own_scores(u, c, h):
                b, (r, ch) = u // 4, place(GROUP * (u % 4) + h)
                return [(0, [(kT[r, ch, S * b + P * c:S * b + P * c + P], qT[r, ch, S * b:S * b + S])])]

            def own_values(u, h, r, t, p):
                return [(p[:, c, prob_cols(h, P * t)], v[:, 2 * (u // 4) + c, GROUP * (u % 4) + h, :])
                        for c in range(2)]

            own.max_products, own.score_products, own.value_products = own_max, own_scores, own_values
            own.max_column = lambda u, h, out, t: (u * GROUP + h) * 2 + t

            def cross_max(u, h):
                r, ch = place(GROUP * u + h)
                return [(slice(C * t, C * t + C),
                         [(qb[r, ch, P * t:P * t + P], kb[r, ch, C * (t // 2):C * (t // 2) + C])]) for t in range(PT)]

            def cross_scores(u, c, h):
                r, ch = place(GROUP * u + h)
                return [(C * b, [(kT[r, ch, C * b:C * b + C], qT[r, ch, S * b:S * b + S])]) for b in range(2)]

            def cross_values(u, h, r, t, p):
                return [(p[C * r:C * r + C, 0, prob_cols(h, P * t)],
                         v[C * r:C * r + C, 0, GROUP * u + h, :])]

            cross.max_products, cross.score_products, cross.value_products = cross_max, cross_scores, cross_values
            cross.max_column = lambda u, h, out, t: (u * GROUP + h) * 4 + 2 * (out // C) + t
            for a in (own, cross):
                a.key_bias = lambda u, c: 0.0
                a.neg_ident = cst["neg_ident"][:]

            def heads(z):
                return z.rearrange("p (h e) -> p h e", e=L3_DH)

            with engines_pass(nc) as (block, sig):
                @block.tensor
                def _(pe):
                    def turn_norm(n):
                        pe.wait_ge(sig[n + "_normed"], 1)
                        turn_tensor(pe, cst["ident"], psum[:, 7, :], lambda t: xn[:, t, :])\
                            .then_inc(sig[n + "_turned"], 1)
                        pe.wait_ge(sig[n + "_modulated"], 2)

                    def bank_free(n, use):
                        if use >= 8:
                            pe.wait_ge(sig[n + "_scalar_taken"], use - 7)
                            pe.wait_ge(sig[n + "_vector_taken"], use - 7)

                    def project(n, first, keys, tiles):
                        for i in range(2):
                            src = xnT[:] if i == 0 else keys
                            for ch in range(L3_CH):
                                use = i * L3_CH + ch
                                bank_free(n, use)
                                pe.matmul(psum[:, use % 8, 0:src.shape[1]], W[:, first + i, P * ch:P * ch + P], src,
                                          start=True, stop=True).then_inc(sig[n + "_proj_ready"], 1)
                        for t in range(tiles):
                            for half in range(2):
                                use = 2 * L3_CH + 2 * t + half
                                bank_free(n, use)
                                pe.matmul(psum[:, use % 8, :], keys[:, P * t:P * t + P],
                                          W[:, first + 2, 512 * half:512 * half + 512], start=True, stop=True)\
                                    .then_inc(sig[n + "_proj_ready"], 1)
                        pe.wait_ge(sig[n + "_scalar_taken"], 2 * L3_CH)
                        pe.wait_ge(sig[n + "_vector_taken"], 2 * L3_CH + 2 * tiles)

                    def project_out(n, i, rounds):
                        pe.wait_ge(sig[n + "_values_taken"], rounds)
                        for ch in range(L3_CH):
                            if ch >= 2:
                                pe.wait_ge(sig[n + "_outT_ready"], ch - 1)
                            turn_tensor(pe, cst["ident"], psum[:, ch % 2, :], lambda t: o[:, t, P * ch:P * ch + P])\
                                .then_inc(sig[n + "_out_turned"], 1)
                        pe.wait_ge(sig[n + "_outT_ready"], L3_CH)
                        for t in range(PT):
                            for ch in range(L3_CH):
                                last = pe.matmul(psum[:, 2, P * t:P * t + P], qT[:, ch, P * t:P * t + P], wo[:, i, ch, :],
                                                 start=ch == 0, stop=ch == L3_CH - 1)
                        last.then_inc(sig[n + "_projected"], 1)

                    turn_norm("n1")
                    project("self", 0, xnT[:], PT)
                    attention_tensor(pe, sig, own, psum, m, probs)
                    project_out("self", 0, own.units)
                    turn_norm("n2")
                    pe.wait_ge(sig["ctx_ready"], 1)
                    project("cross", 3, cctx[:], 1)
                    attention_tensor(pe, sig, cross, psum, m2, probs)
                    project_out("cross", 1, 2 * cross.units)
                    turn_norm("n3")
                    for i in range(L3_FF):
                        pe.matmul(psum[:, i, :], w1[:, L3_FF + i, :], xnT[:], start=True, stop=True)\
                            .then_inc(sig["gates_ready"], 1)
                        pe.matmul(psum[:, 4 + i, :], w1[:, i, :], xnT[:], start=True, stop=True)\
                            .then_inc(sig["units_ready"], 1)
                    pe.wait_ge(sig["gated_ready"], L3_FF)
                    for t in range(PT):
                        for i in range(L3_FF):
                            last = pe.matmul(psum[:, 0, P * t:P * t + P], hT[:, i, P * t:P * t + P], w2[:, i, :],
                                             start=i == 0, stop=i == L3_FF - 1)
                    last.then_inc(sig["ff_ready"], 1)

                @block.gpsimd
                def _(pool):
                    pool.tensor_copy(cctx[:], ctxT[:, ds(pair * (2 * C), 2 * C)]).then_inc(sig["ctx_ready"], 1)
                    norm_pool(pool, sig, "n0", n0)
                    norm_pool(pool, sig, "n1", n1)
                    norm_pool(pool, sig, "n2", n2)
                    norm_pool(pool, sig, "n3", n3)

                @block.scalar
                def _(act):
                    def modulate(n, i):
                        act.wait_ge(sig[n + "_turned"], 1)
                        for b in range(2):
                            act.activation(xnT[:, S * b:S * b + S], psum[:, 7, S * b:S * b + S], ACT.Identity,
                                           bias=shift(i, b), scale=gain(i, b)).then_inc(sig[n + "_modulated"], 1)

                    def take(n, kcols):
                        for use in range(2 * L3_CH):
                            act.wait_ge(sig[n + "_proj_ready"], use + 1)
                            dst, cols = (qT, PTOK) if use < L3_CH else (kT, kcols)
                            act.copy(dst[:, use % L3_CH, 0:cols], psum[:, use % 8, 0:cols])\
                                .then_inc(sig[n + "_scalar_taken"], 1)

                    def out_turned(n):
                        for ch in range(L3_CH):
                            act.wait_ge(sig[n + "_out_turned"], ch + 1)
                            act.copy(qT[:, ch, :], psum[:, ch % 2, :]).then_inc(sig[n + "_outT_ready"], 1)

                    modulate("n1", 0)
                    take("self", PTOK)
                    attention_scalar(act, sig, own, psum, probs)
                    out_turned("self")
                    modulate("n2", 1)
                    take("cross", 2 * C)
                    attention_scalar(act, sig, cross, psum, probs)
                    out_turned("cross")
                    modulate("n3", 2)
                    act.wait_ge(sig["cross_projected"], 1)
                    for i in range(L3_FF):
                        act.wait_ge(sig["gates_ready"], i + 1)
                        act.activation(gT[:, i, :], psum[:, i, :], ACT.Gelu, bias=b1[:, L3_FF + i:L3_FF + i + 1])\
                            .then_inc(sig["gelu_ready"], 1)

                @block.vector
                def _(dve):
                    steps = Steps(dve, sig["vector_steps"])

                    def take(n, kcols, tiles):
                        for use in range(2 * L3_CH):
                            dve.wait_ge(sig[n + "_scalar_taken"], use + 1)
                            dst, src, cols = (qb, qT, PTOK) if use < L3_CH else (kb, kT, kcols)
                            dve.tensor_copy(dst[:, use % L3_CH, 0:cols], src[:, use % L3_CH, 0:cols])\
                                .then_inc(sig[n + "_vector_taken"], 1)
                        for t in range(tiles):
                            for half in range(2):
                                use = 2 * L3_CH + 2 * t + half
                                dve.wait_ge(sig[n + "_proj_ready"], use + 1)
                                dve.tensor_copy(v[:, t, 8 * half:8 * half + 8, 0:L3_DH], heads(psum[:, use % 8, :]))\
                                    .then_inc(sig[n + "_vector_taken"], 1)

                    def residual(n, bank, i):
                        steps.after(dve.tensor_tensor(Y[:], Y[:], rows_b[:, i, :].unsqueeze(1).to_broadcast([P, PT, D]),
                                                      ALU.add))
                        dve.wait_ge(sig[n], 1)
                        steps.after(dve.tensor_tensor(Y[:], Y[:], psum[:, bank, :].rearrange("p (t d) -> p t d", t=PT),
                                                      ALU.add))

                    norm_vector(dve, sig, steps, "n0", x, n0, y)
                    norm_vector(dve, sig, steps, "n1", y, n1, lambda t: xn[:, t, :])
                    take("self", PTOK, PT)
                    attention_vector(dve, sig, steps, own, psum, m, rsum,
                                     lambda u, r, t: heads(o[:, 2 * (u // 4) + t, 256 * (u % 4):256 * (u % 4) + 256]))
                    residual("self_projected", 2, 0)
                    norm_vector(dve, sig, steps, "n2", y, n2, lambda t: xn[:, t, :])
                    take("cross", 2 * C, 1)
                    attention_vector(dve, sig, steps, cross, psum, m2, rsum,
                                     lambda u, r, t: heads(o[:, 2 * r + t, 256 * u:256 * u + 256]))
                    residual("cross_projected", 2, 1)
                    norm_vector(dve, sig, steps, "n3", y, n3, lambda t: xn[:, t, :])
                    for i in range(L3_FF):
                        dve.wait_ge(sig["units_ready"], i + 1)
                        dve.wait_ge(sig["gelu_ready"], i + 1)
                        dve.scalar_tensor_tensor(hT[:, i, :], psum[:, 4 + i, :], b1[:, i:i + 1], gT[:, i, :],
                                                 ALU.add, ALU.mult).then_inc(sig["gated_ready"], 1)
                    residual("ff_ready", 0, 2)
                    xall = X[:, ds(pair * PT, PT), :]
                    dve.tensor_tensor(xall, xall, Y[:], ALU.add)



POS, NEGQ = 7.0, 8.0
ROUND = 1.5 * 2.0 ** 23


def ternary_linear(nc, dram, X, psum, cst):
    with ExitStack() as ctx:
        def sb(name, shape, dt=F32):
            return ctx.enter_context(nc.sbuf_tensor("t3_" + name, shape, dt))

        hada, wt = sb("hada", [P, P]), sb("wt", [P, P])
        wabs, wscale, wrec = sb("wabs", [P, P]), sb("wscale", [P, 1]), sb("wrec", [P, 1])
        wn, wlow, wqT = sb("wn", [P, P]), sb("wlow", [P, P]), sb("wqT", [P, P])
        n0 = norm_buffers(sb, "n0")
        n0["mhalf"] = cst["mhalf"]
        z, zT, xh = sb("z", [P, PT, D]), sb("zT", [P, PTOK]), sb("xh", [P, PT, D])
        hi, lo, scale, rec = (sb(n, [P, PT]) for n in ("hi", "lo", "scale", "rec"))
        q, qT = sb("q", [P, PT, D]), sb("qT", [P, PTOK])

        with engines_pass(nc) as (block, sig):
            @block.sync
            def _(sp):
                sp.dma_start(hada[:], dram["c_hadamard"]).then_inc(sig["loads"], 16)
                sp.dma_start(wt[:], dram["T3_w"]).then_inc(sig["loads"], 16)

            @block.scalar
            def _(act):
                act.wait_ge(sig["loads"], 32)
                act.activation(wabs[:], wt[:], ACT.Abs, accum_out=wscale[:]).then_inc(sig["abs_sum_ready"], 1)
                act.wait_ge(sig["w_turned"], 1)
                act.copy(wqT[:], psum[:, 0, 0:P])

            @block.tensor
            def _(pe):
                pe.wait_ge(sig["ternary_ready"], 1)
                pe.transpose(psum[:, 0, 0:P], wn[:], cst["ident"][:]).then_inc(sig["w_turned"], 1)

            @block.vector
            def _(dve):
                steps = Steps(dve, sig["vector_steps"])
                dve.wait_ge(sig["abs_sum_ready"], 1)
                steps.after(dve.tensor_scalar(wscale[:], wscale[:], 1.0 / P, 1e-5, ALU.mult, ALU.max))
                steps.after(dve.reciprocal(wrec[:], wscale[:]))
                steps.after(dve.tensor_scalar(wn[:], wt[:], wrec[:], None, ALU.mult))
                steps.after(dve.tensor_scalar(wlow[:], wn[:], -0.5, None, ALU.is_lt))
                steps.after(dve.tensor_scalar(wn[:], wn[:], 0.5, None, ALU.is_gt))
                steps.after(dve.tensor_tensor(wn[:], wn[:], wlow[:], ALU.subtract))
                steps.after(dve.scalar_tensor_tensor(wn[:], wn[:], wscale[:], wt[:], ALU.mult, ALU.subtract))
                dve.tensor_tensor(wn[:], wn[:], wt[:], ALU.add).then_inc(sig["ternary_ready"], 1)

        with nc.Fori(0, PAIRS) as pair:
            def x(t):
                return X[:, ds(pair * PT + t, 1), :].rearrange("p a d -> p (a d)")

            with engines_pass(nc) as (block, sig):
                @block.tensor
                def _(pe):
                    pe.wait_ge(sig["n0_normed"], 1)
                    turn_tensor(pe, cst["ident"], psum[:, 0, :], lambda t: z[:, t, :]).then_inc(sig["z_turned"], 1)
                    pe.wait_ge(sig["zT_ready"], 1)
                    for t in range(PT):
                        last = pe.matmul(psum[:, 1, P * t:P * t + P], zT[:, P * t:P * t + P], hada[:], start=True, stop=True)
                    last.then_inc(sig["xh_ready"], 1)
                    pe.wait_ge(sig["q_ready"], 1)
                    turn_tensor(pe, cst["ident"], psum[:, 2, :], lambda t: q[:, t, :]).then_inc(sig["q_turned"], 1)
                    pe.wait_ge(sig["qT_ready"], 1)
                    for t in range(PT):
                        last = pe.matmul(psum[:, 3, P * t:P * t + P], qT[:, P * t:P * t + P], wqT[:], start=True, stop=True)
                    last.then_inc(sig["product_ready"], 1)

                @block.gpsimd
                def _(pool):
                    norm_pool(pool, sig, "n0", n0)

                @block.scalar
                def _(act):
                    act.wait_ge(sig["z_turned"], 1)
                    act.copy(zT[:], psum[:, 0, :]).then_inc(sig["zT_ready"], 1)
                    act.wait_ge(sig["xh_ready"], 1)
                    act.copy(xh[:].rearrange("p t d -> p (t d)"), psum[:, 1, :]).then_inc(sig["xh_taken"], 1)
                    act.wait_ge(sig["q_turned"], 1)
                    act.copy(qT[:], psum[:, 2, :]).then_inc(sig["qT_ready"], 1)

                @block.vector
                def _(dve):
                    steps = Steps(dve, sig["vector_steps"])
                    norm_vector(dve, sig, steps, "n0", x, n0, lambda t: z[:, t, :])
                    dve.wait_ge(sig["xh_taken"], 1)
                    dve.tensor_reduce(hi[:], xh[:], AX.X, ALU.max)
                    steps.after(dve.tensor_reduce(lo[:], xh[:], AX.X, ALU.min))
                    steps.after(dve.tensor_scalar(lo[:], lo[:], -1.0, 1e-5, ALU.mult, ALU.max))
                    steps.after(dve.tensor_tensor(hi[:], hi[:], lo[:], ALU.max))
                    steps.after(dve.tensor_scalar(scale[:], hi[:], 1.0 / POS, None, ALU.mult))
                    steps.after(dve.reciprocal(rec[:], scale[:]))
                    for t in range(PT):
                        last = dve.tensor_scalar(q[:, t, :], xh[:, t, :], rec[:, t:t + 1], ROUND, ALU.mult, ALU.add)
                    steps.after(last)
                    steps.after(dve.tensor_scalar(q[:], q[:], -ROUND, -NEGQ, ALU.add, ALU.max))
                    for t in range(PT):
                        last = dve.tensor_scalar(q[:, t, :], q[:, t, :], POS, scale[:, t:t + 1], ALU.min, ALU.mult)
                    steps.after(last)
                    steps.after(dve.tensor_tensor(q[:], q[:], xh[:], ALU.subtract))
                    dve.tensor_tensor(q[:], q[:], xh[:], ALU.add).then_inc(sig["q_ready"], 1)
                    dve.wait_ge(sig["product_ready"], 1)
                    xall = X[:, ds(pair * PT, PT), :]
                    dve.tensor_tensor(xall, xall, psum[:, 3, :].rearrange("p (t d) -> p t d", t=PT), ALU.add)



PHASES = [slot_attention, top_heads, attentive_gru, switch_experts, dit_layers, top2_block, glu_block, ternary_linear]


def program(nc, dram, phases=None):
    with ExitStack() as ctx:
        def sb(name, shape, dt=F32):
            return ctx.enter_context(nc.sbuf_tensor(name, shape, dt))

        X = sb("x_tokens", [P, TILES, D])
        psum = ctx.enter_context(nc.psum_tensor("psum", [P, 8, 512], F32))
        ident, neg_ident, ident_bf = sb("ident", [P, P]), sb("neg_ident", [P, P], BF16), sb("ident_bf", [P, P], BF16)
        cos, sin = sb("cos", [P, PTOK + 2 * C]), sb("sin", [P, PTOK + 2 * C])
        head, mhalf = sb("head", [P, GROUP]), sb("mhalf", [P, PT, 1])
        cst = {"ident": ident, "neg_ident": neg_ident, "ident_bf": ident_bf, "head": head, "mhalf": mhalf,
               "cos": lambda cols: cos[:, 0:PTOK] if cols == PTOK else cos[:, PTOK:PTOK + cols],
               "sin": lambda cols: sin[:, 0:PTOK] if cols == PTOK else sin[:, PTOK:PTOK + cols]}

        cst["tokens_sent"] = ctx.enter_context(nc.semaphore("tokens_sent"))
        cst["results_got"] = ctx.enter_context(nc.semaphore("results_got"))

        with engines_pass(nc) as (block, sig):
            @block.sync
            def _(sp):
                sp.dma_start(X[:], dram["x"].rearrange("(t p) d -> p t d", p=P)).then_inc(sig["loads"], 16)
                for dst, src in ((ident, "c_ident"), (cos, "c_cos"), (sin, "c_sin"), (head, "c_head")):
                    sp.dma_start(dst[:], dram[src]).then_inc(sig["loads"], 16)

            @block.gpsimd
            def _(pool):
                pool.memset(mhalf[:], -0.5)

            @block.vector
            def _(dve):
                dve.wait_ge(sig["loads"], 80)
                dve.tensor_scalar(neg_ident[:], ident[:], -1.0, None, ALU.mult)
                dve.tensor_copy(ident_bf[:], ident[:])

        for phase in (PHASES if phases is None else phases):
            phase(nc, dram, X, psum, cst)

        with engines_pass(nc) as (block, sig):
            @block.sync
            def _(sp):
                sp.dma_start(dram["out"].rearrange("(t p) d -> p t d", p=P), X[:]).then_inc(sig["stored"], 16)
                sp.wait_ge(sig["stored"], 16)



def laid_out(a):
    c = np.ascontiguousarray
    d = dict(shape_constants())
    d["x"] = a["x"].reshape(B * S, D)
    d["embT"] = c(a["cond_1024"].T)
    d["ctxT"] = c(a["ctx_1024"].reshape(B * C, D).T)
    m, mc = a["mask_BxS_bf0"], a["mask_BxS2_bf0"]
    d["mask_row"], d["cmask_row"] = c(m.reshape(1, -1)), c(mc.reshape(1, -1))
    d["mask_col"], d["cmask_col"] = c(m.reshape(TILES, P).T), c(mc.reshape(PAIRS, P).T)
    S0 = {k[9:]: v for k, v in a.items() if k.startswith("L0_xcond_")}
    d["S0_W"] = np.stack([S0[n] for n in ("wk", "wv", "wq", "wu", "w1", "w2")], 1)
    d["S0_col"] = np.stack([S0[n] for n in ("lnkv_g", "lnkv_b", "lnq_g", "lnq_b", "lnm_g", "lnm_b", "bk", "bq", "b1")], 1)
    d["S0_row"] = np.concatenate([S0[n].reshape(-1) for n in ("q_mu", "q_logsig", "bv", "bu", "b2", "lnp_g", "lnp_b")])[None]
    d["ctx_rows"] = a["ctx_1024"].reshape(PAIRS, P, D).transpose(1, 0, 2)
    d["cond_row"] = a["cond_1024"].reshape(1, B * D)
    H0 = {k[7:]: v for k, v in a.items() if k.startswith("L0_ffn_")}
    d["H0_wr"], d["H0_br"], d["H0_bo"] = H0["Wr"], H0["br"][None], H0["bo"][None]
    d["H0_wo"] = H0["Wo"].reshape(2, P, D).transpose(1, 0, 2)
    d["H0_W"] = np.stack([H0[n].reshape(D, HEADS, H_DH) for n in ("Wq", "Wk", "Wv")], 1)
    d["H0_bcol"] = np.stack([H0[n].reshape(HEADS, H_DH) for n in ("bq", "bk")], 2)
    d["H0_bv"] = H0["bv"].reshape(HEADS, H_DH)
    G1 = {k[9:]: v for k, v in a.items() if k.startswith("L1_xcond_")}
    d["G1_wa"] = G1["W_att"].reshape(2, D, D).transpose(1, 0, 2)
    d["G1_wi"] = G1["Wi"].reshape(2, D, 3, D).transpose(1, 0, 2, 3)
    d["G1_uh"], d["G1_bias"], d["G1_v"] = G1["Uh"].reshape(D, 3, D), G1["b"].reshape(3, D).T, G1["V_att"]
    d["G1_enc"] = a["ctx_1024"].transpose(1, 0, 2)
    d["S1_wr"] = a["L1_ffn_router_w"]
    d["S1_w1"] = a["L1_ffn_w1"].reshape(E, D, EF, P)
    d["S1_w2"] = a["L1_ffn_w2"].reshape(E, EF, P, D).transpose(0, 2, 1, 3)
    nw = np.stack([a[f"L2_xcond_n{i}_w"] for i in (1, 2, 3)], 1)
    d["L2_nw"] = nw.reshape(L2_LAYERS * 3 * 2, D, D).transpose(2, 0, 1)
    d["L2_nb"] = np.stack([a[f"L2_xcond_n{i}_b"] for i in (1, 2, 3)], 1).reshape(L2_LAYERS * 6, D).T
    d["L2_f1b"] = a["L2_xcond_f1_b"].reshape(L2_LAYERS * L2_FF, P).T
    d["L2_f2b"] = a["L2_xcond_f2_b"].reshape(1, L2_LAYERS * D)
    qkv = a["L2_xcond_qkv_w"]
    turned = lambda w: w.transpose(0, 2, 1)
    q, k, v = qkv[:, 0:D], qkv[:, D:2 * D], qkv[:, 2 * D:3 * D]
    cq, ck = a["L2_xcond_cq_w"], a["L2_xcond_ck_w"]
    f2 = turned(a["L2_xcond_f2_w"]).reshape(L2_LAYERS, L2_FF, P, D).transpose(0, 2, 1, 3).reshape(L2_LAYERS, P, L2_FF * D)
    d["L2_W"] = np.concatenate([turned(w) for w in (q, swap_halves(q), k, swap_halves(k), v, a["L2_xcond_so_w"],
                                                    cq, swap_halves(cq), ck, swap_halves(ck), a["L2_xcond_cv_w"],
                                                    a["L2_xcond_co_w"], a["L2_xcond_f1_w"])] + [f2], 2)
    F2 = {k[7:]: v for k, v in a.items() if k.startswith("L2_ffn_")}
    d["F2_wqkv"], d["F2_wo"], d["F2_wg"] = F2["w_qkv"].reshape(D, 3, D), F2["w_o"], F2["wg"]
    d["F2_w1"] = F2["w1"].transpose(1, 0, 2).reshape(D, E, EF, P)
    d["F2_w2"] = F2["w2"].reshape(E, EF, P, D).transpose(2, 0, 1, 3)
    d["F2_b1"] = F2["bb1"].reshape(E * EF, P).T
    d["F2_b2"] = F2["bb2"].reshape(1, E * D)
    d["F2_affine"] = np.concatenate([F2["g1"], F2["b1"], F2["g2"], F2["b2"]])[None]
    L3 = {k[9:]: v for k, v in a.items() if k.startswith("L3_xcond_")}
    d["L3_W"] = np.stack([L3[f"attn{i}_w{p}"] for i in (1, 2) for p in "qkv"], 1)
    d["L3_wo"] = np.stack([L3[f"attn{i}_wo"].reshape(L3_CH, P, D).transpose(1, 0, 2) for i in (1, 2)], 1)
    d["L3_w1"] = L3["ff_w1"].reshape(D, 2 * L3_FF, P)
    d["L3_b1"] = L3["ff_b1"].reshape(2 * L3_FF, P).T
    d["L3_w2"] = L3["ff_w2"].reshape(L3_FF, P, D).transpose(1, 0, 2)
    d["L3_rows"] = np.concatenate([L3["attn1_bo"], L3["attn2_bo"], L3["ff_b2"]])[None]
    d["L3_nw"] = np.stack([L3[f"norm{i}_w"].reshape(D, 2, D) for i in (1, 2, 3)], 1).reshape(D, 6, D)
    d["L3_nb"] = np.stack([L3[f"norm{i}_b"] for i in (1, 2, 3)]).reshape(6, D).T
    d["T3_w"] = a["L3_ffn_weight"]
    return {k: c(v) for k, v in d.items()}


def kernel(**inputs):
    import concourse.bacc as bacc
    from concourse.bass_utils import run_bass_kernel_spmd

    nc = bacc.Bacc("TRN2", target_bir_lowering=False, num_devices=1)
    arrays = laid_out({k: np.asarray(v) for k, v in inputs.items()})
    dram = {k: nc.dram_tensor("in_" + k, v.shape, mybir.dt.from_np(v.dtype), kind="ExternalInput").ap()
            for k, v in arrays.items()}
    dram["out"] = nc.dram_tensor("out_x", (B * S, D), F32, kind="ExternalOutput").ap()
    program(nc, dram)
    r = run_bass_kernel_spmd(nc, [{"in_" + k: v for k, v in arrays.items()}], core_ids=[0])
    return r.results[0]["out_x"].reshape(B, S, D)
```

```python
from contextlib import ExitStack, contextmanager

import numpy as np

import concourse.bass as bass
from concourse import mybir

ALU = mybir.AluOpType
ACT = mybir.ActivationFunctionType
AX = mybir.AxisListType
F32 = mybir.dt.float32
BF16 = mybir.dt.bfloat16
U8 = mybir.dt.uint8
U32 = mybir.dt.uint32
ds = bass.ds

P = 128
D = 128
B, S = 8, 256
C = 64
TILES = B * S // P
PAIRS = B // 2
PT = 4
PTOK = PT * P
H = 16
GROUP = 4
E, EF = 8, 4
EPS = 1e-5
HALVES = (slice(0, 64), slice(64, P))
NEG = -1e30


class Signals:

    def __init__(self, nc, ctx):
        self.nc, self.ctx, self.found = nc, ctx, {}

    def __getitem__(self, name):
        if name not in self.found:
            self.found[name] = self.ctx.enter_context(self.nc.semaphore(name))
        return self.found[name]


@contextmanager
def engines_pass(nc):
    with ExitStack() as ctx:
        sig = Signals(nc, ctx)
        with nc.Block() as block:
            yield block, sig
        numbers = sorted(s.num for s in sig.found.values())
        runs = [n for n in numbers if n - 1 not in numbers]
        for first in runs:
            end = next(n for n in range(first, 257) if n not in numbers)
            nc.sync.sem_clear(range(first, end))
        if runs:
            nc.all_engine_barrier()


class Steps:

    def __init__(self, engine, sem):
        self.engine, self.sem, self.n = engine, sem, 0

    def after(self, instruction):
        self.n += 1
        instruction.then_inc(self.sem, 1)
        self.engine.wait_ge(self.sem, self.n)



def norm_vector(dve, sig, steps, tag, src, w, out, tiles=PT, rows=P):
    for t in range(tiles):
        last = dve.bn_stats(w["stats"][0:rows, t, :], src(t))
    steps.after(last)
    for t in range(tiles):
        last = dve.bn_aggr(w["mv"][0:rows, t, :], w["stats"][0:rows, t, :])
    last.then_inc(sig[tag + "_var_ready"], 1)
    dve.wait_ge(sig[tag + "_rstd_ready"], 1)
    for t in range(tiles):
        last = dve.tensor_scalar(out(t), src(t), w["mv"][0:rows, t, 0:1], w["rstd"][0:rows, t, :],
                                 ALU.subtract, ALU.mult)
    last.then_inc(sig[tag + "_normed"], 1)
    dve.wait_ge(sig[tag + "_normed"], 1)


def norm_pool(pool, sig, tag, w, tiles=PT, rows=P):
    pool.wait_ge(sig[tag + "_var_ready"], 1)
    pool.tensor_scalar(w["veps"][0:rows, 0:tiles, :], w["mv"][0:rows, 0:tiles, 1:2], EPS, 1.0,
                       ALU.add, ALU.mult).then_inc(sig[tag + "_veps_ready"], 1)
    pool.wait_ge(sig[tag + "_veps_ready"], 1)
    pool.tensor_tensor(w["rstd"][0:rows, 0:tiles, :], w["veps"][0:rows, 0:tiles, :],
                       w["mhalf"][0:rows, 0:tiles, :], ALU.pow).then_inc(sig[tag + "_rstd_ready"], 1)


def turn_tensor(pe, ident, bank, src, tiles=PT, rows=P, width=P):
    for t in range(tiles):
        last = pe.transpose(bank[0:width, t * rows:(t + 1) * rows], src(t), ident[0:rows, 0:rows])
    return last


def norm_buffers(sb, name):
    return {
        "stats": sb(name + "_stats", [P, PT, 6]), "mv": sb(name + "_mv", [P, PT, 2]),
        "veps": sb(name + "_veps", [P, PT, 1]), "rstd": sb(name + "_rstd", [P, PT, 1]),
    }



def prob_cols(h, first, n=P):
    at = 256 * (2 * (h % 2) + h // 2) + first
    return slice(at, at + n)


class Attention:

    def __init__(self, tag, units, chunks, rounds, dh, groups, width, scale):
        self.tag, self.units, self.chunks, self.rounds = tag, units, chunks, rounds
        self.dh, self.groups, self.width, self.scale = dh, groups, width, scale
        self.late_values = False
        self.copies = 0
        self.narrow = self.masked = dh <= 16


def attention_tensor(pe, sig, a, psum, m, probs, heads_out=None):
    tag = a.tag

    def max_scores(u, h):
        if h == 0 and u < a.copies:
            pe.wait_ge(sig[tag + "_bf_queries_ready"], u + 1)
        n = u * GROUP + h
        if n >= 2:
            pe.wait_ge(sig[tag + "_row_max_ready"], n - 1)
        for out, products in a.max_products(u, h):
            for i, (lhsT, rhs) in enumerate(products):
                last = pe.matmul(psum[:, n % 2, out], lhsT, rhs, start=i == 0, stop=i == len(products) - 1)
        last.then_inc(sig[tag + "_max_scores_ready"], 1)

    def key_scores(u):
        pe.wait_ge(sig[tag + "_row_max_ready"], GROUP * (u + 1))
        for c in range(a.chunks):
            n = u * a.chunks + c
            if n >= 2:
                pe.wait_ge(sig[tag + "_probs_ready"], n - 1)
            for h in range(GROUP):
                bank, col = 2 + 2 * (n % 2) + h % 2, 256 * (h // 2)
                parts = [(out, slice(out, out + P // len(a.score_products(u, c, h))), products)
                         for out, products in a.score_products(u, c, h)]
                for i in range(len(parts[0][2])):
                    for _, rows, products in parts:
                        pe.matmul(psum[rows, bank, col:col + 256], *products[i], start=i == 0, stop=False)
                for t in range(2):
                    for out, rows, _ in parts:
                        mcol = a.max_column(u, h, out, t)
                        last = pe.matmul(psum[rows, bank, col + P * t:col + P * (t + 1)],
                                         m[:, mcol:mcol + 1].to_broadcast([P, rows.stop - rows.start]),
                                         a.neg_ident, start=False, stop=t == 1)
                if h == GROUP - 1:
                    last.then_inc(sig[tag + "_scores_ready"], 1)
                done = c * GROUP + h + 1
                if u + 1 < a.units and done % a.chunks == 0:
                    max_scores(u + 1, done // a.chunks - 1)

    def values(u):
        if u == 0 and a.late_values:
            pe.wait_ge(sig[tag + "_v_taken"], 1)
        pe.wait_ge(sig[tag + "_probs_ready"], a.chunks * (u + 1))
        for r in range(a.rounds):
            n = u * a.rounds + r
            if n >= 2:
                pe.wait_ge(sig[tag + "_values_taken"], n - 1)
            products = a.value_products(u, r, probs[:, u % 2])
            for what in range(1 if a.narrow else 2):
                for i, chunk in enumerate(products):
                    for rows, lhsT, rhs in chunk:
                        last = pe.matmul(psum[rows, 6 + n % 2, S * what:S * what + S], lhsT[what], rhs,
                                         start=i == 0, stop=i == len(products) - 1)
            last.then_inc(sig[tag + "_values_ready"], 1)

    def turn_values(u):
        for n in range(u * a.rounds, (u + 1) * a.rounds):
            pe.wait_ge(sig[tag + "_values_copied"], n + 1)
            turn_tensor(pe, a.ident, psum[:, 6 + n % 2, S:2 * S],
                        lambda t: heads_out[:, n % 2, P * t:P * t + P], tiles=2)\
                .then_inc(sig[tag + "_values_turned"], 1)

    for h in range(GROUP):
        max_scores(0, h)
    for u in range(a.units + 2):
        if a.masked and u < 2:
            pe.wait_ge(sig[tag + "_queries_ready"], u + 1)
        if u < a.units:
            key_scores(u)
        if a.narrow and u >= 2:
            turn_values(u - 2)
        if 1 <= u <= a.units:
            values(u - 1)


def attention_scalar(act, sig, a, psum, probs, heads_out=None):
    tag = a.tag

    def exponentials(u):
        if u >= 2:
            act.wait_ge(sig[tag + "_values_ready"], a.rounds * (u - 1))
        for c in range(a.chunks):
            n = u * a.chunks + c
            act.wait_ge(sig[tag + "_scores_ready"], n + 1)
            bank = 2 + 2 * (n % 2)
            act.activation(probs[:, u % 2, c, :], psum[:, bank:bank + 2, :].rearrange("p a n -> p (a n)"),
                           ACT.Exp, bias=a.key_bias(u, c), scale=a.scale).then_inc(sig[tag + "_probs_ready"], 1)

    def copy_values(u):
        for n in range(u * a.rounds, (u + 1) * a.rounds):
            act.wait_ge(sig[tag + "_values_ready"], n + 1)
            if n >= 2:
                act.wait_ge(sig[tag + "_values_turned"], n - 1)
            act.copy(heads_out[:, n % 2, :], psum[:, 6 + n % 2, 0:S]).then_inc(sig[tag + "_values_copied"], 1)

    for u in range(a.units + 2):
        if a.narrow and u >= 2:
            copy_values(u - 2)
        if u < a.units:
            exponentials(u)


def attention_vector(dve, sig, a, psum, m, rsum, out, then=None):
    tag = a.tag

    def row_max(u):
        for h in range(GROUP):
            n = u * GROUP + h
            dve.wait_ge(sig[tag + "_max_scores_ready"], n + 1)
            scores = psum[:, n % 2, 0:a.groups * a.width].rearrange("p (g k) -> p g k", g=a.groups)
            dve.tensor_reduce(m[:, n * a.groups:(n + 1) * a.groups], scores, AX.X, ALU.max)\
               .then_inc(sig[tag + "_row_max_ready"], 1)

    def normalise(u):
        for r in range(a.rounds):
            n = u * a.rounds + r
            dve.wait_ge(sig[tag + ("_values_turned" if a.narrow else "_values_ready")], n + 1)
            if n >= 2:
                dve.wait_ge(sig[tag + "_values_taken"], n - 1)
            if a.narrow:
                turned = psum[:, 6 + n % 2, S:2 * S].rearrange("p (t h e) -> p t h e", t=2, h=GROUP)
                inverse, sums, values = rsum[:, n % 2, :, :], turned[:, :, :, a.dh], turned[:, :, :, 0:a.dh]
                factor = inverse.unsqueeze(3).to_broadcast([P, 2, GROUP, a.dh])
            else:
                inverse, sums, values = rsum[:, n % 2, :], psum[:, 6 + n % 2, S:2 * S], psum[:, 6 + n % 2, 0:S]
                factor = inverse
            dve.reciprocal(inverse, sums).then_inc(sig[tag + "_sums_inverted"], 1)
            dve.wait_ge(sig[tag + "_sums_inverted"], n + 1)
            dve.tensor_tensor(out(u, r), values, factor, ALU.mult).then_inc(sig[tag + "_values_taken"], 1)

    row_max(0)
    if then:
        then(0)
    late = 2 if a.narrow else 1
    for u in range(a.units + late):
        if u + 1 < a.units:
            row_max(u + 1)
            if then:
                then(u + 1)
        if u >= late:
            normalise(u - late)



def rope_tables():
    half = L2_DH // 2
    inv = (np.float32(1.0) / np.float32(10000.0) ** (np.arange(half, dtype=np.float32) / np.float32(half)))
    ang = np.arange(S, dtype=np.float32)[:, None] * inv.astype(np.float32)
    cos, sin = np.cos(ang).T, np.sin(ang).T
    cos8, sin8 = np.concatenate([cos, cos]), np.concatenate([-sin, sin])
    return np.tile(cos8, (H, 1)).astype(np.float32), np.tile(sin8, (H, 1)).astype(np.float32)


def hadamard(size):
    h = np.array([[1.0]], dtype=np.float64)
    while h.shape[0] < size:
        h = np.block([[h, h], [h, -h]])
    return (h / np.sqrt(size)).astype(np.float32)


def shape_constants():
    cos, sin = rope_tables()
    q = np.arange(P)
    causal = np.zeros((P, 2, S), np.float32)
    causalT = np.zeros((P, 2, S), np.float32)
    for t in range(2):
        causal[:, t, :] = np.where(np.arange(S)[None, :] > (q + P * t)[:, None], NEG, 0.0)
        causalT[:, t, :] = np.where((q + P * t)[:, None] > np.arange(S)[None, :], NEG, 0.0)
    pick = np.zeros((P, 2, B), np.float32)
    for b in range(B):
        pick[32 * (b // 2) + b % 2, b % 2, b] = 1.0
    head = np.stack([((q // L2_DH) % (2 * GROUP) == j).astype(np.float32) for j in range(2 * GROUP)], 1)
    keys = lambda table: np.concatenate([np.tile(table, (1, 2)), np.tile(table[:, :C], (1, 2))], 1)
    cos, sin = keys(cos), keys(sin)
    return {"c_pick": pick, "c_ident": np.eye(P, dtype=np.float32), "c_cos": cos, "c_sin": sin, "c_head": head,
            "c_causal": causal.reshape(P, 2 * S), "c_causalT": causalT.reshape(P, 2 * S),
            "c_hadamard": hadamard(P), "c_before": np.triu(np.ones((P, P), np.float32), 1),
            "c_number": np.arange(H, dtype=np.float32)[None, :8]}


def swap_halves(w):
    s = w.shape
    return w.reshape(*s[:-2], H, 2, L2_DH // 2, s[-1])[..., ::-1, :, :].reshape(s)



SLOT_T = 3
SLOT_EPS = 1e-8


def slot_attention(nc, dram, X, psum, cst):
    with ExitStack() as ctx:
        def sb(name, shape, dt=F32):
            return ctx.enter_context(nc.sbuf_tensor("s0_" + name, shape, dt))

        W = sb("w", [P, 6, D])
        wk, wv, wq, wu, w1, w2 = (W[:, i, :] for i in range(6))
        col = sb("col", [P, 9])
        row = sb("row", [P, 7, D])
        cond = sb("cond", [P, B, D])
        context = sb("context", [P, PAIRS, D])
        ones = sb("ones", [P, 1])
        nx, nkv, nq, nm, np_ = (norm_buffers(sb, n) for n in ("nx", "nkv", "nq", "nm", "np"))
        for n in (nx, nkv, nq, nm, np_):
            n["mhalf"] = cst["mhalf"]
        xin, xinT = sb("xin", [P, D]), sb("xinT", [P, P])
        kT, v = sb("kT", [P, P]), sb("v", [P, D])
        slots, sn, snT = sb("slots", [P, PT, D]), sb("sn", [P, PT, D]), sb("snT", [P, PTOK])
        qT, ex, attn = sb("qT", [P, PTOK]), sb("ex", [P, S]), sb("attn", [P, S])
        smax, ssum = sb("smax", [P, 1]), sb("ssum", [P, 1])
        updT, rcount = sb("updT", [P, PTOK]), sb("rcount", [P, PT])
        mid, mn, mnT, hT = sb("mid", [P, PT, D]), sb("mn", [P, PT, D]), sb("mnT", [P, PTOK]), sb("hT", [P, PTOK])

        with engines_pass(nc) as (block, sig):
            @block.sync
            def _(sp):
                for dst, src in ((W, "S0_W"), (col, "S0_col"), (context, "ctx_rows")):
                    sp.dma_start(dst[:], dram[src]).then_inc(sig["loads"], 16)
                sp.dma_start(row[:].rearrange("p l d -> p (l d)"), dram["S0_row"].to_broadcast([P, 7 * D]))\
                    .then_inc(sig["loads"], 16)
                sp.dma_start(cond[:].rearrange("p l d -> p (l d)"), dram["cond_row"].to_broadcast([P, B * D]))\
                    .then_inc(sig["loads"], 16)
                sp.wait_ge(sig["loads"], 80)

            @block.gpsimd
            def _(pool):
                pool.memset(ones[:], 1.0)

            @block.scalar
            def _(act):
                act.wait_ge(sig["loads"], 80)
                act.activation(row[:, 1, :], row[:, 1, :], ACT.Exp)

        with nc.Fori(0, PAIRS) as pair:
            def x(t):
                return X[:, ds(pair * PT + t, 1), :].rearrange("p a d -> p (a d)")

            xall = X[:, ds(pair * PT, PT), :]

            def tiles(bank):
                return psum[:, bank, :].rearrange("p (t d) -> p t d", t=PT)

            def everywhere(i):
                return row[:, i, :].unsqueeze(1).to_broadcast([P, PT, D])

            with engines_pass(nc) as (block, sig):
                @block.tensor
                def _(pe):
                    pe.wait_ge(sig["nkv_normed"], 1)
                    pe.transpose(psum[:, 0, 0:P], xin[:], cst["ident"][:]).then_inc(sig["xin_turned"], 1)
                    pe.wait_ge(sig["xinT_ready"], 1)
                    pe.matmul(psum[:, 1, 0:P], wk, xinT[:], start=True, stop=True).then_inc(sig["k_ready"], 1)
                    pe.matmul(psum[:, 2, 0:P], xinT[:], wv, start=True, stop=True).then_inc(sig["v_ready"], 1)

                @block.gpsimd
                def _(pool):
                    norm_pool(pool, sig, "nkv", nkv, tiles=1)
                    norm_pool(pool, sig, "nx", nx)

                @block.vector
                def _(dve):
                    steps = Steps(dve, sig["vector_steps"])
                    norm_vector(dve, sig, steps, "nkv", lambda t: context[:, ds(pair, 1), :].rearrange("p a d -> p (a d)"),
                                nkv, lambda t: xin[:], tiles=1)
                    dve.wait_ge(sig["xin_turned"], 1)
                    dve.tensor_scalar(xinT[:], psum[:, 0, 0:P], col[:, 0:1], col[:, 1:2], ALU.mult, ALU.add)\
                        .then_inc(sig["xinT_ready"], 1)
                    norm_vector(dve, sig, steps, "nx", x, nx, lambda t: sn[:, t, :])
                    steps.after(dve.tensor_tensor(sn[:], sn[:], everywhere(1), ALU.mult))
                    dve.tensor_tensor(slots[:], sn[:], everywhere(0), ALU.add)
                    dve.wait_ge(sig["k_ready"], 1)
                    dve.tensor_scalar(kT[:], psum[:, 1, 0:P], col[:, 6:7], None, ALU.add)
                    dve.wait_ge(sig["v_ready"], 1)
                    dve.tensor_tensor(v[:], psum[:, 2, 0:P], row[:, 2, :], ALU.add)

            with nc.Fori(0, SLOT_T) as _step:
                with engines_pass(nc) as (block, sig):
                    @block.tensor
                    def _(pe):
                        pe.wait_ge(sig["nq_normed"], 1)
                        turn_tensor(pe, cst["ident"], psum[:, 0, :], lambda t: sn[:, t, :]).then_inc(sig["slots_turned"], 1)
                        pe.wait_ge(sig["snT_ready"], 1)
                        pe.matmul(psum[:, 1, :], wq, snT[:], start=True, stop=True).then_inc(sig["q_ready"], 1)
                        pe.wait_ge(sig["qT_ready"], 1)
                        for b in range(2):
                            last = pe.matmul(psum[C * b:C * b + C, 2, 0:S], kT[:, C * b:C * b + C], qT[:, S * b:S * b + S],
                                             start=True, stop=True)
                        last.then_inc(sig["logits_ready"], 1)
                        pe.wait_ge(sig["attn_ready"], 1)
                        for b in range(2):
                            r = slice(C * b, C * b + C)
                            last = pe.matmul(psum[:, 3 + b, 0:S], v[r, :], attn[r, :], start=True, stop=True)
                        last.then_inc(sig["upd_ready"], 1)
                        for b in range(2):
                            r = slice(C * b, C * b + C)
                            for t in range(2):
                                last = pe.matmul(psum[:, 5 + b, t:t + 1], attn[r, P * t:P * t + P], ones[r, :],
                                                 start=True, stop=True)
                        last.then_inc(sig["count_ready"], 1)
                        pe.wait_ge(sig["updT_ready"], 1)
                        for t in range(PT):
                            last = pe.matmul(psum[:, 7, P * t:P * t + P], updT[:, P * t:P * t + P], wu, start=True, stop=True)
                        last.then_inc(sig["wu_ready"], 1)
                        pe.wait_ge(sig["nm_normed"], 1)
                        turn_tensor(pe, cst["ident"], psum[:, 0, :], lambda t: mn[:, t, :]).then_inc(sig["mid_turned"], 1)
                        pe.wait_ge(sig["mnT_ready"], 1)
                        pe.matmul(psum[:, 1, :], w1, mnT[:], start=True, stop=True).then_inc(sig["units_ready"], 1)
                        pe.wait_ge(sig["gelu_ready"], 1)
                        for t in range(PT):
                            last = pe.matmul(psum[:, 2, P * t:P * t + P], hT[:, P * t:P * t + P], w2, start=True, stop=True)
                        last.then_inc(sig["mlp_ready"], 1)

                    @block.gpsimd
                    def _(pool):
                        norm_pool(pool, sig, "nq", nq)
                        norm_pool(pool, sig, "nm", nm)
                        norm_pool(pool, sig, "np", np_)

                    @block.scalar
                    def _(act):
                        act.wait_ge(sig["slots_turned"], 1)
                        act.activation(snT[:], psum[:, 0, :], ACT.Identity, bias=col[:, 3:4], scale=col[:, 2:3])\
                            .then_inc(sig["snT_ready"], 1)
                        act.wait_ge(sig["q_ready"], 1)
                        act.activation(qT[:], psum[:, 1, :], ACT.Identity, bias=col[:, 7:8]).then_inc(sig["qT_ready"], 1)
                        act.wait_ge(sig["max_ready"], 1)
                        act.activation(ex[:], psum[:, 2, 0:S], ACT.Exp, bias=smax[:], scale=float(D) ** 0.5,
                                       accum_out=ssum[:]).then_inc(sig["exp_ready"], 1)
                        act.wait_ge(sig["upd_ready"], 1)
                        act.copy(updT[:].rearrange("p (b s) -> p b s", b=2), psum[:, 3:5, 0:S]).then_inc(sig["updT_ready"], 1)
                        act.wait_ge(sig["mid_turned"], 1)
                        act.activation(mnT[:], psum[:, 0, :], ACT.Identity, bias=col[:, 5:6], scale=col[:, 4:5])\
                            .then_inc(sig["mnT_ready"], 1)
                        act.wait_ge(sig["units_ready"], 1)
                        act.activation(hT[:], psum[:, 1, :], ACT.Gelu, bias=col[:, 8:9]).then_inc(sig["gelu_ready"], 1)

                    @block.vector
                    def _(dve):
                        steps = Steps(dve, sig["vector_steps"])
                        norm_vector(dve, sig, steps, "nq", lambda t: slots[:, t, :], nq, lambda t: sn[:, t, :])
                        dve.tensor_tensor(mid[:], slots[:], everywhere(3), ALU.add)
                        dve.wait_ge(sig["logits_ready"], 1)
                        steps.after(dve.tensor_reduce(smax[:], psum[:, 2, 0:S], AX.X, ALU.max))
                        dve.tensor_scalar(smax[:], smax[:], -float(D) ** 0.5, None, ALU.mult).then_inc(sig["max_ready"], 1)
                        dve.wait_ge(sig["exp_ready"], 1)
                        steps.after(dve.reciprocal(ssum[:], ssum[:]))
                        dve.tensor_scalar(attn[:], ex[:], ssum[:], SLOT_EPS, ALU.mult, ALU.add)\
                            .then_inc(sig["attn_ready"], 1)
                        dve.wait_ge(sig["count_ready"], 1)
                        steps.after(dve.reciprocal(rcount[:].rearrange("p (b t) -> p b t", b=2), psum[:, 5:7, 0:2]))
                        dve.wait_ge(sig["wu_ready"], 1)
                        for t in range(PT):
                            last = dve.scalar_tensor_tensor(mid[:, t, :], psum[:, 7, P * t:P * t + P], rcount[:, t:t + 1],
                                                            mid[:, t, :], ALU.mult, ALU.add)
                        steps.after(last)
                        norm_vector(dve, sig, steps, "nm", lambda t: mid[:, t, :], nm, lambda t: mn[:, t, :])
                        steps.after(dve.tensor_tensor(mid[:], mid[:], everywhere(4), ALU.add))
                        for b in range(2):
                            c = cond[:, ds(pair * 2 + b, 1), :].to_broadcast([P, 2, D])
                            last = dve.tensor_tensor(mid[:, 2 * b:2 * b + 2, :], mid[:, 2 * b:2 * b + 2, :], c, ALU.add)
                        steps.after(last)
                        dve.wait_ge(sig["mlp_ready"], 1)
                        steps.after(dve.tensor_tensor(mid[:], mid[:], tiles(2), ALU.add))
                        norm_vector(dve, sig, steps, "np", lambda t: mid[:, t, :], np_, lambda t: mn[:, t, :])
                        steps.after(dve.tensor_tensor(mn[:], mn[:], everywhere(5), ALU.mult))
                        dve.tensor_tensor(slots[:], mn[:], everywhere(6), ALU.add)

            with engines_pass(nc) as (block, sig):
                @block.vector
                def _(dve):
                    dve.tensor_tensor(xall, xall, slots[:], ALU.add)



HEADS = 16
KEEP = GROUP
H_DH = 64


def top_heads(nc, dram, X, psum, cst):
    with ExitStack() as ctx:
        def sb(name, shape, dt=F32):
            return ctx.enter_context(nc.sbuf_tensor("h0_" + name, shape, dt))

        wr, br = sb("wr", [P, HEADS]), sb("br", [B, HEADS])
        wo, bo = sb("wo", [P, 2, D]), sb("bo", [P, D])
        onesb = sb("onesb", [B, P])
        n0, n1 = norm_buffers(sb, "n0"), norm_buffers(sb, "n1")
        for n in (n0, n1):
            n["mhalf"] = cst["mhalf"]
        z, zT = sb("z", [P, PT, D]), sb("zT", [P, PTOK])
        tokens_sum = sb("tokens_sum", [P, B])
        dist, dmax, dsum = sb("dist", [B, HEADS]), sb("dmax", [B, 1]), sb("dsum", [B, 1])
        top, topi = sb("top", [B, 8]), sb("topi", [B, 8], U32)
        gexp, gmax, gsum, gother = sb("gexp", [B, KEEP]), sb("gmax", [B, 1]), sb("gsum", [B, 1]), sb("gother", [B, 1])
        gdiag, gates = sb("gdiag", [B, B, KEEP]), sb("gates", [P, B * KEEP])
        picked = sb("picked", [1, B * 8], U32)
        W = sb("w", [P, 3, KEEP, H_DH])
        bcol = sb("bcol", [P, 2, 2])
        brow = sb("brow", [P, KEEP, H_DH])
        gcol, gbat = sb("gcol", [P, 2]), sb("gbat", [P, KEEP])
        t2, tT = sb("t2", [P, 2, D]), sb("tT", [P, S])
        qT, kT = sb("qT", [P, 2, S]), sb("kT", [P, 2, S])
        qb, kb = sb("qb", [P, 2, S], BF16), sb("kb", [P, 2, S], BF16)
        v = sb("v", [P, 2, KEEP, H_DH])
        vt = sb("vt", [P, 2, KEEP, H_DH])
        m = sb("m", [P, 2 * KEEP], BF16)
        probs = sb("probs", [P, 2, 2, GROUP * S])
        rsum = sb("rsum", [P, 2, S])
        oT = sb("oT", [P, 2, S])

        with engines_pass(nc) as (block, sig):
            @block.sync
            def _(sp):
                for dst, src in ((wr, "H0_wr"), (wo, "H0_wo")):
                    sp.dma_start(dst[:], dram[src]).then_inc(sig["loads"], 16)
                sp.dma_start(br[:], dram["H0_br"].to_broadcast([B, HEADS])).then_inc(sig["loads"], 16)
                sp.dma_start(bo[:], dram["H0_bo"].to_broadcast([P, D])).then_inc(sig["loads"], 16)
                sp.wait_ge(sig["loads"], 64)

            @block.gpsimd
            def _(pool):
                pool.memset(onesb[:], 1.0)

        with nc.Fori(0, PAIRS) as pair:
            def x(t):
                return X[:, ds(pair * PT + t, 1), :].rearrange("p a d -> p (a d)")

            with engines_pass(nc) as (block, sig):
                @block.tensor
                def _(pe):
                    pe.wait_ge(sig["n0_normed"], 1)
                    turn_tensor(pe, cst["ident"], psum[:, 0, :], lambda t: z[:, t, :]).then_inc(sig["z_turned"], 1)

                @block.gpsimd
                def _(pool):
                    norm_pool(pool, sig, "n0", n0)

                @block.vector
                def _(dve):
                    steps = Steps(dve, sig["vector_steps"])
                    norm_vector(dve, sig, steps, "n0", x, n0, lambda t: z[:, t, :])
                    dve.wait_ge(sig["z_turned"], 1)
                    dve.tensor_reduce(tokens_sum[:, ds(pair * 2, 2)], psum[:, 0, :].rearrange("p (b s) -> p b s", b=2),
                                      AX.X, ALU.add)

        with engines_pass(nc) as (block, sig):
            @block.tensor
            def _(pe):
                pe.matmul(psum[0:B, 0, 0:HEADS], tokens_sum[:], wr[:], start=True, stop=True).then_inc(sig["logits_ready"], 1)
                pe.wait_ge(sig["gdiag_ready"], 1)
                pe.matmul(psum[:, 1, 0:B * KEEP], onesb[:], gdiag[:].rearrange("p b k -> p (b k)"), start=True, stop=True)\
                    .then_inc(sig["gates_ready"], 1)

            @block.scalar
            def _(act):
                act.wait_ge(sig["dist_shifted"], 1)
                act.activation(dist[:], dist[:], ACT.Exp, accum_out=dsum[:]).then_inc(sig["dist_exp"], 1)
                act.wait_ge(sig["top_ready"], 1)
                act.activation(gexp[:], top[:, 0:KEEP], ACT.Exp, bias=gmax[:], accum_out=gsum[:])
                act.activation(gother[:], gmax[:], ACT.Exp).then_inc(sig["gate_exp"], 1)

            @block.vector
            def _(dve):
                steps = Steps(dve, sig["vector_steps"])
                dve.wait_ge(sig["logits_ready"], 1)
                steps.after(dve.scalar_tensor_tensor(dist[:], psum[0:B, 0, 0:HEADS], 1.0 / S, br[:], ALU.mult, ALU.add))
                steps.after(dve.tensor_reduce(dmax[:], dist[:], AX.X, ALU.max))
                dve.tensor_scalar(dist[:], dist[:], dmax[:], None, ALU.subtract).then_inc(sig["dist_shifted"], 1)
                dve.wait_ge(sig["dist_exp"], 1)
                steps.after(dve.reciprocal(dsum[:], dsum[:]))
                steps.after(dve.tensor_scalar(dist[:], dist[:], dsum[:], None, ALU.mult))
                steps.after(dve.max(top[:], dist[:]))
                dve.max_index(topi[:], top[:], dist[:]).then_inc(sig["picked_ready"], 1)
                dve.tensor_scalar(gmax[:], top[:, 0:1], -1.0, None, ALU.mult).then_inc(sig["top_ready"], 1)
                dve.wait_ge(sig["gate_exp"], 1)
                steps.after(dve.scalar_tensor_tensor(gsum[:], gother[:], float(HEADS - KEEP), gsum[:], ALU.mult, ALU.add))
                steps.after(dve.reciprocal(gsum[:], gsum[:]))
                steps.after(dve.tensor_scalar(gexp[:], gexp[:], gsum[:], None, ALU.mult))
                dve.tensor_tensor(gdiag[:], gexp[:].unsqueeze(1).to_broadcast([B, B, KEEP]),
                                  cst["ident"][0:B, 0:B].unsqueeze(2).to_broadcast([B, B, KEEP]), ALU.mult)\
                    .then_inc(sig["gdiag_ready"], 1)
                dve.wait_ge(sig["gates_ready"], 1)
                dve.tensor_copy(gates[:], psum[:, 1, 0:B * KEEP])

            @block.sync
            def _(sp):
                sp.wait_ge(sig["picked_ready"], 1)
                sp.dma_start(picked[:], topi[:]).then_inc(sig["picked_moved"], 16)
                sp.wait_ge(sig["picked_moved"], 16)

        with nc.Fori(0, B) as b:
            def xb(t):
                return X[:, ds(b * 2 + t, 1), :].rearrange("p a d -> p (a d)")

            xboth = X[:, ds(b * 2, 2), :]
            own = Attention("self", 1, 2, 2, H_DH, 2, S, H_DH ** -0.5)

            def place(h):
                return slice(H_DH * (h % 2), H_DH * (h % 2) + H_DH), h // 2

            def own_max(u, h):
                r, ch = place(h)
                return [(slice(256 * t, 256 * t + 256), [(qb[r, ch, P * t:P * t + P], kb[r, ch, :])]) for t in range(2)]

            def own_scores(u, c, h):
                r, ch = place(h)
                return [(0, [(kT[r, ch, P * c:P * c + P], qT[r, ch, :])])]

            def own_values(u, r, p):
                return [[(slice(H_DH * j, H_DH * j + H_DH), (v[:, c, 2 * r + j, :], cst["ones"][:, 0:H_DH]),
                          p[:, c, prob_cols(2 * r + j, 0, S)]) for j in range(2)] for c in range(2)]

            own.max_products, own.score_products, own.value_products = own_max, own_scores, own_values
            own.max_column = lambda u, h, out, t: h * 2 + t
            own.key_bias = lambda u, c: 0.0
            own.neg_ident = cst["neg_ident"][:]

            with engines_pass(nc) as (block, sig):
                @block.sync
                def _(sp):
                    for k in range(KEEP):
                        head = sp.value_load(picked[0:1, ds(b * 8 + k, 1)], min_val=0, max_val=HEADS - 1)
                        r, ch = place(k)
                        sp.dma_start(W[:, :, k, :], dram["H0_W"][:, :, ds(head, 1), :].rearrange("p i a e -> p i (a e)"))\
                            .then_inc(sig["weights"], 16)
                        sp.dma_start(bcol[r, ch, :], dram["H0_bcol"][ds(head, 1), :, :].rearrange("a e i -> (a e) i"))\
                            .then_inc(sig["biases"], 16)
                        sp.dma_start(brow[:, k, :], dram["H0_bv"][ds(head, 1), :].to_broadcast([P, H_DH]))\
                            .then_inc(sig["biases"], 16)

                @block.tensor
                def _(pe):
                    pe.wait_ge(sig["n1_normed"], 1)
                    turn_tensor(pe, cst["ident"], psum[:, 7, :], lambda t: t2[:, t, :], tiles=2).then_inc(sig["turned"], 1)
                    pe.wait_ge(sig["tT_ready"], 1)
                    pe.wait_ge(sig["weights"], 16 * KEEP)
                    for i in range(2):
                        for ch in range(2):
                            pe.matmul(psum[:, 2 * i + ch, 0:S], W[:, i, 2 * ch:2 * ch + 2, :].rearrange("p k e -> p (k e)"),
                                      tT[:], start=True, stop=True).then_inc(sig["proj_ready"], 1)
                    for t in range(2):
                        pe.matmul(psum[:, 4 + t, 0:S], tT[:, P * t:P * t + P], W[:, 2, :, :].rearrange("p k e -> p (k e)"),
                                  start=True, stop=True).then_inc(sig["proj_ready"], 1)
                    pe.wait_ge(sig["operands_ready"], 1)
                    attention_tensor(pe, sig, own, psum, m, probs)
                    pe.wait_ge(sig["self_values_taken"], 2)
                    for t in range(2):
                        for ch in range(2):
                            last = pe.matmul(psum[:, 2, P * t:P * t + P], oT[:, ch, P * t:P * t + P], wo[:, ch, :],
                                             start=ch == 0, stop=ch == 1)
                    last.then_inc(sig["projected"], 1)

                @block.gpsimd
                def _(pool):
                    norm_pool(pool, sig, "n1", n1, tiles=2)

                @block.scalar
                def _(act):
                    act.wait_ge(sig["turned"], 1)
                    act.copy(tT[:], psum[:, 7, 0:S]).then_inc(sig["tT_ready"], 1)
                    attention_scalar(act, sig, own, psum, probs)

                @block.vector
                def _(dve):
                    steps = Steps(dve, sig["vector_steps"])
                    norm_vector(dve, sig, steps, "n1", xb, n1, lambda t: t2[:, t, :], tiles=2)
                    dve.tensor_copy(gbat[:], gates[:, ds(b * KEEP, KEEP)]).then_inc(sig["gates_taken"], 1)
                    dve.wait_ge(sig["gates_taken"], 1)
                    halves = gbat[:].rearrange("p (c h) -> p c h", h=2)
                    dve.tensor_copy(gcol[0:H_DH, :], halves[0:H_DH, :, 0])
                    steps.after(dve.tensor_copy(gcol[H_DH:P, :], halves[H_DH:P, :, 1]))
                    dve.wait_ge(sig["biases"], 32 * KEEP)
                    for i, dst in enumerate((qT, kT)):
                        for ch in range(2):
                            dve.wait_ge(sig["proj_ready"], 2 * i + ch + 1)
                            last = dve.tensor_scalar(dst[:, ch, :], psum[:, 2 * i + ch, 0:S], bcol[:, ch, i:i + 1],
                                                     gcol[:, ch:ch + 1], ALU.add, ALU.mult)
                    steps.after(last)
                    dve.tensor_copy(qb[:], qT[:])
                    dve.tensor_copy(kb[:], kT[:])
                    dve.wait_ge(sig["proj_ready"], 6)
                    steps.after(dve.tensor_tensor(vt[:].rearrange("p t k e -> p t (k e)"), psum[:, 4:6, 0:S],
                                                  brow[:].rearrange("p k e -> p (k e)").unsqueeze(1).to_broadcast([P, 2, S]),
                                                  ALU.add))
                    for k in range(KEEP):
                        last = dve.tensor_scalar(v[:, :, k, 0:H_DH], vt[:, :, k, :], gbat[:, k:k + 1], None, ALU.mult)
                    last.then_inc(sig["operands_ready"], 1)
                    attention_vector(dve, sig, own, psum, m, rsum, lambda u, r: oT[:, r, :])
                    steps.after(dve.tensor_tensor(xboth, xboth, bo[:].unsqueeze(1).to_broadcast([P, 2, D]), ALU.add))
                    dve.wait_ge(sig["projected"], 1)
                    dve.tensor_tensor(xboth, xboth, psum[:, 2, 0:2 * D].rearrange("p (t d) -> p t d", t=2), ALU.add)



STEPS_A_PASS = 16


def attentive_gru(nc, dram, X, psum, cst):
    with ExitStack() as ctx:
        def sb(name, shape, dt=F32):
            return ctx.enter_context(nc.sbuf_tensor("g1_" + name, shape, dt))

        wa = sb("wa", [P, 2, D])
        wi = sb("wi", [P, 2, 3, D])
        uh = sb("uh", [P, 3, D])
        bias = sb("bias", [P, 3])
        vcol = sb("vcol", [P, 1])
        vneg = sb("vneg", [P, 2, 32])
        ctxT = sb("ctxT", [P, B * C])
        encw = sb("encw", [P, PAIRS, 3, D])
        pick = sb("pick", [P, 2, B])
        n0 = norm_buffers(sb, "n0")
        n0["mhalf"] = cst["mhalf"]
        z, zT = sb("z", [P, PT, D]), sb("zT", [P, PTOK])
        GX = sb("gx", [P, 3, B, S])
        HT = sb("ht", [P, B, S])
        encp = sb("encp", [P, 2, PAIRS, C])
        h = sb("h", [P, 2, B])
        pre, th = sb("pre", [P, 2, PAIRS, C]), sb("th", [P, 2, PAIRS, C])
        smin, ssum, attn, attnT = sb("smin", [P, 1]), sb("ssum", [P, 1]), sb("attn", [P, C]), sb("attnT", [P, B + 32])
        shares = sb("shares", [P, 2, B])
        crows = sb("crows", [P, 3, D])
        rest, gates, gh, gxh = sb("rest", [P, 2, B]), sb("gates", [P, 2, B]), sb("gh", [P, B]), sb("gxh", [P, B])
        wa_half = sb("wa_half", [P, D])
        tr, tz, u, cand, omz, zh, part = (sb(n, [P, B]) for n in ("tr", "tz", "u", "cand", "omz", "zh", "part"))

        with engines_pass(nc) as (block, sig):
            @block.sync
            def _(sp):
                for dst, src in ((wa, "G1_wa"), (wi, "G1_wi"), (uh, "G1_uh"), (bias, "G1_bias"), (vcol, "G1_v"),
                                 (ctxT, "ctxT"), (pick, "c_pick")):
                    sp.dma_start(dst[:], dram[src]).then_inc(sig["loads"], 16)
                sp.dma_start(h[:, 0, :], dram["embT"]).then_inc(sig["loads"], 16)

            @block.tensor
            def _(pe):
                pe.wait_ge(sig["loads"], 128)
                pe.matmul(psum[:, 0, :], wa[:, 1, :], ctxT[:], start=True, stop=True).then_inc(sig["encp_ready"], 1)
                for p in range(PAIRS):
                    pe.matmul(psum[:, 1 + p, 0:3 * D], ctxT[:, P * p:P * p + P], wi[:, 1, :, :].rearrange("p g d -> p (g d)"),
                              start=True, stop=True).then_inc(sig["encw_ready"], 1)

            @block.scalar
            def _(act):
                for p in range(PAIRS):
                    act.wait_ge(sig["encw_ready"], p + 1)
                    act.copy(encw[:, p, :, :].rearrange("p g d -> p (g d)"), psum[:, 1 + p, 0:3 * D])
                act.wait_ge(sig["encp_ready"], 1)
                act.copy(encp[:], psum[:, 0, :].rearrange("p (b i s) -> p i b s", i=2, s=C))

            @block.vector
            def _(dve):
                steps = Steps(dve, sig["vector_steps"])
                dve.wait_ge(sig["loads"], 128)
                dve.memset(attnT[:], 0.0)
                steps.after(dve.memset(vneg[:], 0.0))
                dve.tensor_scalar(wa_half[:], wa[:, 0, :], 0.5, None, ALU.mult)
                for i in range(2):
                    dve.tensor_scalar(vneg[:, i, i:i + 1], vcol[:], -1.0, None, ALU.mult)

        with nc.Fori(0, PAIRS) as pair:
            def x(t):
                return X[:, ds(pair * PT + t, 1), :].rearrange("p a d -> p (a d)")

            with engines_pass(nc) as (block, sig):
                @block.tensor
                def _(pe):
                    pe.wait_ge(sig["n0_normed"], 1)
                    turn_tensor(pe, cst["ident"], psum[:, 0, :], lambda t: z[:, t, :]).then_inc(sig["z_turned"], 1)
                    pe.wait_ge(sig["zT_ready"], 1)
                    for i in range(3):
                        pe.matmul(psum[:, 1 + i, :], wi[:, 0, i, :], zT[:], start=True, stop=True)\
                            .then_inc(sig["gates_ready"], 1)

                @block.gpsimd
                def _(pool):
                    norm_pool(pool, sig, "n0", n0)

                @block.scalar
                def _(act):
                    act.wait_ge(sig["z_turned"], 1)
                    act.copy(zT[:], psum[:, 0, :]).then_inc(sig["zT_ready"], 1)
                    for i in range(3):
                        act.wait_ge(sig["gates_ready"], i + 1)
                        act.activation(GX[:, i, ds(pair * 2, 2), :], psum[:, 1 + i, :].rearrange("p (b s) -> p b s", b=2),
                                       ACT.Identity, bias=bias[:, i:i + 1])

                @block.vector
                def _(dve):
                    steps = Steps(dve, sig["vector_steps"])
                    norm_vector(dve, sig, steps, "n0", x, n0, lambda t: z[:, t, :])

        with nc.Fori(0, S // STEPS_A_PASS) as group:
            with engines_pass(nc) as (block, sig):
                def gx(first, n, s):
                    return GX[:, first:first + n, :, ds(group * STEPS_A_PASS + s, 1)].rearrange("p g b a -> p g (b a)")

                def by_pair(columns):
                    return columns.rearrange("p (b i) -> p b i", i=2)

                @block.tensor
                def _(pe):
                    for s in range(STEPS_A_PASS):
                        hs = h[:, s % 2, :]
                        if s == 0:
                            pe.matmul(psum[:, 0, 0:B], wa[:, 0, :], hs, start=True, stop=True)\
                                .then_inc(sig["query_ready"], 1)
                        else:
                            pe.wait_ge(sig["kept_part_ready"], s)
                            pe.matmul(psum[:, 0, 0:B], wa_half[:], zh[:], start=True, stop=False)
                            pe.wait_ge(sig["new_part_ready"], s)
                            pe.matmul(psum[:, 0, 0:B], wa[:, 0, :], part[:], start=False, stop=True)\
                                .then_inc(sig["query_ready"], 1)
                        for i in range(2):
                            pe.wait_ge(sig["tanh_ready"], 2 * s + i + 1)
                            for p in range(PAIRS):
                                last = pe.matmul(psum[32 * p:32 * p + 32, 1, 0:C], vneg[:, i, :], th[:, i, p, :],
                                                 start=i == 0, stop=i == 1)
                        last.then_inc(sig["scores_ready"], 1)
                        if s >= 1:
                            pe.wait_ge(sig["state_ready"], s)
                        for gate, bank in ((0, 4), (1, 5), (2, 6)):
                            pe.matmul(psum[:, bank, 0:B], uh[:, gate, :], hs, start=True, stop=True)\
                                .then_inc(sig["state_products_ready"], 1)
                        pe.wait_ge(sig["shares_ready"], s + 1)
                        for i in range(2):
                            last = pe.matmul(psum[C * i:C * i + C, 2, 0:B], attn[:], shares[:, i, :], start=True, stop=True)
                        last.then_inc(sig["attn_turned"], 1)
                        pe.wait_ge(sig["attnT_ready"], s + 1)

                        def context_part(gate, bank):
                            for p in range(PAIRS):
                                last = pe.matmul(psum[32 * p:32 * p + 32, bank, 0:D], attnT[:, 2 * p:2 * p + 32],
                                                 encw[:, p, gate, :], start=True, stop=True)
                            last.then_inc(sig["context_ready"], 1)

                        def turn_part(i, bank, taken, count):
                            pe.wait_ge(sig[taken], count)
                            pe.transpose(psum[:, bank, 0:P], crows[:, i, :], cst["ident"][:]).then_inc(sig["context_turned"], 1)

                        context_part(1, 3)
                        context_part(2, 1)
                        context_part(0, 2)
                        turn_part(0, 3, "context_taken", 2 * s + 1)
                        turn_part(1, 1, "context_taken_by_scalar", s + 1)
                        turn_part(2, 2, "context_taken", 2 * s + 2)

                @block.scalar
                def _(act):
                    for s in range(STEPS_A_PASS):
                        for i in range(2):
                            act.wait_ge(sig["tanh_input_ready"], 2 * s + i + 1)
                            act.activation(th[:, i, :, :], pre[:, i, :, :], ACT.Tanh).then_inc(sig["tanh_ready"], 1)
                        act.wait_ge(sig["smin_ready"], s + 1)
                        act.activation(attn[:], psum[:, 1, 0:C], ACT.Exp, bias=smin[:], scale=-1.0,
                                       accum_out=ssum[:]).then_inc(sig["exp_ready"], 1)
                        act.wait_ge(sig["context_ready"], 3 * s + 2)
                        act.copy(crows[:, 1, :], psum[:, 1, 0:D]).then_inc(sig["context_taken_by_scalar"], 1)
                        act.wait_ge(sig["gate_r_ready"], s + 1)
                        act.activation(tr[:], gates[:, 1, :], ACT.Tanh, scale=0.5).then_inc(sig["tanh_r_ready"], 1)
                        act.wait_ge(sig["gate_z_ready"], s + 1)
                        act.activation(tz[:], gates[:, 0, :], ACT.Tanh, scale=0.5).then_inc(sig["tanh_z_ready"], 1)
                        act.wait_ge(sig["candidate_input_ready"], s + 1)
                        act.activation(cand[:], u[:], ACT.Tanh).then_inc(sig["candidate_ready"], 1)

                @block.gpsimd
                def _(pool):
                    for s in range(STEPS_A_PASS):
                        pool.wait_ge(sig["state_ready"], s + 1)
                        pool.tensor_copy(HT[:, :, ds(group * STEPS_A_PASS + s, 1)], h[:, (s + 1) % 2, :].unsqueeze(2))\
                            .then_inc(sig["state_kept"], 1)

                @block.vector
                def _(dve):
                    steps = Steps(dve, sig["vector_steps"])

                    for s in range(STEPS_A_PASS):
                        dve.wait_ge(sig["query_ready"], s + 1)
                        query = psum[:, 0, 0:B].rearrange("p (b i) -> p i b", i=2)
                        for i in range(2):
                            dve.tensor_tensor(pre[:, i, :, :], encp[:, i, :, :],
                                              query[:, i, :].unsqueeze(2).to_broadcast([P, PAIRS, C]), ALU.add)\
                                .then_inc(sig["tanh_input_ready"], 1)
                        if s >= 1:
                            if s >= 2:
                                dve.wait_ge(sig["state_kept"], s - 1)
                            dve.scalar_tensor_tensor(h[:, s % 2, :], zh[:], 0.5, part[:], ALU.mult, ALU.add).then_inc(sig["state_ready"], 1)
                        dve.wait_ge(sig["scores_ready"], s + 1)
                        dve.tensor_reduce(smin[:], psum[:, 1, 0:C], AX.X, ALU.min).then_inc(sig["smin_ready"], 1)
                        dve.wait_ge(sig["exp_ready"], s + 1)
                        steps.after(dve.reciprocal(ssum[:], ssum[:]))
                        dve.tensor_scalar(shares[:], pick[:], ssum[:], None, ALU.mult).then_inc(sig["shares_ready"], 1)
                        dve.wait_ge(sig["attn_turned"], s + 1)
                        dve.tensor_copy(attnT[:, 0:B], psum[:, 2, 0:B]).then_inc(sig["attnT_ready"], 1)
                        dve.wait_ge(sig["state_products_ready"], 3 * s + 2)
                        dve.tensor_tensor(rest[:], psum[:, 4:6, 0:B], gx(0, 2, s), ALU.add).then_inc(sig["rest_ready"], 1)
                        dve.tensor_copy(gxh[:].unsqueeze(1), gx(2, 1, s))
                        dve.wait_ge(sig["context_ready"], 3 * s + 1)
                        dve.tensor_copy(crows[:, 0, :], psum[:, 3, 0:D]).then_inc(sig["context_taken"], 1)
                        dve.wait_ge(sig["context_ready"], 3 * s + 3)
                        dve.tensor_copy(crows[:, 2, :], psum[:, 2, 0:D]).then_inc(sig["context_taken"], 1)

                        def turned(bank):
                            return psum[:, bank, 0:P].rearrange("q (p c) -> q p c", c=32)[:, :, 0:2]

                        dve.wait_ge(sig["rest_ready"], s + 1)
                        dve.wait_ge(sig["context_turned"], 3 * s + 1)
                        dve.tensor_tensor(by_pair(gates[:, 1, :]), turned(3), by_pair(rest[:, 1, :]), ALU.add)\
                            .then_inc(sig["gate_r_ready"], 1)
                        dve.wait_ge(sig["context_turned"], 3 * s + 2)
                        dve.tensor_tensor(by_pair(gh[:]), turned(1), by_pair(gxh[:]), ALU.add)\
                            .then_inc(sig["candidate_part_ready"], 1)
                        dve.wait_ge(sig["context_turned"], 3 * s + 3)
                        dve.tensor_tensor(by_pair(gates[:, 0, :]), turned(2), by_pair(rest[:, 0, :]), ALU.add)\
                            .then_inc(sig["gate_z_ready"], 1)
                        dve.wait_ge(sig["tanh_r_ready"], s + 1)
                        dve.wait_ge(sig["state_products_ready"], 3 * s + 3)
                        steps.after(dve.scalar_tensor_tensor(u[:], tr[:], 1.0, psum[:, 6, 0:B], ALU.add, ALU.mult))
                        dve.wait_ge(sig["candidate_part_ready"], s + 1)
                        dve.scalar_tensor_tensor(u[:], u[:], 0.5, gh[:], ALU.mult, ALU.add)\
                            .then_inc(sig["candidate_input_ready"], 1)
                        dve.wait_ge(sig["tanh_z_ready"], s + 1)
                        dve.tensor_scalar(omz[:], tz[:], -0.5, 0.5, ALU.mult, ALU.add)
                        dve.scalar_tensor_tensor(zh[:], tz[:], 1.0, h[:, s % 2, :], ALU.add, ALU.mult)\
                            .then_inc(sig["kept_part_ready"], 1)
                        dve.wait_ge(sig["kept_part_ready"], s + 1)
                        dve.wait_ge(sig["candidate_ready"], s + 1)
                        dve.tensor_tensor(part[:], omz[:], cand[:], ALU.mult).then_inc(sig["new_part_ready"], 1)
                        dve.wait_ge(sig["new_part_ready"], s + 1)
                    dve.wait_ge(sig["kept_part_ready"], STEPS_A_PASS)
                    dve.wait_ge(sig["state_kept"], STEPS_A_PASS - 1)
                    dve.scalar_tensor_tensor(h[:, 0, :], zh[:], 0.5, part[:], ALU.mult, ALU.add).then_inc(sig["state_ready"], 1)

        with engines_pass(nc) as (block, sig):
            @block.tensor
            def _(pe):
                for i in range(PAIRS):
                    for t in range(PT):
                        b, half = 2 * i + t // 2, t % 2
                        last = pe.transpose(psum[:, i, P * t:P * t + P], HT[:, b, P * half:P * half + P], cst["ident"][:])
                    last.then_inc(sig["states_turned"], 1)

            @block.vector
            def _(dve):
                for i in range(PAIRS):
                    dve.wait_ge(sig["states_turned"], i + 1)
                    xs = X[:, PT * i:PT * i + PT, :]
                    dve.tensor_tensor(xs, xs, psum[:, i, :].rearrange("p (t d) -> p t d", t=PT), ALU.add)



CAP = B * S // 8


def switch_experts(nc, dram, X, psum, cst):
    with ExitStack() as ctx:
        def sb(name, shape, dt=F32):
            return ctx.enter_context(nc.sbuf_tensor("s1_" + name, shape, dt))

        sent = nc.dram_tensor("s1_sent", (E * CAP, D), F32, kind="Internal").ap()
        back = nc.dram_tensor("s1_back", (E * CAP, D), F32, kind="Internal").ap()
        wr, number, before, ones = sb("wr", [P, E]), sb("number", [P, E]), sb("before", [P, P]), sb("ones", [P, P])
        zeros = sb("zeros", [P, 2, D])
        n0 = norm_buffers(sb, "n0")
        n0["mhalf"] = cst["mhalf"]
        XN = sb("xn", [P, TILES, D])
        z, zT = sb("z", [P, PT, D]), sb("zT", [P, PTOK])
        logits, ex, lmax, lsum = sb("logits", [P, PT, E]), sb("ex", [P, PT, E]), sb("lmax", [P, PT]), sb("lsum", [P, PT])
        top, topi, topf = sb("top", [P, PT, 8]), sb("topi", [P, PT, 8], U32), sb("topf", [P, PT, 1])
        chosen = sb("chosen", [P, TILES, E])
        earlier = sb("earlier", [P, TILES, E])
        gate, expert = sb("gate", [P, TILES]), sb("expert", [P, TILES])
        place3, place = sb("place3", [P, TILES, E]), sb("place", [P, TILES])
        keep, slot, away = sb("keep", [P, TILES]), sb("slot", [P, TILES]), sb("away", [P, TILES])
        slot_i, away_i = sb("slot_i", [P, TILES], U32), sb("away_i", [P, TILES], U32)
        w1, w2 = sb("w1", [P, EF, P]), sb("w2", [P, EF, D])
        tok, tokT, hid, res = sb("tok", [P, 2, D]), sb("tokT", [P, CAP]), sb("hid", [P, EF, CAP]), sb("res", [P, 2, D])
        got = sb("got", [P, TILES, D])

        with engines_pass(nc) as (block, sig):
            @block.sync
            def _(sp):
                sp.dma_start(wr[:], dram["S1_wr"]).then_inc(sig["loads"], 16)
                sp.dma_start(before[:], dram["c_before"]).then_inc(sig["loads"], 16)
                sp.dma_start(number[:], dram["c_number"].to_broadcast([P, E])).then_inc(sig["loads"], 16)
                sp.wait_ge(sig["zeros_ready"], 1)
                for e in range(E):
                    sp.dma_start(sent[CAP * e:CAP * (e + 1), :].rearrange("(t p) d -> p t d", p=P), zeros[:])\
                        .then_inc(sig["cleared"], 16)
                sp.wait_ge(sig["cleared"], 16 * E)
                sp.wait_ge(sig["loads"], 48)

            @block.gpsimd
            def _(pool):
                pool.memset(zeros[:], 0.0).then_inc(sig["zeros_ready"], 1)
                pool.memset(ones[:], 1.0)

        with nc.Fori(0, PAIRS) as pair:
            def x(t):
                return X[:, ds(pair * PT + t, 1), :].rearrange("p a d -> p (a d)")

            with engines_pass(nc) as (block, sig):
                @block.tensor
                def _(pe):
                    pe.wait_ge(sig["n0_normed"], 1)
                    turn_tensor(pe, cst["ident"], psum[:, 0, :], lambda t: z[:, t, :]).then_inc(sig["z_turned"], 1)
                    pe.wait_ge(sig["zT_ready"], 1)
                    for t in range(PT):
                        last = pe.matmul(psum[:, 1, E * t:E * t + E], zT[:, P * t:P * t + P], wr[:], start=True, stop=True)
                    last.then_inc(sig["logits_ready"], 1)

                @block.gpsimd
                def _(pool):
                    norm_pool(pool, sig, "n0", n0)
                    pool.wait_ge(sig["n0_normed"], 1)
                    pool.tensor_copy(XN[:, ds(pair * PT, PT), :], z[:])

                @block.scalar
                def _(act):
                    act.wait_ge(sig["z_turned"], 1)
                    act.copy(zT[:], psum[:, 0, :]).then_inc(sig["zT_ready"], 1)
                    act.wait_ge(sig["shifted_logits_ready"], 1)
                    act.activation(ex[:], logits[:], ACT.Exp).then_inc(sig["exp_ready"], 1)

                @block.vector
                def _(dve):
                    steps = Steps(dve, sig["vector_steps"])

                    def wide(col):
                        return col.unsqueeze(2).to_broadcast([P, PT, E])

                    norm_vector(dve, sig, steps, "n0", x, n0, lambda t: z[:, t, :])
                    dve.wait_ge(sig["logits_ready"], 1)
                    steps.after(dve.tensor_copy(logits[:], psum[:, 1, 0:PT * E].rearrange("p (t e) -> p t e", e=E)))
                    steps.after(dve.tensor_reduce(lmax[:], logits[:], AX.X, ALU.max))
                    dve.tensor_tensor(logits[:], logits[:], wide(lmax[:]), ALU.subtract)\
                        .then_inc(sig["shifted_logits_ready"], 1)
                    dve.wait_ge(sig["exp_ready"], 1)
                    steps.after(dve.tensor_reduce(lsum[:], ex[:], AX.X, ALU.add))
                    for t in range(PT):
                        last = dve.max(top[:, t, :], ex[:, t, :])
                    steps.after(last)
                    for t in range(PT):
                        last = dve.max_index(topi[:, t, :], top[:, t, :], ex[:, t, :])
                    steps.after(last)
                    steps.after(dve.tensor_copy(topf[:], topi[:, :, 0:1]))
                    dve.reciprocal(gate[:, ds(pair * PT, PT)], lsum[:])
                    dve.tensor_copy(expert[:, ds(pair * PT, PT)].unsqueeze(2), topf[:])
                    dve.tensor_tensor(chosen[:, ds(pair * PT, PT), :], topf[:].to_broadcast([P, PT, E]),
                                      number[:].unsqueeze(1).to_broadcast([P, PT, E]), ALU.is_equal)

        with engines_pass(nc) as (block, sig):
            @block.tensor
            def _(pe):
                pe.wait_ge(sig["vector_steps"], TILES)
                for i in range(TILES):
                    out = psum[:, 0, E * i:E * i + E]
                    pe.matmul(out, before[:], chosen[:, i, :], start=True, stop=False)
                    last = pe.matmul(out, ones[:], earlier[:, i, :], start=False, stop=True)
                last.then_inc(sig["counts_ready"], 1)

            @block.vector
            def _(dve):
                steps = Steps(dve, sig["vector_steps"])
                steps.after(dve.memset(earlier[:, 0, :], 0.0))
                for i in range(1, TILES):
                    steps.after(dve.tensor_tensor(earlier[:, i, :], earlier[:, i - 1, :], chosen[:, i - 1, :], ALU.add))
                dve.wait_ge(sig["counts_ready"], 1)
                steps.after(dve.tensor_tensor(place3[:], psum[:, 0, 0:TILES * E].rearrange("p (t e) -> p t e", e=E),
                                              chosen[:], ALU.mult))
                steps.after(dve.tensor_reduce(place[:], place3[:], AX.X, ALU.add))
                steps.after(dve.tensor_scalar(keep[:], place[:], float(CAP), None, ALU.is_lt))
                steps.after(dve.tensor_scalar(slot[:], place[:], float(CAP - 1), None, ALU.min))
                steps.after(dve.scalar_tensor_tensor(slot[:], expert[:], float(CAP), slot[:], ALU.mult, ALU.add))
                steps.after(dve.tensor_scalar(away[:], keep[:], -float(2 * E * CAP), float(2 * E * CAP), ALU.mult, ALU.add))
                steps.after(dve.tensor_tensor(away[:], away[:], slot[:], ALU.add))
                steps.after(dve.tensor_tensor(gate[:], gate[:], keep[:], ALU.mult))
                dve.tensor_copy(slot_i[:], slot[:])
                dve.tensor_copy(away_i[:], away[:]).then_inc(sig["slots_ready"], 1)

            @block.gpsimd
            def _(pool):
                pool.wait_ge(sig["slots_ready"], 1)
                for i in range(TILES):
                    pool.indirect_dma_start(out=sent[:, :], out_offset=bass.IndirectOffsetOnAxis(ap=away_i[:, i:i + 1], axis=0),
                                            in_=XN[:, i, :], in_offset=None, bounds_check=E * CAP - 1, oob_is_err=False)\
                        .then_inc(cst["tokens_sent"], 16)
                pool.wait_ge(cst["tokens_sent"], 16 * TILES)

        with nc.Fori(0, E) as e:
            with engines_pass(nc) as (block, sig):
                @block.sync
                def _(sp):
                    sp.dma_start(tok[:], sent[ds(e * CAP, CAP), :].rearrange("(t p) d -> p t d", p=P))\
                        .then_inc(sig["tokens"], 16)
                    sp.dma_start(w1[:], dram["S1_w1"][ds(e, 1)].rearrange("a p f n -> (a p) f n")).then_inc(sig["w1"], 16)
                    sp.dma_start(w2[:], dram["S1_w2"][ds(e, 1)].rearrange("a p f n -> (a p) f n")).then_inc(sig["w2"], 16)
                    sp.wait_ge(sig["res_ready"], 1)
                    sp.dma_start(back[ds(e * CAP, CAP), :].rearrange("(t p) d -> p t d", p=P), res[:])\
                        .then_inc(sig["returned"], 16)
                    sp.wait_ge(sig["returned"], 16)

                @block.tensor
                def _(pe):
                    pe.wait_ge(sig["tokens"], 16)
                    turn_tensor(pe, cst["ident"], psum[:, 0, :], lambda t: tok[:, t, :], tiles=2)\
                        .then_inc(sig["tokens_turned"], 1)
                    pe.wait_ge(sig["tokT_ready"], 1)
                    pe.wait_ge(sig["w1"], 16)
                    for i in range(EF):
                        pe.matmul(psum[:, 1 + i, 0:CAP], w1[:, i, :], tokT[:], start=True, stop=True)\
                            .then_inc(sig["units_ready"], 1)
                    pe.wait_ge(sig["w2"], 16)
                    pe.wait_ge(sig["gelu_ready"], EF)
                    for t in range(2):
                        for i in range(EF):
                            last = pe.matmul(psum[:, 5, P * t:P * t + P], hid[:, i, P * t:P * t + P], w2[:, i, :],
                                             start=i == 0, stop=i == EF - 1)
                    last.then_inc(sig["result_ready"], 1)

                @block.vector
                def _(dve):
                    dve.wait_ge(sig["tokens_turned"], 1)
                    dve.tensor_copy(tokT[:], psum[:, 0, 0:CAP]).then_inc(sig["tokT_ready"], 1)
                    dve.wait_ge(sig["result_ready"], 1)
                    dve.tensor_copy(res[:].rearrange("p t d -> p (t d)"), psum[:, 5, 0:2 * D]).then_inc(sig["res_ready"], 1)

                @block.scalar
                def _(act):
                    for i in range(EF):
                        act.wait_ge(sig["units_ready"], i + 1)
                        act.activation(hid[:, i, :], psum[:, 1 + i, 0:CAP], ACT.Gelu_apprx_tanh)\
                            .then_inc(sig["gelu_ready"], 1)

        with engines_pass(nc) as (block, sig):
            @block.gpsimd
            def _(pool):
                for i in range(TILES):
                    pool.indirect_dma_start(out=got[:, i, :], out_offset=None, in_=back[:, :],
                                            in_offset=bass.IndirectOffsetOnAxis(ap=slot_i[:, i:i + 1], axis=0))\
                        .then_inc(cst["results_got"], 16)

            @block.vector
            def _(dve):
                dve.wait_ge(cst["results_got"], 16 * TILES)
                for i in range(TILES):
                    dve.scalar_tensor_tensor(X[:, i, :], got[:, i, :], gate[:, i:i + 1], X[:, i, :], ALU.mult, ALU.add)



L2_LAYERS = 6
L2_DH = 8
MASK_ROWS = (slice(64, 65), slice(0, 1))
TURNED = (7, 0)
FF_BANKS = (0, 1, 6, 7)
L2_FF = 4
L2_W = {"q": 0, "qs": 128, "k": 256, "ks": 384, "v": 512, "so": 640, "cq": 768, "cqs": 896, "ck": 1024,
        "cks": 1152, "cv": 1280, "co": 1408, "f1": 1536, "f2": 2048}
L2_WCOLS = 2560


def dit_layers(nc, dram, X, psum, cst):
    with ExitStack() as ctx:
        def sb(name, shape, dt=F32):
            return ctx.enter_context(nc.sbuf_tensor("l2_" + name, shape, dt))

        Y = sb("y", [P, TILES, D])
        nw = sb("nw", [P, L2_LAYERS * 3 * 2, D])
        nb = sb("nb", [P, L2_LAYERS * 3 * 2])
        embT = sb("embT", [P, B])
        ada = sb("ada", [P, L2_LAYERS * 3 * 2 * B])
        W = sb("w", [P, L2_WCOLS])
        f1b = sb("f1b", [P, L2_LAYERS * L2_FF])
        f2b = sb("f2b", [P, L2_LAYERS, D])
        f2bl = sb("f2bl", [P, D])
        ctxT = sb("ctxT", [P, B * C])
        cctx = sb("cctx", [P, 2 * C])
        mcol = sb("mcol", [P, TILES])
        mccol = sb("mccol", [P, PAIRS])
        mrow8 = sb("mrow8", [P, B * S], U8)
        mcrow8 = sb("mcrow8", [P, B * C], U8)
        mcol8 = sb("mcol8", [P, TILES], U8)
        mccol8 = sb("mccol8", [P, PAIRS], U8)
        mrow = sb("mrow", [P, B * S], BF16)
        mcrow = sb("mcrow", [P, B * C], BF16)
        n1, n2, n3 = (norm_buffers(sb, n) for n in ("n1", "n2", "n3"))
        for n in (n1, n2, n3):
            n["mhalf"] = cst["mhalf"]
        xn = sb("xn", [P, PT, D])
        xnT = sb("xnT", [P, PTOK])
        t1, t2 = sb("t1", [P, PTOK]), sb("t2", [P, PTOK])
        qT, kT = sb("qT", [P, PTOK]), sb("kT", [P, 2, PTOK])
        qm = sb("qm", [P, 2 * GROUP, PTOK])
        qmb = sb("qmb", [P, H, PTOK], BF16)
        kb, kcb = sb("kb", [P, 2, PTOK], BF16), sb("kcb", [P, 2, 2 * C], BF16)
        v = sb("v", [P, PT, H, 32])
        m = sb("m", [P, H * 4], BF16)
        m2 = sb("m2", [P, H * 4], BF16)
        probs = sb("probs", [P, 2, 2, GROUP * S])
        rsum = sb("rsum", [P, 2, 2, GROUP])
        heads_out = sb("heads_out", [P, 2, S])
        o = sb("o", [P, PT, D])
        warm = sb("warm", [P, 1])
        oT = sb("oT", [P, PTOK])
        hT = sb("hT", [P, L2_FF, PTOK])

        with engines_pass(nc) as (block, sig):
            @block.sync
            def _(sp):
                for dst, src in ((nw, "L2_nw"), (nb, "L2_nb"), (embT, "embT"), (f1b, "L2_f1b"),
                                 (ctxT, "ctxT"), (mcol8, "mask_col"), (mccol8, "cmask_col")):
                    sp.dma_start(dst[:], dram[src]).then_inc(sig["loads"], 16)
                for dst, src, n in ((mrow8, "mask_row", B * S), (mcrow8, "cmask_row", B * C)):
                    sp.dma_start(dst[:], dram[src].to_broadcast([P, n])).then_inc(sig["loads"], 16)
                sp.dma_start(f2b[:].rearrange("p l d -> p (l d)"),
                             dram["L2_f2b"].to_broadcast([P, L2_LAYERS * D])).then_inc(sig["loads"], 16)

            @block.tensor
            def _(pe):
                pe.wait_ge(sig["loads"], 160)
                for i in range(L2_LAYERS * 3 * 2):
                    last = pe.matmul(psum[:, 0, i * B:(i + 1) * B], nw[:, i, :], embT[:], start=True, stop=True)
                last.then_inc(sig["ada_ready"], 1)

            @block.gpsimd
            def _(pool):
                pool.memset(kT[:], 0.0)
                pool.memset(kb[:], 0.0)
                pool.memset(kcb[:], 0.0)
                pool.memset(qmb[:], 0.0).then_inc(sig["copies_cleared"], 1)
                pool.memset(v[:, :, :, L2_DH:L2_DH + 1], 1.0)
                pool.memset(v[:, :, :, L2_DH + 1:32], 0.0)
                for i in range(PAIRS):
                    w = {k: (t if k == "mhalf" else t) for k, t in n1.items()}
                    pool.wait_ge(sig["x_var_ready"], i + 1)
                    pool.tensor_scalar(w["veps"][:], w["mv"][:, :, 1:2], EPS, 1.0, ALU.add, ALU.mult)\
                        .then_inc(sig["x_veps_ready"], 1)
                    pool.wait_ge(sig["x_veps_ready"], i + 1)
                    pool.tensor_tensor(w["rstd"][:], w["veps"][:], w["mhalf"][:], ALU.pow)\
                        .then_inc(sig["x_rstd_ready"], 1)

            @block.vector
            def _(dve):
                steps = Steps(dve, sig["vector_steps"])
                dve.wait_ge(sig["copies_cleared"], 1)
                for i, r in enumerate(MASK_ROWS):
                    dve.memset(qmb[r, 8 * i:8 * i + 8, :], 1.0)
                for i in range(PAIRS):
                    for t in range(PT):
                        last = dve.bn_stats(n1["stats"][:, t, :], X[:, PT * i + t, :])
                    steps.after(last)
                    for t in range(PT):
                        last = dve.bn_aggr(n1["mv"][:, t, :], n1["stats"][:, t, :])
                    last.then_inc(sig["x_var_ready"], 1)
                    dve.wait_ge(sig["x_rstd_ready"], i + 1)
                    for t in range(PT):
                        last = dve.tensor_scalar(Y[:, PT * i + t, :], X[:, PT * i + t, :], n1["mv"][:, t, 0:1],
                                                 n1["rstd"][:, t, :], ALU.subtract, ALU.mult)
                    steps.after(last)
                dve.wait_ge(sig["loads"], 160)
                dve.tensor_scalar(mrow[:], mrow8[:], NEG, None, ALU.mult)
                dve.tensor_scalar(mcrow[:], mcrow8[:], NEG, None, ALU.mult)
                dve.tensor_scalar(mcol[:], mcol8[:], NEG, None, ALU.mult)
                dve.tensor_scalar(mccol[:], mccol8[:], NEG, None, ALU.mult)
                gains = nb[:].rearrange("p (i two) -> p i two", two=2)[:, :, 0]
                steps.after(dve.tensor_scalar(gains, gains, 1.0, None, ALU.add))
                dve.wait_ge(sig["ada_ready"], 1)
                dve.tensor_tensor(ada[:].rearrange("p (i b) -> p i b", b=B),
                                  psum[:, 0, 0:L2_LAYERS * 6 * B].rearrange("p (i b) -> p i b", b=B),
                                  nb[:].unsqueeze(2).to_broadcast([P, L2_LAYERS * 6, B]), ALU.add)

        with nc.Fori(0, L2_LAYERS) as layer:
            with engines_pass(nc) as (block, sig):
                @block.sync
                def _(sp):
                    sp.dma_start(W[:], dram["L2_W"][ds(layer, 1)].rearrange("a p n -> (a p) n"))\
                        .then_inc(sig["weights"], 16)
                    sp.wait_ge(sig["weights"], 16)

                @block.scalar
                def _(act):
                    act.copy(f2bl[:], f2b[:, ds(layer, 1), :].rearrange("p a d -> p (a d)"))

            with nc.Fori(0, PAIRS) as pair:
                tag = {}

                def w(name, cols=P):
                    return W[:, L2_W[name]:L2_W[name] + cols]

                def gain(norm, b):
                    return ada[:, ds(layer * (6 * B) + norm * (2 * B) + pair * 2 + b, 1)]

                def shift(norm, b):
                    return ada[:, ds(layer * (6 * B) + norm * (2 * B) + B + pair * 2 + b, 1)]

                def y(t):
                    return Y[:, ds(pair * PT + t, 1), :].rearrange("p a d -> p (a d)")

                yall = Y[:, ds(pair * PT, PT), :]

                def half(g):
                    return g // 2

                def alone(g, h):
                    return GROUP * (g % 2) + h

                own = Attention("self", 2 * (H // GROUP), 2, 1, L2_DH, 2, S, L2_DH ** -0.5)

                def own_max(u, h):
                    b, g = u // 4, u % 4
                    return [(slice(256 * t, 256 * t + 256),
                             [(qmb[:, GROUP * g + h, S * b + P * t:S * b + P * t + P], kb[:, half(g), S * b:S * b + S])]) for t in range(2)]

                def own_scores(u, c, h):
                    b, g = u // 4, u % 4
                    return [(0, [(kT[:, half(g), S * b + P * c:S * b + P * c + P], qm[:, alone(g, h), S * b:S * b + S])])]

                def own_values(u, r, p):
                    b, g = u // 4, u % 4
                    return [[(slice(32 * h, 32 * h + 32), (v[:, 2 * b + c, GROUP * g + h, :],),
                              p[:, c, prob_cols(h, 0, S)]) for h in range(GROUP)] for c in range(2)]

                own.max_products, own.score_products, own.value_products = own_max, own_scores, own_values
                own.max_column = lambda u, h, out, t: (u * GROUP + h) * 2 + t
                own.key_bias = lambda u, c: mcol[:, ds(pair * PT + 2 * (u // 4) + c, 1)]
                own.neg_ident = cst["neg_ident"][:]

                cross = Attention("cross", H // GROUP, 1, 2, L2_DH, 4, C, L2_DH ** -0.5)

                def cross_max(u, h):
                    return [(slice(C * t, C * t + C),
                             [(qmb[:, GROUP * u + h, P * t:P * t + P], kcb[:, half(u), C * (t // 2):C * (t // 2) + C])]) for t in range(PT)]

                def cross_scores(u, c, h):
                    return [(C * b, [(kT[:, half(u), C * b:C * b + C], qm[:, alone(u, h), S * b:S * b + S])])
                            for b in range(2)]

                def cross_values(u, r, p):
                    keys = slice(C * r, C * r + C)
                    return [[(slice(32 * h, 32 * h + 32), (v[keys, 0, GROUP * u + h, :],),
                              p[keys, 0, prob_cols(h, 0, S)]) for h in range(GROUP)]]

                cross.max_products, cross.score_products, cross.value_products = cross_max, cross_scores, cross_values
                cross.max_column = lambda u, h, out, t: (u * GROUP + h) * 4 + 2 * (out // C) + t
                cross.key_bias = lambda u, c: mccol[:, ds(pair, 1)]
                cross.neg_ident = cst["neg_ident"][:]

                def both(x, t, first):
                    return x[:, t:t + 2, first:first + 32].rearrange("p t (h e) -> p t h e", e=L2_DH)

                own.ident = cross.ident = cst["ident"]
                own.copies = cross.copies = H // GROUP
                own.late_values = cross.late_values = True


                def heads(x):
                    return x.rearrange("p (h e) -> p h e", e=L2_DH)

                with engines_pass(nc) as (block, sig):
                    @block.tensor
                    def _(pe):
                        def turn_norm(n):
                            pe.wait_ge(sig[n + "_normed"], 1)
                            for t in range(PT):
                                last = pe.transpose(psum[:, TURNED[t // 2], P * t:P * t + P], xn[:, t, :], cst["ident"][:])
                            last.then_inc(sig[n + "_turned"], 1)
                            pe.wait_ge(sig[n + "_modulated"], 2)

                        def project_out(n, weight):
                            pe.wait_ge(sig[n + "_values_taken"], own.units if n == "self" else 2 * cross.units)
                            turn_tensor(pe, cst["ident"], psum[:, 0, :], lambda t: o[:, t, :])\
                                .then_inc(sig[n + "_out_turned"], 1)
                            pe.wait_ge(sig[n + "_outT_ready"], 1)
                            for t in range(PT):
                                last = pe.matmul(psum[:, 1, P * t:P * t + P], oT[:, P * t:P * t + P], w(weight),
                                                 start=True, stop=True)
                            last.then_inc(sig[n + "_projected"], 1)

                        turn_norm("n1")
                        for i, name in enumerate(("q", "qs", "k", "ks")):
                            pe.matmul(psum[:, 2 + i, :], w(name), xnT[:], start=True, stop=True)\
                                .then_inc(sig["self_proj_ready"], 1)
                        for t in range(PT):
                            last = pe.matmul(psum[:, 6, P * t:P * t + P], xnT[:, P * t:P * t + P], w("v"),
                                             start=True, stop=True)
                        last.then_inc(sig["self_v_ready"], 1)
                        pe.wait_ge(sig["self_keys_ready"], 1)
                        pe.wait_ge(sig["ctx_ready"], 1)
                        attention_tensor(pe, sig, own, psum, m, probs, heads_out)
                        project_out("self", "so")
                        turn_norm("n2")
                        for i, name in enumerate(("cq", "cqs")):
                            pe.matmul(psum[:, 2 + i, :], w(name), xnT[:], start=True, stop=True)\
                                .then_inc(sig["cross_proj_ready"], 1)
                        for i, name in enumerate(("ck", "cks")):
                            pe.matmul(psum[:, 4 + i, 0:2 * C], w(name), cctx[:], start=True, stop=True)\
                                .then_inc(sig["cross_proj_ready"], 1)
                        pe.matmul(psum[:, 6, 0:P], cctx[:], w("cv"), start=True, stop=True)\
                            .then_inc(sig["cross_v_ready"], 1)
                        pe.wait_ge(sig["cross_keys_ready"], 1)
                        attention_tensor(pe, sig, cross, psum, m2, probs, heads_out)
                        project_out("cross", "co")
                        turn_norm("n3")
                        for i in range(L2_FF):
                            pe.matmul(psum[:, 2 + i, :], w("f1", 512)[:, P * i:P * i + P], xnT[:],
                                      start=True, stop=True).then_inc(sig["hidden_ready"], 1)
                        for i in range(L2_FF):
                            pe.wait_ge(sig["gelu_ready"], i + 1)
                            for t in range(PT):
                                last = pe.matmul(psum[:, FF_BANKS[t], 0:D], hT[:, i, P * t:P * t + P],
                                                 w("f2", 512)[:, P * i:P * i + P], start=i == 0, stop=i == L2_FF - 1)
                        last.then_inc(sig["ff_ready"], 1)

                    @block.gpsimd
                    def _(pool):
                        norm_pool(pool, sig, "n1", n1)
                        pool.tensor_copy(cctx[:], ctxT[:, ds(pair * (2 * C), 2 * C)]).then_inc(sig["ctx_ready"], 1)
                        norm_pool(pool, sig, "n2", n2)
                        norm_pool(pool, sig, "n3", n3)

                    @block.scalar
                    def _(act):
                        def modulate(n, i):
                            act.wait_ge(sig[n + "_turned"], 1)
                            act.activation(xnT[:, 0:S], psum[:, 7, 0:S], ACT.Identity, bias=shift(i, 0), scale=gain(i, 0))\
                                .then_inc(sig[n + "_modulated"], 1)

                        def out_turned(n):
                            act.wait_ge(sig[n + "_out_turned"], 1)
                            act.copy(oT[:], psum[:, 0, :]).then_inc(sig[n + "_outT_ready"], 1)

                        def lone_heads(n, g):
                            r = HALVES[g // 2]
                            for head in range(GROUP * g, GROUP * g + GROUP):
                                last = act.activation(qmb[r, head, :], qT[r, :], ACT.Copy,
                                                      scale=cst["head"][r, head % 8:head % 8 + 1])
                            last.then_inc(sig[n + "_bf_queries_ready"], 1)

                        def first_heads(n):
                            act.wait_ge(sig[n + "_rotated"], 1)
                            lone_heads(n, 0)
                            lone_heads(n, 1)

                        act.activation(warm[:], cst["mhalf"][:, 0, :], ACT.Exp)
                        for i, r in enumerate(MASK_ROWS):
                            act.copy(kb[r, i, :], mrow[r, ds(pair * (2 * S), 2 * S)])
                            act.copy(kcb[r, i, :], mcrow[r, ds(pair * (2 * C), 2 * C)])
                        modulate("n1", 0)
                        first_heads("self")
                        act.wait_ge(sig["self_v_ready"], 1)
                        act.copy(v[:, :, :, 0:L2_DH], psum[:, 6, :].rearrange("p (t h e) -> p t h e", t=PT, h=H))\
                            .then_inc(sig["self_v_taken"], 1)
                        attention_scalar(act, sig, own, psum, probs, heads_out)
                        out_turned("self")
                        modulate("n2", 1)
                        first_heads("cross")
                        act.wait_ge(sig["cross_v_ready"], 1)
                        act.copy(v[:, 0, :, 0:L2_DH], heads(psum[:, 6, 0:P])).then_inc(sig["cross_v_taken"], 1)
                        attention_scalar(act, sig, cross, psum, probs, heads_out)
                        out_turned("cross")
                        act.activation(warm[:], cst["mhalf"][:, 0, :], ACT.Gelu)
                        for i in range(L2_FF):
                            act.wait_ge(sig["hidden_ready"], i + 1)
                            act.activation(hT[:, i, :], psum[:, 2 + i, :], ACT.Gelu,
                                           bias=f1b[:, ds(layer * L2_FF + i, 1)]).then_inc(sig["gelu_ready"], 1)

                    @block.vector
                    def _(dve):
                        steps = Steps(dve, sig["vector_steps"])

                        def rotate(n, first, bank, cols, *parts):
                            dve.wait_ge(sig[n + "_proj_ready"], first + 1)
                            dve.tensor_tensor(t1[:, 0:cols], psum[:, bank, 0:cols], cst["cos"](cols), ALU.mult)
                            dve.wait_ge(sig[n + "_proj_ready"], first + 2)
                            steps.after(dve.tensor_tensor(t2[:, 0:cols], psum[:, bank + 1, 0:cols],
                                                          cst["sin"](cols), ALU.mult))
                            for out, r in parts:
                                last = dve.tensor_tensor(out, t1[r, 0:cols], t2[r, 0:cols], ALU.add)
                            last.then_inc(sig[n + "_rotated"], 1)
                            dve.wait_ge(sig[n + "_rotated"], first // 2 + 1)

                        def modulate(n, i, batches):
                            dve.wait_ge(sig[n + "_turned"], 1)
                            for b in batches:
                                cols = slice(S * b, S * b + S)
                                dve.tensor_scalar(xnT[:, cols], psum[:, TURNED[b], cols], gain(i, b), shift(i, b),
                                                  ALU.mult, ALU.add).then_inc(sig[n + "_modulated"], 1)

                        def operands(n, kcols, kb):
                            rotate(n, 0, 2, PTOK, (qT[:], slice(0, P)))
                            rotate(n, 2, 4, kcols, *((kT[r, i, 0:kcols], r) for i, r in enumerate(HALVES)))
                            for i, r in enumerate(HALVES):
                                last = dve.tensor_copy(kb[r, i, 0:kcols], kT[r, i, 0:kcols])
                            last.then_inc(sig[n + "_keys_ready"], 1)
                            lone_heads(n, 0)

                        def more_heads(n, u):
                            if u == 0:
                                lone_heads(n, 1)
                            elif u < 3:
                                r = HALVES[1]
                                for head in range(GROUP * (u + 1), GROUP * (u + 2)):
                                    last = dve.tensor_scalar(qmb[r, head, :], qT[r, :],
                                                             cst["head"][r, head % 8:head % 8 + 1], None, ALU.mult)
                                last.then_inc(sig[n + "_bf_queries_ready"], 1)

                        def lone_heads(n, g):
                            for j in range(GROUP * g, GROUP * g + GROUP):
                                last = dve.tensor_scalar(qm[:, j, :], qT[:], cst["head"][:, j:j + 1], None, ALU.mult)
                            last.then_inc(sig[n + "_queries_ready"], 1)

                        def residual(n, bank):
                            dve.wait_ge(sig[n], 1)
                            steps.after(dve.tensor_tensor(yall, yall, psum[:, bank, :].rearrange("p (t d) -> p t d", t=PT),
                                                          ALU.add))

                        norm_vector(dve, sig, steps, "n1", y, n1, lambda t: xn[:, t, :])
                        modulate("n1", 0, (1,))
                        operands("self", PTOK, kb)
                        attention_vector(dve, sig, own, psum, m, rsum,
                                         lambda u, r: both(o, 2 * (u // 4), 32 * (u % 4)),
                                         lambda u: more_heads("self", u))
                        residual("self_projected", 1)
                        norm_vector(dve, sig, steps, "n2", y, n2, lambda t: xn[:, t, :])
                        modulate("n2", 1, (1,))
                        operands("cross", 2 * C, kcb)
                        attention_vector(dve, sig, cross, psum, m2, rsum, lambda u, r: both(o, 2 * r, 32 * u),
                                         lambda u: more_heads("cross", u))
                        residual("cross_projected", 1)
                        norm_vector(dve, sig, steps, "n3", y, n3, lambda t: xn[:, t, :])
                        modulate("n3", 2, (0, 1))
                        steps.after(dve.tensor_tensor(yall, yall, f2bl[:].unsqueeze(1).to_broadcast([P, PT, D]), ALU.add))
                        dve.wait_ge(sig["ff_ready"], 1)
                        for t in range(0, PT, 2):
                            tiles = Y[:, ds(pair * PT + t, 2), :]
                            dve.tensor_tensor(tiles, tiles, psum[:, FF_BANKS[t]:FF_BANKS[t] + 2, 0:D], ALU.add)

        with engines_pass(nc) as (block, sig):
            @block.vector
            def _(dve):
                dve.tensor_tensor(X[:], X[:], Y[:], ALU.add)



F_DH = 8


def top2_block(nc, dram, X, psum, cst):
    with ExitStack() as ctx:
        def sb(name, shape, dt=F32):
            return ctx.enter_context(nc.sbuf_tensor("f2_" + name, shape, dt))

        wqkv, wo, wg = sb("wqkv", [P, 3, D]), sb("wo", [P, D]), sb("wg", [P, E])
        w1, w2 = sb("w1", [P, E, EF, P]), sb("w2", [P, E, EF, D])
        b1 = sb("b1", [P, E * EF])
        b2 = sb("b2", [1, E * D])
        onerow = sb("onerow", [1, P])
        aff = sb("aff", [P, 4, D])
        number = sb("number", [P, E])
        causal32, causalT32 = sb("causal32", [P, 2 * S]), sb("causalT32", [P, 2 * S])
        causal, causalT = sb("causal", [P, 2, S], BF16), sb("causalT", [P, 2, S], BF16)
        n0, n1, n2 = (norm_buffers(sb, n) for n in ("n0", "n1", "n2"))
        for n in (n0, n1, n2):
            n["mhalf"] = cst["mhalf"]
        Z, zn = sb("z", [P, PT, D]), sb("zn", [P, PT, D])
        zT = sb("zT", [P, PTOK])
        qT, kT = sb("qT", [P, PTOK]), sb("kT", [P, 2, PTOK])
        qm, qmb = sb("qm", [P, 2 * GROUP, PTOK]), sb("qmb", [P, 2 * GROUP, PTOK], BF16)
        kb = sb("kb", [P, 2, PTOK], BF16)
        v = sb("v", [P, PT, H, 32])
        m = sb("m", [P, H * 4], BF16)
        probs = sb("probs", [P, 2, 2, GROUP * S])
        rsum = sb("rsum", [P, 2, 2, GROUP])
        heads_out = sb("heads_out", [P, 2, S])
        o, oT = sb("o", [P, PT, D]), sb("oT", [P, PTOK])
        hm, hT = sb("hm", [P, PT, D]), sb("hT", [P, PTOK])
        logits, lmax, lsum = sb("logits", [P, PT, E]), sb("lmax", [P, PT]), sb("lsum", [P, PT])
        top, topi, topf = sb("top", [P, PT, 8]), sb("topi", [P, PT, 8], U32), sb("topf", [P, PT, 8])
        pair_sum = sb("pair_sum", [P, PT])
        w_a, w_b = sb("w_a", [P, PT, E]), sb("w_b", [P, PT, E])
        hid = sb("hid", [P, 2, EF, PTOK])

        with engines_pass(nc) as (block, sig):
            @block.sync
            def _(sp):
                for dst, src in ((wqkv, "F2_wqkv"), (wo, "F2_wo"), (wg, "F2_wg"), (w1, "F2_w1"), (w2, "F2_w2"),
                                 (b1, "F2_b1"), (b2, "F2_b2"), (causal32, "c_causal"), (causalT32, "c_causalT")):
                    sp.dma_start(dst[:], dram[src]).then_inc(sig["loads"], 16)
                sp.dma_start(aff[:].rearrange("p l d -> p (l d)"),
                             dram["F2_affine"].to_broadcast([P, 4 * D])).then_inc(sig["loads"], 16)
                sp.dma_start(number[:], dram["c_number"].to_broadcast([P, E])).then_inc(sig["loads"], 16)

            @block.gpsimd
            def _(pool):
                pool.memset(kT[:], 0.0)
                pool.memset(kb[:], 0.0)
                pool.memset(v[:, :, :, F_DH:F_DH + 1], 1.0)
                pool.memset(v[:, :, :, F_DH + 1:32], 0.0)
                pool.memset(onerow[:], 1.0)

            @block.vector
            def _(dve):
                dve.wait_ge(sig["loads"], 176)
                dve.tensor_copy(causal[:].rearrange("p t k -> p (t k)"), causal32[:])
                dve.tensor_copy(causalT[:].rearrange("p t k -> p (t k)"), causalT32[:])

        with nc.Fori(0, PAIRS) as pair:
            def x(t):
                return X[:, ds(pair * PT + t, 1), :].rearrange("p a d -> p (a d)")

            def half(g):
                return g // 2

            def alone(g, h):
                return GROUP * (g % 2) + h

            own = Attention("self", 2 * (H // GROUP), 2, 1, F_DH, 2, S, F_DH ** -0.5)

            def own_max(u, h):
                b, g = u // 4, u % 4
                return [(slice(256 * t, 256 * t + 256),
                         [(qmb[:, alone(g, h), S * b + P * t:S * b + P * t + P], kb[:, half(g), S * b:S * b + S]),
                          (cst["ident_bf"][:], causal[:, t, :])]) for t in range(2)]

            def own_scores(u, c, h):
                b, g = u // 4, u % 4
                return [(0, [(kT[:, half(g), S * b + P * c:S * b + P * c + P], qm[:, alone(g, h), S * b:S * b + S]),
                             (cst["ident_bf"][:], causalT[:, c, :])])]

            def own_values(u, r, p):
                b, g = u // 4, u % 4
                return [[(slice(32 * h, 32 * h + 32), (v[:, 2 * b + c, GROUP * g + h, :],),
                          p[:, c, prob_cols(h, 0, S)]) for h in range(GROUP)] for c in range(2)]

            own.max_products, own.score_products, own.value_products = own_max, own_scores, own_values
            own.max_column = lambda u, h, out, t: (u * GROUP + h) * 2 + t
            own.key_bias = lambda u, c: 0.0
            own.copies = 2
            own.neg_ident, own.ident = cst["neg_ident"][:], cst["ident"]

            with engines_pass(nc) as (block, sig):
                @block.tensor
                def _(pe):
                    def turn(ready, bank, src, turned, taken, count=1):
                        pe.wait_ge(sig[ready], count)
                        turn_tensor(pe, cst["ident"], psum[:, bank, :], src).then_inc(sig[turned], 1)
                        pe.wait_ge(sig[taken], 1)

                    turn("n0_normed", 7, lambda t: Z[:, t, :], "z_turned", "zT_ready")
                    for i in range(2):
                        pe.matmul(psum[:, 2 + i, :], wqkv[:, i, :], zT[:], start=True, stop=True)\
                            .then_inc(sig["proj_ready"], 1)
                    for t in range(PT):
                        last = pe.matmul(psum[:, 6, P * t:P * t + P], zT[:, P * t:P * t + P], wqkv[:, 2, :],
                                         start=True, stop=True)
                    last.then_inc(sig["v_ready"], 1)
                    pe.wait_ge(sig["operands_ready"], 1)
                    pe.wait_ge(sig["v_taken"], 1)
                    attention_tensor(pe, sig, own, psum, m, probs, heads_out)
                    turn("self_values_taken", 0, lambda t: o[:, t, :], "o_turned", "oT_ready", own.units)
                    for t in range(PT):
                        last = pe.matmul(psum[:, 1, P * t:P * t + P], oT[:, P * t:P * t + P], wo[:], start=True, stop=True)
                    last.then_inc(sig["projected"], 1)
                    turn("h_ready", 7, lambda t: hm[:, t, :], "h_turned", "hT_ready")
                    for t in range(PT):
                        last = pe.matmul(psum[:, 6, E * t:E * t + E], hT[:, P * t:P * t + P], wg[:], start=True, stop=True)
                    last.then_inc(sig["logits_ready"], 1)
                    for e in range(E + 1):
                        if e < E:
                            for i in range(EF):
                                if e >= 1:
                                    pe.wait_ge(sig["gelu_ready"], EF * (e - 1) + i + 1)
                                pe.matmul(psum[:, i, :], w1[:, e, i, :], hT[:], start=True, stop=True)\
                                    .then_inc(sig["units_ready"], 1)
                        if e >= 1:
                            pe.wait_ge(sig["gelu_ready"], EF * e)
                            if e >= 3:
                                pe.wait_ge(sig["expert_added"], e - 2)
                            for t in range(PT):
                                out = psum[:, 4 + (e - 1) % 2, P * t:P * t + P]
                                for i in range(EF):
                                    pe.matmul(out, hid[:, (e - 1) % 2, i, P * t:P * t + P], w2[:, e - 1, i, :],
                                              start=i == 0, stop=False)
                                last = pe.matmul(out, onerow[:], b2[:, D * (e - 1):D * e], start=False, stop=True)
                            last.then_inc(sig["expert_ready"], 1)

                @block.gpsimd
                def _(pool):
                    norm_pool(pool, sig, "n0", n0)
                    norm_pool(pool, sig, "n1", n1)
                    norm_pool(pool, sig, "n2", n2)

                @block.scalar
                def _(act):
                    def take(turned, bank, dst, ready):
                        act.wait_ge(sig[turned], 1)
                        act.copy(dst[:], psum[:, bank, :]).then_inc(sig[ready], 1)

                    take("z_turned", 7, zT, "zT_ready")
                    act.wait_ge(sig["v_ready"], 1)
                    act.copy(v[:, :, :, 0:F_DH], psum[:, 6, :].rearrange("p (t h e) -> p t h e", t=PT, h=H))\
                        .then_inc(sig["v_taken"], 1)
                    act.wait_ge(sig["qT_ready"], 1)
                    for j in range(2 * GROUP):
                        last = act.activation(qmb[:, j, :], qT[:], ACT.Copy, scale=cst["head"][:, j:j + 1])
                        if j % GROUP == GROUP - 1:
                            last.then_inc(sig["self_bf_queries_ready"], 1)
                    attention_scalar(act, sig, own, psum, probs, heads_out)
                    take("o_turned", 0, oT, "oT_ready")
                    take("h_turned", 7, hT, "hT_ready")
                    act.wait_ge(sig["shifted_logits_ready"], 1)
                    act.activation(w_a[:], logits[:], ACT.Exp).then_inc(sig["router_exp_ready"], 1)
                    for e in range(E):
                        if e >= 2:
                            act.wait_ge(sig["expert_ready"], e - 1)
                        for i in range(EF):
                            act.wait_ge(sig["units_ready"], EF * e + i + 1)
                            act.activation(hid[:, e % 2, i, :], psum[:, i, :], ACT.Gelu_apprx_tanh,
                                           bias=b1[:, EF * e + i:EF * e + i + 1]).then_inc(sig["gelu_ready"], 1)

                @block.vector
                def _(dve):
                    steps = Steps(dve, sig["vector_steps"])

                    def wide(col):
                        return col.unsqueeze(2).to_broadcast([P, PT, E])

                    def affine(dst, src, g, b):
                        steps.after(dve.tensor_tensor(dst, src, aff[:, g, :].unsqueeze(1).to_broadcast([P, PT, D]), ALU.mult))
                        return dve.tensor_tensor(dst, dst, aff[:, b, :].unsqueeze(1).to_broadcast([P, PT, D]), ALU.add)

                    def tiles(bank):
                        return psum[:, bank, :].rearrange("p (t d) -> p t d", t=PT)

                    norm_vector(dve, sig, steps, "n0", x, n0, lambda t: Z[:, t, :])
                    dve.wait_ge(sig["proj_ready"], 1)
                    dve.tensor_copy(qT[:], psum[:, 2, :]).then_inc(sig["qT_ready"], 1)
                    dve.wait_ge(sig["proj_ready"], 2)
                    for i, r in enumerate(HALVES):
                        dve.tensor_copy(kT[r, i, :], psum[r, 3, :])
                        last = dve.tensor_copy(kb[r, i, :], psum[r, 3, :])
                    last.then_inc(sig["operands_ready"], 1)
                    dve.wait_ge(sig["qT_ready"], 1)

                    def lone_heads(g):
                        for j in range(GROUP * g, GROUP * g + GROUP):
                            last = dve.tensor_scalar(qm[:, j, :], qT[:], cst["head"][:, j:j + 1], None, ALU.mult)
                        last.then_inc(sig["self_queries_ready"], 1)

                    lone_heads(0)
                    attention_vector(dve, sig, own, psum, m, rsum,
                                     lambda u, r: o[:, 2 * (u // 4):2 * (u // 4) + 2, 32 * (u % 4):32 * (u % 4) + 32]
                                     .rearrange("p t (h e) -> p t h e", e=F_DH), lambda u: lone_heads(1) if u == 0 else None)
                    dve.wait_ge(sig["projected"], 1)
                    steps.after(dve.tensor_tensor(Z[:], Z[:], tiles(1), ALU.add))
                    norm_vector(dve, sig, steps, "n1", lambda t: Z[:, t, :], n1, lambda t: zn[:, t, :])
                    affine(hm[:], zn[:], 0, 1).then_inc(sig["h_ready"], 1)
                    dve.wait_ge(sig["logits_ready"], 1)
                    steps.after(dve.tensor_copy(logits[:], psum[:, 6, 0:PT * E].rearrange("p (t e) -> p t e", e=E)))
                    steps.after(dve.tensor_reduce(lmax[:], logits[:], AX.X, ALU.max))
                    dve.tensor_tensor(logits[:], logits[:], wide(lmax[:]), ALU.subtract)\
                        .then_inc(sig["shifted_logits_ready"], 1)
                    dve.wait_ge(sig["router_exp_ready"], 1)
                    steps.after(dve.tensor_reduce(lsum[:], w_a[:], AX.X, ALU.add))
                    steps.after(dve.reciprocal(lsum[:], lsum[:]))
                    steps.after(dve.tensor_tensor(w_b[:], w_a[:], wide(lsum[:]), ALU.mult))
                    for t in range(PT):
                        last = dve.max(top[:, t, :], w_b[:, t, :])
                    steps.after(last)
                    for t in range(PT):
                        last = dve.max_index(topi[:, t, :], top[:, t, :], w_b[:, t, :])
                    steps.after(last)
                    steps.after(dve.tensor_copy(topf[:], topi[:]))
                    steps.after(dve.tensor_tensor(pair_sum[:], top[:, :, 0], top[:, :, 1], ALU.add))
                    steps.after(dve.reciprocal(pair_sum[:], pair_sum[:]))
                    numbers = number[:].unsqueeze(1).to_broadcast([P, PT, E])
                    dve.tensor_tensor(w_a[:], wide(topf[:, :, 0]), numbers, ALU.is_equal)
                    steps.after(dve.tensor_tensor(logits[:], wide(topf[:, :, 1]), numbers, ALU.is_equal))
                    steps.after(dve.tensor_tensor(w_a[:], w_a[:], logits[:], ALU.add))
                    steps.after(dve.tensor_tensor(w_a[:], w_a[:], w_b[:], ALU.mult))
                    steps.after(dve.tensor_tensor(w_a[:], w_a[:], wide(pair_sum[:]), ALU.mult))
                    for e in range(E):
                        dve.wait_ge(sig["expert_ready"], e + 1)
                        for t in range(PT):
                            last = dve.scalar_tensor_tensor(hm[:, t, :], psum[:, 4 + e % 2, P * t:P * t + P],
                                                            w_a[:, t, e:e + 1], hm[:, t, :], ALU.mult, ALU.add)
                        last.then_inc(sig["expert_added"], 1)
                        dve.wait_ge(sig["expert_added"], e + 1)
                    norm_vector(dve, sig, steps, "n2", lambda t: hm[:, t, :], n2, lambda t: zn[:, t, :])
                    steps.after(affine(zn[:], zn[:], 2, 3))
                    xall = X[:, ds(pair * PT, PT), :]
                    dve.tensor_tensor(xall, xall, zn[:], ALU.add)



L3_DH = 64
L3_CH = H * L3_DH // P
L3_FF = 4


def glu_block(nc, dram, X, psum, cst):
    with ExitStack() as ctx:
        def sb(name, shape, dt=F32):
            return ctx.enter_context(nc.sbuf_tensor("l3_" + name, shape, dt))

        W = sb("w", [P, 6, H * L3_DH])
        wo = sb("wo", [P, 2, L3_CH, D])
        w1 = sb("w1", [P, 2 * L3_FF, P])
        w2 = sb("w2", [P, L3_FF, D])
        b1 = sb("b1", [P, 2 * L3_FF])
        rows_b = sb("rows_b", [P, 3, D])
        nw = sb("nw", [P, 6, D])
        nb = sb("nb", [P, 6])
        embT = sb("embT", [P, B])
        ada = sb("ada", [P, 6 * B])
        ctxT = sb("ctxT", [P, B * C])
        cctx = sb("cctx", [P, 2 * C])
        n0, n1, n2, n3 = (norm_buffers(sb, n) for n in ("n0", "n1", "n2", "n3"))
        for n in (n0, n1, n2, n3):
            n["mhalf"] = cst["mhalf"]
        Y = sb("y", [P, PT, D])
        xn = sb("xn", [P, PT, D])
        xnT = sb("xnT", [P, PTOK])
        qT, kT = sb("qT", [P, L3_CH, PTOK]), sb("kT", [P, L3_CH, PTOK])
        qb, kb = sb("qb", [P, L3_CH, PTOK], BF16), sb("kb", [P, L3_CH, PTOK], BF16)
        v = sb("v", [P, PT, H, L3_DH])
        vc = sb("vc", [P, 2, H, L3_DH])
        onesc = sb("onesc", [P, 2, L3_DH])
        m = sb("m", [P, H * 4], BF16)
        m2 = sb("m2", [P, H * 4], BF16)
        probs = sb("probs", [P, 2, 2, GROUP * S])
        rsum = sb("rsum", [P, 2, S])
        hT = kT[:, 0:L3_FF, :]
        gT = qT[:, 0:L3_FF, :]

        with engines_pass(nc) as (block, sig):
            @block.sync
            def _(sp):
                for dst, src in ((W, "L3_W"), (wo, "L3_wo"), (w1, "L3_w1"), (w2, "L3_w2"), (b1, "L3_b1"),
                                 (nw, "L3_nw"), (nb, "L3_nb"), (embT, "embT"), (ctxT, "ctxT")):
                    sp.dma_start(dst[:], dram[src]).then_inc(sig["loads"], 16)
                sp.dma_start(rows_b[:].rearrange("p l d -> p (l d)"),
                             dram["L3_rows"].to_broadcast([P, 3 * D])).then_inc(sig["loads"], 16)

            @block.tensor
            def _(pe):
                pe.wait_ge(sig["loads"], 160)
                for i in range(6):
                    last = pe.matmul(psum[:, 0, i * B:(i + 1) * B], nw[:, i, :], embT[:], start=True, stop=True)
                last.then_inc(sig["ada_ready"], 1)

            @block.vector
            def _(dve):
                steps = Steps(dve, sig["vector_steps"])
                dve.memset(vc[:], 0.0)
                steps.after(dve.memset(onesc[:], 0.0))
                for b, r in enumerate(HALVES):
                    dve.memset(onesc[r, b, :], 1.0)
                dve.wait_ge(sig["loads"], 160)
                gains = nb[:].rearrange("p (i two) -> p i two", two=2)[:, :, 0]
                steps.after(dve.tensor_scalar(gains, gains, 1.0, None, ALU.add))
                dve.wait_ge(sig["ada_ready"], 1)
                dve.tensor_tensor(ada[:].rearrange("p (i b) -> p i b", b=B),
                                  psum[:, 0, 0:6 * B].rearrange("p (i b) -> p i b", b=B),
                                  nb[:].unsqueeze(2).to_broadcast([P, 6, B]), ALU.add)

        with nc.Fori(0, PAIRS) as pair:
            def gain(norm, b):
                return ada[:, ds(norm * (2 * B) + pair * 2 + b, 1)]

            def shift(norm, b):
                return ada[:, ds(norm * (2 * B) + B + pair * 2 + b, 1)]

            def x(t):
                return X[:, ds(pair * PT + t, 1), :].rearrange("p a d -> p (a d)")

            def y(t):
                return Y[:, t, :]

            own = Attention("self", 2 * (H // GROUP), 2, 2, L3_DH, 2, S, L3_DH ** -0.5)
            cross = Attention("cross", H // GROUP, 1, 4, L3_DH, 4, C, L3_DH ** -0.5)

            def place(head):
                return slice(L3_DH * (head % 2), L3_DH * (head % 2) + L3_DH), head // 2

            def own_max(u, h):
                b, (r, ch) = u // 4, place(GROUP * (u % 4) + h)
                return [(slice(256 * t, 256 * t + 256),
                         [(qb[r, ch, S * b + P * t:S * b + P * t + P], kb[r, ch, S * b:S * b + S])]) for t in range(2)]

            def own_scores(u, c, h):
                b, (r, ch) = u // 4, place(GROUP * (u % 4) + h)
                return [(0, [(kT[r, ch, S * b + P * c:S * b + P * c + P], qT[r, ch, S * b:S * b + S])])]

            def own_values(u, r, p):
                return [[(slice(L3_DH * j, L3_DH * j + L3_DH),
                          (v[:, 2 * (u // 4) + c, GROUP * (u % 4) + 2 * r + j, :], cst["ones"][:, 0:L3_DH]),
                          p[:, c, prob_cols(2 * r + j, 0, S)]) for j in range(2)] for c in range(2)]

            own.max_products, own.score_products, own.value_products = own_max, own_scores, own_values
            own.max_column = lambda u, h, out, t: (u * GROUP + h) * 2 + t

            def cross_max(u, h):
                r, ch = place(GROUP * u + h)
                return [(slice(C * t, C * t + C),
                         [(qb[r, ch, P * t:P * t + P], kb[r, ch, C * (t // 2):C * (t // 2) + C])]) for t in range(PT)]

            def cross_scores(u, c, h):
                r, ch = place(GROUP * u + h)
                return [(C * b, [(kT[r, ch, C * b:C * b + C], qT[r, ch, S * b:S * b + S])]) for b in range(2)]

            def cross_values(u, r, p):
                return [[(slice(L3_DH * j, L3_DH * j + L3_DH),
                          (vc[:, r % 2, GROUP * u + 2 * (r // 2) + j, :], onesc[:, r % 2, :]),
                          p[:, 0, prob_cols(2 * (r // 2) + j, 0, S)]) for j in range(2)]]

            cross.max_products, cross.score_products, cross.value_products = cross_max, cross_scores, cross_values
            cross.max_column = lambda u, h, out, t: (u * GROUP + h) * 4 + 2 * (out // C) + t
            for a in (own, cross):
                a.key_bias = lambda u, c: 0.0
                a.neg_ident = cst["neg_ident"][:]

            def heads(z):
                return z.rearrange("p (h e) -> p h e", e=L3_DH)

            with engines_pass(nc) as (block, sig):
                @block.tensor
                def _(pe):
                    def turn_norm(n):
                        pe.wait_ge(sig[n + "_normed"], 1)
                        turn_tensor(pe, cst["ident"], psum[:, 7, :], lambda t: xn[:, t, :])\
                            .then_inc(sig[n + "_turned"], 1)
                        pe.wait_ge(sig[n + "_modulated"], 2)

                    def bank_free(n, use):
                        if use >= 8:
                            pe.wait_ge(sig[n + "_scalar_taken"], use - 7)
                            pe.wait_ge(sig[n + "_vector_taken"], use - 7)

                    def project(n, first, keys, tiles):
                        for i in range(2):
                            src = xnT[:] if i == 0 else keys
                            for ch in range(L3_CH):
                                use = i * L3_CH + ch
                                bank_free(n, use)
                                pe.matmul(psum[:, use % 8, 0:src.shape[1]], W[:, first + i, P * ch:P * ch + P], src,
                                          start=True, stop=True).then_inc(sig[n + "_proj_ready"], 1)
                        for t in range(tiles):
                            for half in range(2):
                                use = 2 * L3_CH + 2 * t + half
                                bank_free(n, use)
                                pe.matmul(psum[:, use % 8, :], keys[:, P * t:P * t + P],
                                          W[:, first + 2, 512 * half:512 * half + 512], start=True, stop=True)\
                                    .then_inc(sig[n + "_proj_ready"], 1)
                        pe.wait_ge(sig[n + "_scalar_taken"], 2 * L3_CH)
                        pe.wait_ge(sig[n + "_vector_taken"], 2 * L3_CH + 2 * tiles)

                    def project_out(n, i, rounds):
                        pe.wait_ge(sig[n + "_values_taken"], rounds)
                        for t in range(PT):
                            for ch in range(L3_CH):
                                last = pe.matmul(psum[:, 2, P * t:P * t + P], qT[:, ch, P * t:P * t + P], wo[:, i, ch, :],
                                                 start=ch == 0, stop=ch == L3_CH - 1)
                        last.then_inc(sig[n + "_projected"], 1)

                    turn_norm("n1")
                    project("self", 0, xnT[:], PT)
                    attention_tensor(pe, sig, own, psum, m, probs)
                    project_out("self", 0, own.units * own.rounds)
                    turn_norm("n2")
                    pe.wait_ge(sig["ctx_ready"], 1)
                    project("cross", 3, cctx[:], 1)
                    attention_tensor(pe, sig, cross, psum, m2, probs)
                    project_out("cross", 1, cross.units * cross.rounds)
                    turn_norm("n3")
                    for i in range(L3_FF):
                        pe.matmul(psum[:, i, :], w1[:, L3_FF + i, :], xnT[:], start=True, stop=True)\
                            .then_inc(sig["gates_ready"], 1)
                        pe.matmul(psum[:, 4 + i, :], w1[:, i, :], xnT[:], start=True, stop=True)\
                            .then_inc(sig["units_ready"], 1)
                    pe.wait_ge(sig["gated_ready"], L3_FF)
                    for t in range(PT):
                        for i in range(L3_FF):
                            last = pe.matmul(psum[:, 0, P * t:P * t + P], hT[:, i, P * t:P * t + P], w2[:, i, :],
                                             start=i == 0, stop=i == L3_FF - 1)
                    last.then_inc(sig["ff_ready"], 1)

                @block.gpsimd
                def _(pool):
                    pool.tensor_copy(cctx[:], ctxT[:, ds(pair * (2 * C), 2 * C)]).then_inc(sig["ctx_ready"], 1)
                    norm_pool(pool, sig, "n0", n0)
                    norm_pool(pool, sig, "n1", n1)
                    norm_pool(pool, sig, "n2", n2)
                    norm_pool(pool, sig, "n3", n3)

                @block.scalar
                def _(act):
                    def modulate(n, i):
                        act.wait_ge(sig[n + "_turned"], 1)
                        for b in range(2):
                            act.activation(xnT[:, S * b:S * b + S], psum[:, 7, S * b:S * b + S], ACT.Identity,
                                           bias=shift(i, b), scale=gain(i, b)).then_inc(sig[n + "_modulated"], 1)

                    def take(n, kcols):
                        for use in range(2 * L3_CH):
                            act.wait_ge(sig[n + "_proj_ready"], use + 1)
                            dst, cols = (qT, PTOK) if use < L3_CH else (kT, kcols)
                            act.copy(dst[:, use % L3_CH, 0:cols], psum[:, use % 8, 0:cols])\
                                .then_inc(sig[n + "_scalar_taken"], 1)

                    modulate("n1", 0)
                    take("self", PTOK)
                    attention_scalar(act, sig, own, psum, probs)
                    modulate("n2", 1)
                    take("cross", 2 * C)
                    attention_scalar(act, sig, cross, psum, probs)
                    modulate("n3", 2)
                    act.wait_ge(sig["cross_projected"], 1)
                    for i in range(L3_FF):
                        act.wait_ge(sig["gates_ready"], i + 1)
                        act.activation(gT[:, i, :], psum[:, i, :], ACT.Gelu, bias=b1[:, L3_FF + i:L3_FF + i + 1])\
                            .then_inc(sig["gelu_ready"], 1)

                @block.vector
                def _(dve):
                    steps = Steps(dve, sig["vector_steps"])

                    def take(n, kcols, tiles):
                        for use in range(2 * L3_CH):
                            dve.wait_ge(sig[n + "_scalar_taken"], use + 1)
                            dst, src, cols = (qb, qT, PTOK) if use < L3_CH else (kb, kT, kcols)
                            dve.tensor_copy(dst[:, use % L3_CH, 0:cols], src[:, use % L3_CH, 0:cols])\
                                .then_inc(sig[n + "_vector_taken"], 1)
                        for t in range(tiles):
                            for half in range(2):
                                use = 2 * L3_CH + 2 * t + half
                                dve.wait_ge(sig[n + "_proj_ready"], use + 1)
                                if n == "self":
                                    last = dve.tensor_copy(v[:, t, 8 * half:8 * half + 8, :], heads(psum[:, use % 8, :]))
                                else:
                                    for b, r in enumerate(HALVES):
                                        last = dve.tensor_copy(vc[r, b, 8 * half:8 * half + 8, :], heads(psum[r, use % 8, :]))
                                last.then_inc(sig[n + "_vector_taken"], 1)

                    def residual(n, bank, i):
                        steps.after(dve.tensor_tensor(Y[:], Y[:], rows_b[:, i, :].unsqueeze(1).to_broadcast([P, PT, D]),
                                                      ALU.add))
                        dve.wait_ge(sig[n], 1)
                        steps.after(dve.tensor_tensor(Y[:], Y[:], psum[:, bank, :].rearrange("p (t d) -> p t d", t=PT),
                                                      ALU.add))

                    norm_vector(dve, sig, steps, "n0", x, n0, y)
                    norm_vector(dve, sig, steps, "n1", y, n1, lambda t: xn[:, t, :])
                    take("self", PTOK, PT)
                    attention_vector(dve, sig, own, psum, m, rsum,
                                     lambda u, r: qT[:, 2 * (u % 4) + r, S * (u // 4):S * (u // 4) + S])
                    residual("self_projected", 2, 0)
                    norm_vector(dve, sig, steps, "n2", y, n2, lambda t: xn[:, t, :])
                    take("cross", 2 * C, 1)
                    attention_vector(dve, sig, cross, psum, m2, rsum,
                                     lambda u, r: qT[:, 2 * u + r // 2, S * (r % 2):S * (r % 2) + S])
                    residual("cross_projected", 2, 1)
                    norm_vector(dve, sig, steps, "n3", y, n3, lambda t: xn[:, t, :])
                    for i in range(L3_FF):
                        dve.wait_ge(sig["units_ready"], i + 1)
                        dve.wait_ge(sig["gelu_ready"], i + 1)
                        dve.scalar_tensor_tensor(hT[:, i, :], psum[:, 4 + i, :], b1[:, i:i + 1], gT[:, i, :],
                                                 ALU.add, ALU.mult).then_inc(sig["gated_ready"], 1)
                    residual("ff_ready", 0, 2)
                    xall = X[:, ds(pair * PT, PT), :]
                    dve.tensor_tensor(xall, xall, Y[:], ALU.add)



POS, NEGQ = 7.0, 8.0
ROUND = 1.5 * 2.0 ** 23


def ternary_linear(nc, dram, X, psum, cst):
    with ExitStack() as ctx:
        def sb(name, shape, dt=F32):
            return ctx.enter_context(nc.sbuf_tensor("t3_" + name, shape, dt))

        hada, wt = sb("hada", [P, P]), sb("wt", [P, P])
        wabs, wscale, wrec = sb("wabs", [P, P]), sb("wscale", [P, 1]), sb("wrec", [P, 1])
        wn, wlow, wqT = sb("wn", [P, P]), sb("wlow", [P, P]), sb("wqT", [P, P])
        n0 = norm_buffers(sb, "n0")
        n0["mhalf"] = cst["mhalf"]
        z, zT, xh = sb("z", [P, PT, D]), sb("zT", [P, PTOK]), sb("xh", [P, PT, D])
        hi, lo, scale, rec = (sb(n, [P, PT]) for n in ("hi", "lo", "scale", "rec"))
        q, qT = sb("q", [P, PT, D]), sb("qT", [P, PTOK])

        with engines_pass(nc) as (block, sig):
            @block.sync
            def _(sp):
                sp.dma_start(hada[:], dram["c_hadamard"]).then_inc(sig["loads"], 16)
                sp.dma_start(wt[:], dram["T3_w"]).then_inc(sig["loads"], 16)

            @block.scalar
            def _(act):
                act.wait_ge(sig["loads"], 32)
                act.activation(wabs[:], wt[:], ACT.Abs, accum_out=wscale[:]).then_inc(sig["abs_sum_ready"], 1)
                act.wait_ge(sig["w_turned"], 1)
                act.copy(wqT[:], psum[:, 0, 0:P])

            @block.tensor
            def _(pe):
                pe.wait_ge(sig["ternary_ready"], 1)
                pe.transpose(psum[:, 0, 0:P], wn[:], cst["ident"][:]).then_inc(sig["w_turned"], 1)

            @block.vector
            def _(dve):
                steps = Steps(dve, sig["vector_steps"])
                dve.wait_ge(sig["abs_sum_ready"], 1)
                steps.after(dve.tensor_scalar(wscale[:], wscale[:], 1.0 / P, 1e-5, ALU.mult, ALU.max))
                steps.after(dve.reciprocal(wrec[:], wscale[:]))
                steps.after(dve.tensor_scalar(wn[:], wt[:], wrec[:], None, ALU.mult))
                steps.after(dve.tensor_scalar(wlow[:], wn[:], -0.5, None, ALU.is_lt))
                steps.after(dve.tensor_scalar(wn[:], wn[:], 0.5, None, ALU.is_gt))
                steps.after(dve.tensor_tensor(wn[:], wn[:], wlow[:], ALU.subtract))
                steps.after(dve.scalar_tensor_tensor(wn[:], wn[:], wscale[:], wt[:], ALU.mult, ALU.subtract))
                dve.tensor_tensor(wn[:], wn[:], wt[:], ALU.add).then_inc(sig["ternary_ready"], 1)

        with nc.Fori(0, PAIRS) as pair:
            def x(t):
                return X[:, ds(pair * PT + t, 1), :].rearrange("p a d -> p (a d)")

            with engines_pass(nc) as (block, sig):
                @block.tensor
                def _(pe):
                    pe.wait_ge(sig["n0_normed"], 1)
                    turn_tensor(pe, cst["ident"], psum[:, 0, :], lambda t: z[:, t, :]).then_inc(sig["z_turned"], 1)
                    pe.wait_ge(sig["zT_ready"], 1)
                    for t in range(PT):
                        last = pe.matmul(psum[:, 1, P * t:P * t + P], zT[:, P * t:P * t + P], hada[:], start=True, stop=True)
                    last.then_inc(sig["xh_ready"], 1)
                    pe.wait_ge(sig["q_ready"], 1)
                    turn_tensor(pe, cst["ident"], psum[:, 2, :], lambda t: q[:, t, :]).then_inc(sig["q_turned"], 1)
                    pe.wait_ge(sig["qT_ready"], 1)
                    for t in range(PT):
                        last = pe.matmul(psum[:, 3, P * t:P * t + P], qT[:, P * t:P * t + P], wqT[:], start=True, stop=True)
                    last.then_inc(sig["product_ready"], 1)

                @block.gpsimd
                def _(pool):
                    norm_pool(pool, sig, "n0", n0)

                @block.scalar
                def _(act):
                    act.wait_ge(sig["z_turned"], 1)
                    act.copy(zT[:], psum[:, 0, :]).then_inc(sig["zT_ready"], 1)
                    act.wait_ge(sig["xh_ready"], 1)
                    act.copy(xh[:].rearrange("p t d -> p (t d)"), psum[:, 1, :]).then_inc(sig["xh_taken"], 1)
                    act.wait_ge(sig["q_turned"], 1)
                    act.copy(qT[:], psum[:, 2, :]).then_inc(sig["qT_ready"], 1)

                @block.vector
                def _(dve):
                    steps = Steps(dve, sig["vector_steps"])
                    norm_vector(dve, sig, steps, "n0", x, n0, lambda t: z[:, t, :])
                    dve.wait_ge(sig["xh_taken"], 1)
                    dve.tensor_reduce(hi[:], xh[:], AX.X, ALU.max)
                    steps.after(dve.tensor_reduce(lo[:], xh[:], AX.X, ALU.min))
                    steps.after(dve.tensor_scalar(lo[:], lo[:], -1.0, 1e-5, ALU.mult, ALU.max))
                    steps.after(dve.tensor_tensor(hi[:], hi[:], lo[:], ALU.max))
                    steps.after(dve.tensor_scalar(scale[:], hi[:], 1.0 / POS, None, ALU.mult))
                    steps.after(dve.reciprocal(rec[:], scale[:]))
                    for t in range(PT):
                        last = dve.tensor_scalar(q[:, t, :], xh[:, t, :], rec[:, t:t + 1], ROUND, ALU.mult, ALU.add)
                    steps.after(last)
                    steps.after(dve.tensor_scalar(q[:], q[:], -ROUND, -NEGQ, ALU.add, ALU.max))
                    for t in range(PT):
                        last = dve.tensor_scalar(q[:, t, :], q[:, t, :], POS, scale[:, t:t + 1], ALU.min, ALU.mult)
                    steps.after(last)
                    steps.after(dve.tensor_tensor(q[:], q[:], xh[:], ALU.subtract))
                    dve.tensor_tensor(q[:], q[:], xh[:], ALU.add).then_inc(sig["q_ready"], 1)
                    dve.wait_ge(sig["product_ready"], 1)
                    xall = X[:, ds(pair * PT, PT), :]
                    dve.tensor_tensor(xall, xall, psum[:, 3, :].rearrange("p (t d) -> p t d", t=PT), ALU.add)



PHASES = [slot_attention, top_heads, attentive_gru, switch_experts, dit_layers, top2_block, glu_block, ternary_linear]


def program(nc, dram, phases=None):
    with ExitStack() as ctx:
        def sb(name, shape, dt=F32):
            return ctx.enter_context(nc.sbuf_tensor(name, shape, dt))

        X = sb("x_tokens", [P, TILES, D])
        psum = ctx.enter_context(nc.psum_tensor("psum", [P, 8, 512], F32))
        ident, neg_ident, ident_bf = sb("ident", [P, P]), sb("neg_ident", [P, P], BF16), sb("ident_bf", [P, P], BF16)
        cos, sin = sb("cos", [P, PTOK + 2 * C]), sb("sin", [P, PTOK + 2 * C])
        head, mhalf = sb("head", [P, 2 * GROUP]), sb("mhalf", [P, PT, 1])
        ones = sb("ones", [P, 64])
        cst = {"ident": ident, "neg_ident": neg_ident, "ident_bf": ident_bf, "head": head, "mhalf": mhalf, "ones": ones,
               "cos": lambda cols: cos[:, 0:PTOK] if cols == PTOK else cos[:, PTOK:PTOK + cols],
               "sin": lambda cols: sin[:, 0:PTOK] if cols == PTOK else sin[:, PTOK:PTOK + cols]}

        cst["tokens_sent"] = ctx.enter_context(nc.semaphore("tokens_sent"))
        cst["results_got"] = ctx.enter_context(nc.semaphore("results_got"))

        with engines_pass(nc) as (block, sig):
            @block.sync
            def _(sp):
                sp.dma_start(X[:], dram["x"].rearrange("(t p) d -> p t d", p=P)).then_inc(sig["loads"], 16)
                for dst, src in ((ident, "c_ident"), (cos, "c_cos"), (sin, "c_sin"), (head, "c_head")):
                    sp.dma_start(dst[:], dram[src]).then_inc(sig["loads"], 16)

            @block.gpsimd
            def _(pool):
                pool.memset(mhalf[:], -0.5)
                pool.memset(ones[:], 1.0)

            @block.vector
            def _(dve):
                dve.wait_ge(sig["loads"], 80)
                dve.tensor_scalar(neg_ident[:], ident[:], -1.0, None, ALU.mult)
                dve.tensor_copy(ident_bf[:], ident[:])

        for phase in (PHASES if phases is None else phases):
            phase(nc, dram, X, psum, cst)

        with engines_pass(nc) as (block, sig):
            @block.sync
            def _(sp):
                sp.dma_start(dram["out"].rearrange("(t p) d -> p t d", p=P), X[:]).then_inc(sig["stored"], 16)
                sp.wait_ge(sig["stored"], 16)



def laid_out(a):
    c = np.ascontiguousarray
    d = dict(shape_constants())
    d["x"] = a["x"].reshape(B * S, D)
    d["embT"] = c(a["cond_1024"].T)
    d["ctxT"] = c(a["ctx_1024"].reshape(B * C, D).T)
    m, mc = a["mask_BxS_bf0"], a["mask_BxS2_bf0"]
    d["mask_row"], d["cmask_row"] = c(m.reshape(1, -1)), c(mc.reshape(1, -1))
    d["mask_col"], d["cmask_col"] = c(m.reshape(TILES, P).T), c(mc.reshape(PAIRS, P).T)
    S0 = {k[9:]: v for k, v in a.items() if k.startswith("L0_xcond_")}
    d["S0_W"] = np.stack([S0[n] for n in ("wk", "wv", "wq", "wu", "w1", "w2")], 1)
    d["S0_col"] = np.stack([S0[n] for n in ("lnkv_g", "lnkv_b", "lnq_g", "lnq_b", "lnm_g", "lnm_b", "bk", "bq", "b1")], 1)
    d["S0_row"] = np.concatenate([S0[n].reshape(-1) for n in ("q_mu", "q_logsig", "bv", "bu", "b2", "lnp_g", "lnp_b")])[None]
    d["ctx_rows"] = a["ctx_1024"].reshape(PAIRS, P, D).transpose(1, 0, 2)
    d["cond_row"] = a["cond_1024"].reshape(1, B * D)
    H0 = {k[7:]: v for k, v in a.items() if k.startswith("L0_ffn_")}
    d["H0_wr"], d["H0_br"], d["H0_bo"] = H0["Wr"], H0["br"][None], H0["bo"][None]
    d["H0_wo"] = H0["Wo"].reshape(2, P, D).transpose(1, 0, 2)
    d["H0_W"] = np.stack([H0[n].reshape(D, HEADS, H_DH) for n in ("Wq", "Wk", "Wv")], 1)
    d["H0_bcol"] = np.stack([H0[n].reshape(HEADS, H_DH) for n in ("bq", "bk")], 2)
    d["H0_bv"] = H0["bv"].reshape(HEADS, H_DH)
    G1 = {k[9:]: v for k, v in a.items() if k.startswith("L1_xcond_")}
    d["G1_wa"] = G1["W_att"].reshape(2, D, D).transpose(1, 0, 2)
    d["G1_wi"] = G1["Wi"].reshape(2, D, 3, D).transpose(1, 0, 2, 3)
    d["G1_uh"], d["G1_bias"], d["G1_v"] = G1["Uh"].reshape(D, 3, D), G1["b"].reshape(3, D).T, G1["V_att"]
    d["S1_wr"] = a["L1_ffn_router_w"]
    d["S1_w1"] = a["L1_ffn_w1"].reshape(E, D, EF, P)
    d["S1_w2"] = a["L1_ffn_w2"].reshape(E, EF, P, D).transpose(0, 2, 1, 3)
    nw = np.stack([a[f"L2_xcond_n{i}_w"] for i in (1, 2, 3)], 1)
    d["L2_nw"] = nw.reshape(L2_LAYERS * 3 * 2, D, D).transpose(2, 0, 1)
    d["L2_nb"] = np.stack([a[f"L2_xcond_n{i}_b"] for i in (1, 2, 3)], 1).reshape(L2_LAYERS * 6, D).T
    d["L2_f1b"] = a["L2_xcond_f1_b"].reshape(L2_LAYERS * L2_FF, P).T
    d["L2_f2b"] = a["L2_xcond_f2_b"].reshape(1, L2_LAYERS * D)
    qkv = a["L2_xcond_qkv_w"]
    turned = lambda w: w.transpose(0, 2, 1)
    q, k, v = qkv[:, 0:D], qkv[:, D:2 * D], qkv[:, 2 * D:3 * D]
    cq, ck = a["L2_xcond_cq_w"], a["L2_xcond_ck_w"]
    f2 = turned(a["L2_xcond_f2_w"]).reshape(L2_LAYERS, L2_FF, P, D).transpose(0, 2, 1, 3).reshape(L2_LAYERS, P, L2_FF * D)
    d["L2_W"] = np.concatenate([turned(w) for w in (q, swap_halves(q), k, swap_halves(k), v, a["L2_xcond_so_w"],
                                                    cq, swap_halves(cq), ck, swap_halves(ck), a["L2_xcond_cv_w"],
                                                    a["L2_xcond_co_w"], a["L2_xcond_f1_w"])] + [f2], 2)
    F2 = {k[7:]: v for k, v in a.items() if k.startswith("L2_ffn_")}
    d["F2_wqkv"], d["F2_wo"], d["F2_wg"] = F2["w_qkv"].reshape(D, 3, D), F2["w_o"], F2["wg"]
    d["F2_w1"] = F2["w1"].transpose(1, 0, 2).reshape(D, E, EF, P)
    d["F2_w2"] = F2["w2"].reshape(E, EF, P, D).transpose(2, 0, 1, 3)
    d["F2_b1"] = F2["bb1"].reshape(E * EF, P).T
    d["F2_b2"] = F2["bb2"].reshape(1, E * D)
    d["F2_affine"] = np.concatenate([F2["g1"], F2["b1"], F2["g2"], F2["b2"]])[None]
    L3 = {k[9:]: v for k, v in a.items() if k.startswith("L3_xcond_")}
    d["L3_W"] = np.stack([L3[f"attn{i}_w{p}"] for i in (1, 2) for p in "qkv"], 1)
    d["L3_wo"] = np.stack([L3[f"attn{i}_wo"].reshape(L3_CH, P, D).transpose(1, 0, 2) for i in (1, 2)], 1)
    d["L3_w1"] = L3["ff_w1"].reshape(D, 2 * L3_FF, P)
    d["L3_b1"] = L3["ff_b1"].reshape(2 * L3_FF, P).T
    d["L3_w2"] = L3["ff_w2"].reshape(L3_FF, P, D).transpose(1, 0, 2)
    d["L3_rows"] = np.concatenate([L3["attn1_bo"], L3["attn2_bo"], L3["ff_b2"]])[None]
    d["L3_nw"] = np.stack([L3[f"norm{i}_w"].reshape(D, 2, D) for i in (1, 2, 3)], 1).reshape(D, 6, D)
    d["L3_nb"] = np.stack([L3[f"norm{i}_b"] for i in (1, 2, 3)]).reshape(6, D).T
    d["T3_w"] = a["L3_ffn_weight"]
    return {k: c(v) for k, v in d.items()}


def kernel(**inputs):
    import concourse.bacc as bacc
    from concourse.bass_utils import run_bass_kernel_spmd

    nc = bacc.Bacc("TRN2", target_bir_lowering=False, num_devices=1)
    arrays = laid_out({k: np.asarray(v) for k, v in inputs.items()})
    dram = {k: nc.dram_tensor("in_" + k, v.shape, mybir.dt.from_np(v.dtype), kind="ExternalInput").ap()
            for k, v in arrays.items()}
    dram["out"] = nc.dram_tensor("out_x", (B * S, D), F32, kind="ExternalOutput").ap()
    program(nc, dram)
    r = run_bass_kernel_spmd(nc, [{"in_" + k: v for k, v in arrays.items()}], core_ids=[0])
    return r.results[0]["out_x"].reshape(B, S, D)
```
